# Optimizing a Trainium2 kernel written in Bass

```python
import numpy as np
import jax
import jax.numpy as jnp

def _softmax(x, axis=-1):
    return jax.nn.softmax(x, axis=axis)

def _gelu(x):
    return jax.nn.gelu(x, approximate=True)

def _silu(x):
    return jax.nn.silu(x)

def _sigmoid(x):
    return jax.nn.sigmoid(x)

def _layernorm(x, axis=-1, eps=1e-05):
    m = jnp.mean(x, axis=axis, keepdims=True)
    v = jnp.var(x, axis=axis, keepdims=True)
    return (x - m) / jnp.sqrt(v + eps)

def _scatter_add(tgt, idx, src, axis=0):
    return tgt.at[idx].add(src)

def _segment_sum(src, seg, n):
    return jax.ops.segment_sum(src, seg, n)
kernel_name = 'mk_xattn_seq_d2_seqx_r2_9772ad'

def setup_inputs(seed: int=0):
    np.random.seed(seed)
    _w = jnp.asarray

    def _rec_inputs():
        import jax
        import jax.numpy as jnp
        _rk = jax.random.key(seed)
        x = 7.22e-05 + 1 * jax.random.normal(jax.random.fold_in(_rk, 1), (2, 2048, 512), jnp.float32)
        _lenS = 2048 - jax.random.randint(jax.random.fold_in(_rk, 7), (2,), 0, max(1, 2048 // 4) + 1, jnp.int32)
        _lenS2 = 154 - jax.random.randint(jax.random.fold_in(_rk, 8), (2,), 0, max(1, 154 // 4) + 1, jnp.int32)
        _ctx_1024P = jax.random.normal(jax.random.fold_in(_rk, 11), (2, 16, 512), jnp.float32)
        _ctx_1024c = jax.random.dirichlet(jax.random.fold_in(_rk, 511), 0.3 * jnp.ones((16,), jnp.float32), (2, 154))
        _ctx_1024t = jnp.einsum('bsk,bkd->bsd', _ctx_1024c, _ctx_1024P)
        _ctx_1024t = _ctx_1024t * jax.lax.rsqrt(jnp.mean(jnp.square(_ctx_1024t)) + 1e-12) * 0.953939
        ctx_1024 = 4.13588e-05 + 0.999923 * (_ctx_1024t + 0.3 * jax.random.normal(jax.random.fold_in(_rk, 611), (2, 154, 512), jnp.float32))
        itok_BxS2_4_31999 = jax.random.randint(jax.random.fold_in(_rk, 12), (2, 154), 4, 16000, jnp.int32)
        _ctxb_2048x64P = jax.random.normal(jax.random.fold_in(_rk, 13), (2, 16, 64), jnp.float32)
        _ctxb_2048x64c = jax.random.dirichlet(jax.random.fold_in(_rk, 513), 0.3 * jnp.ones((16,), jnp.float32), (2, 154))
        _ctxb_2048x64t = jnp.einsum('bsk,bkd->bsd', _ctxb_2048x64c, _ctxb_2048x64P)
        _ctxb_2048x64t = _ctxb_2048x64t * jax.lax.rsqrt(jnp.mean(jnp.square(_ctxb_2048x64t)) + 1e-12) * 0.953939
        ctxb_2048x64 = 0.50053 + 0.288505 * (_ctxb_2048x64t + 0.3 * jax.random.normal(jax.random.fold_in(_rk, 613), (2, 154, 64), jnp.float32))
        _validS = jnp.arange(2048)[None, :] < _lenS[:, None]
        _validS2 = jnp.arange(154)[None, :] < _lenS2[:, None]
        _causal = jnp.tril(jnp.ones((2048, 2048), dtype=bool))
        mask_BxS2_ik0 = jnp.where(jnp.broadcast_to(_validS2[:, :], (2, 154)), 0, 1).astype(jnp.int32)
        return (x, ctx_1024, itok_BxS2_4_31999, ctxb_2048x64, mask_BxS2_ik0)
    x, ctx_1024, itok_BxS2_4_31999, ctxb_2048x64, mask_BxS2_ik0 = _rec_inputs()

    def _L0_xattn_setup():
        import jax, jax.numpy as jnp
        import numpy as np
        BATCH, T, H, S, P, NH = (4, 1024, 512, 64, 64, 8)
        HD = H // NH

        def _layernorm(x, g, b):
            mu = jnp.mean(x, axis=-1, keepdims=True)
            var = jnp.mean((x - mu) ** 2, axis=-1, keepdims=True)
            return (x - mu) * jax.lax.rsqrt(var + 1e-05) * g + b

        def _mha(q_in, kv_in, W_qkv, b_qkv, W_o, b_o):
            Wq, Wk, Wv = jnp.split(W_qkv, 3, axis=0)
            bq, bk, bv = jnp.split(b_qkv, 3, axis=0)

            def heads(x, W, b):
                y = x @ W.T + b
                return y.reshape(y.shape[0], y.shape[1], NH, HD).transpose(0, 2, 1, 3)
            q, k, v = (heads(q_in, Wq, bq), heads(kv_in, Wk, bk), heads(kv_in, Wv, bv))
            scores = jnp.einsum('bhqd,bhkd->bhqk', q, k) * (1.0 / np.sqrt(HD))
            attn = jax.nn.softmax(scores, axis=-1)
            out = jnp.einsum('bhqk,bhkd->bhqd', attn, v)
            out = out.transpose(0, 2, 1, 3).reshape(q_in.shape)
            return out @ W_o.T + b_o
        key = jax.random.key(seed)
        ks = jax.random.split(key, 16)
        sH = 1.0 / np.sqrt(H)
        d = {}
        d['builder_state'] = jax.random.normal(ks[0], (BATCH, T, H), jnp.float32)
        d['base_state'] = jax.random.normal(ks[1], (BATCH, T, H), jnp.float32)
        d['input_ids'] = jax.random.randint(ks[2], (BATCH, T), 0, 16000)
        d['program_probs'] = jax.random.uniform(ks[3], (BATCH, T, P), jnp.float32)
        d['A'] = jax.random.normal(ks[4], (S, S), jnp.float32) * (0.5 / np.sqrt(S))
        d['Bmat'] = jax.random.normal(ks[5], (H, S), jnp.float32) * sH
        d['Cmat'] = jax.random.normal(ks[6], (S, H), jnp.float32) * (1.0 / np.sqrt(S))
        d['W_in'] = jax.random.normal(ks[7], (H, H), jnp.float32) * sH
        d['b_in'] = jnp.zeros((H,), jnp.float32)
        d['W_qkv'] = jax.random.normal(ks[8], (3 * H, H), jnp.float32) * sH
        d['b_qkv'] = jnp.zeros((3 * H,), jnp.float32)
        d['W_o'] = jax.random.normal(ks[9], (H, H), jnp.float32) * sH
        d['b_o'] = jnp.zeros((H,), jnp.float32)
        d['W_prog'] = jax.random.normal(ks[10], (H, P), jnp.float32) * (1.0 / np.sqrt(P))
        d['b_prog'] = jnp.zeros((H,), jnp.float32)
        d['g1'] = jnp.ones((H,), jnp.float32)
        d['beta1'] = jnp.zeros((H,), jnp.float32)
        d['g2'] = jnp.ones((H,), jnp.float32)
        d['beta2'] = jnp.zeros((H,), jnp.float32)
        return d
    _L0_xattn_all = _L0_xattn_setup()
    _L0_xattn_in = {k: v for k, v in _L0_xattn_all.items() if k in ('A', 'Bmat', 'Cmat', 'W_in', 'b_in', 'W_qkv', 'b_qkv', 'W_o', 'b_o', 'W_prog', 'b_prog', 'g1', 'beta1', 'g2', 'beta2')}
    del _L0_xattn_all

    def _L1_xattn_setup():
        import jax, jax.numpy as jnp
        import numpy as np
        H, D_MODEL, LEN_Q, LEN_K, D_K, D_V = (16, 512, 256, 1024, 64, 64)
        B = 4

        def _layernorm(x, gamma, beta, eps=1e-05):
            mu = jnp.mean(x, axis=-1, keepdims=True)
            var = jnp.mean((x - mu) ** 2, axis=-1, keepdims=True)
            return (x - mu) * jax.lax.rsqrt(var + eps) * gamma + beta
        key = jax.random.key(seed)
        ks = jax.random.split(key, 16)
        s = 0.02
        return {'Q': jax.random.normal(ks[0], (B, LEN_Q, D_MODEL), jnp.float32), 'K': jax.random.normal(ks[1], (B, LEN_K, D_MODEL), jnp.float32), 'V': jax.random.normal(ks[2], (B, LEN_K, D_MODEL), jnp.float32), 'node_num': LEN_Q, 'mask': jax.random.randint(ks[3], (B, LEN_K), 0, 2, jnp.int32), 'Wq': jax.random.normal(ks[4], (D_MODEL, H * D_K), jnp.float32) * s, 'bq': jnp.zeros((H * D_K,), jnp.float32), 'Wk': jax.random.normal(ks[5], (D_MODEL, H * D_K), jnp.float32) * s, 'bk': jnp.zeros((H * D_K,), jnp.float32), 'Wv': jax.random.normal(ks[6], (D_MODEL, H * D_V), jnp.float32) * s, 'bv': jnp.zeros((H * D_V,), jnp.float32), 'Wo': jax.random.normal(ks[7], (H * D_V, D_MODEL), jnp.float32) * s, 'bo': jnp.zeros((D_MODEL,), jnp.float32), 'gamma': jnp.ones((D_MODEL,), jnp.float32), 'beta': jnp.zeros((D_MODEL,), jnp.float32)}
    _L1_xattn_all = _L1_xattn_setup()
    _L1_xattn_in = {k: v for k, v in _L1_xattn_all.items() if k in ('Wq', 'bq', 'Wk', 'bk', 'Wv', 'bv', 'Wo', 'bo', 'gamma', 'beta')}
    del _L1_xattn_all
    return {'x': x, 'ctx_1024': ctx_1024, 'itok_BxS2_4_31999': itok_BxS2_4_31999, 'ctxb_2048x64': ctxb_2048x64, 'mask_BxS2_ik0': mask_BxS2_ik0, 'L0_xattn_A': _L0_xattn_in['A'], 'L0_xattn_Bmat': _L0_xattn_in['Bmat'], 'L0_xattn_Cmat': _L0_xattn_in['Cmat'], 'L0_xattn_W_in': _L0_xattn_in['W_in'], 'L0_xattn_b_in': _L0_xattn_in['b_in'], 'L0_xattn_W_qkv': _L0_xattn_in['W_qkv'], 'L0_xattn_b_qkv': _L0_xattn_in['b_qkv'], 'L0_xattn_W_o': _L0_xattn_in['W_o'], 'L0_xattn_b_o': _L0_xattn_in['b_o'], 'L0_xattn_W_prog': _L0_xattn_in['W_prog'], 'L0_xattn_b_prog': _L0_xattn_in['b_prog'], 'L0_xattn_g1': _L0_xattn_in['g1'], 'L0_xattn_beta1': _L0_xattn_in['beta1'], 'L0_xattn_g2': _L0_xattn_in['g2'], 'L0_xattn_beta2': _L0_xattn_in['beta2'], 'L1_xattn_Wq': _L1_xattn_in['Wq'], 'L1_xattn_bq': _L1_xattn_in['bq'], 'L1_xattn_Wk': _L1_xattn_in['Wk'], 'L1_xattn_bk': _L1_xattn_in['bk'], 'L1_xattn_Wv': _L1_xattn_in['Wv'], 'L1_xattn_bv': _L1_xattn_in['bv'], 'L1_xattn_Wo': _L1_xattn_in['Wo'], 'L1_xattn_bo': _L1_xattn_in['bo'], 'L1_xattn_gamma': _L1_xattn_in['gamma'], 'L1_xattn_beta': _L1_xattn_in['beta']}

def reference(x, ctx_1024, itok_BxS2_4_31999, ctxb_2048x64, mask_BxS2_ik0, L0_xattn_A, L0_xattn_Bmat, L0_xattn_Cmat, L0_xattn_W_in, L0_xattn_b_in, L0_xattn_W_qkv, L0_xattn_b_qkv, L0_xattn_W_o, L0_xattn_b_o, L0_xattn_W_prog, L0_xattn_b_prog, L0_xattn_g1, L0_xattn_beta1, L0_xattn_g2, L0_xattn_beta2, L1_xattn_Wq, L1_xattn_bq, L1_xattn_Wk, L1_xattn_bk, L1_xattn_Wv, L1_xattn_bv, L1_xattn_Wo, L1_xattn_bo, L1_xattn_gamma, L1_xattn_beta):
    import jax
    import jax.numpy as jnp

    def _L0_xattn_ref(builder_state, base_state, input_ids, program_probs, A, Bmat, Cmat, W_in, b_in, W_qkv, b_qkv, W_o, b_o, W_prog, b_prog, g1, beta1, g2, beta2):
        import jax, jax.numpy as jnp
        import numpy as np
        BATCH, T, H, S, P, NH = (4, 1024, 512, 64, 64, 8)
        HD = H // NH

        def _layernorm(x, g, b):
            mu = jnp.mean(x, axis=-1, keepdims=True)
            var = jnp.mean((x - mu) ** 2, axis=-1, keepdims=True)
            return (x - mu) * jax.lax.rsqrt(var + 1e-05) * g + b

        def _mha(q_in, kv_in, W_qkv, b_qkv, W_o, b_o):
            Wq, Wk, Wv = jnp.split(W_qkv, 3, axis=0)
            bq, bk, bv = jnp.split(b_qkv, 3, axis=0)

            def heads(x, W, b):
                y = x @ W.T + b
                return y.reshape(y.shape[0], y.shape[1], NH, HD).transpose(0, 2, 1, 3)
            q, k, v = (heads(q_in, Wq, bq), heads(kv_in, Wk, bk), heads(kv_in, Wv, bv))
            scores = jnp.einsum('bhqd,bhkd->bhqk', q, k) * (1.0 / np.sqrt(HD))
            attn = jax.nn.softmax(scores, axis=-1)
            out = jnp.einsum('bhqk,bhkd->bhqd', attn, v)
            out = out.transpose(0, 2, 1, 3).reshape(q_in.shape)
            return out @ W_o.T + b_o
        residual = builder_state
        x = _layernorm(builder_state, g1, beta1)
        base_n = _layernorm(base_state, g1, beta1)
        x = residual + _mha(x, base_n, W_qkv, b_qkv, W_o, b_o)
        residual = x
        xn = _layernorm(x, g2, beta2)
        U = (xn @ W_in.T + b_in) @ Bmat

        def step(s, u_t):
            s = jax.nn.silu(s @ A.T) + u_t
            return (s, s)
        _, states = jax.lax.scan(step, jnp.zeros((builder_state.shape[0], S), U.dtype), U.transpose(1, 0, 2))
        ssm_out = jnp.einsum('tbs,sh->bth', states, Cmat)
        x = residual + ssm_out
        mod = program_probs.mean(axis=1) @ W_prog.T + b_prog
        return x + mod[:, None, :]

    def _L1_xattn_ref(Q, K, V, node_num, mask, Wq, bq, Wk, bk, Wv, bv, Wo, bo, gamma, beta):
        import jax, jax.numpy as jnp
        import numpy as np
        H, D_MODEL, LEN_Q, LEN_K, D_K, D_V = (16, 512, 256, 1024, 64, 64)
        B = 4

        def _layernorm(x, gamma, beta, eps=1e-05):
            mu = jnp.mean(x, axis=-1, keepdims=True)
            var = jnp.mean((x - mu) ** 2, axis=-1, keepdims=True)
            return (x - mu) * jax.lax.rsqrt(var + eps) * gamma + beta
        b, lq, _ = Q.shape
        lk = K.shape[1]
        q = (Q @ Wq + bq).reshape(b, lq, H, D_K)
        k = (K @ Wk + bk).reshape(b, lk, H, D_K)
        v = (V @ Wv + bv).reshape(b, lk, H, D_V)
        scores = jnp.einsum('bqhd,bkhd->bhqk', q, k) / jnp.sqrt(jnp.float32(D_K))
        scores = jnp.where(mask[:, None, None, :] == 0, -jnp.inf, scores)
        alpha = jax.nn.softmax(scores, axis=-1)
        out = jnp.einsum('bhqk,bkhd->bqhd', alpha, v).reshape(b, lq, H * D_V)
        out = out @ Wo + bo + Q
        return _layernorm(out, gamma, beta)
    x = _L0_xattn_ref(x, ctx_1024, itok_BxS2_4_31999, ctxb_2048x64, L0_xattn_A, L0_xattn_Bmat, L0_xattn_Cmat, L0_xattn_W_in, L0_xattn_b_in, L0_xattn_W_qkv, L0_xattn_b_qkv, L0_xattn_W_o, L0_xattn_b_o, L0_xattn_W_prog, L0_xattn_b_prog, L0_xattn_g1, L0_xattn_beta1, L0_xattn_g2, L0_xattn_beta2)
    x = _L1_xattn_ref(x, ctx_1024, ctx_1024, 2048, mask_BxS2_ik0, L1_xattn_Wq, L1_xattn_bq, L1_xattn_Wk, L1_xattn_bk, L1_xattn_Wv, L1_xattn_bv, L1_xattn_Wo, L1_xattn_bo, L1_xattn_gamma, L1_xattn_beta)
    return x

_drawn_inputs = setup_inputs


def setup_inputs(seed=0):
    import zlib

    import numpy as np

    out = dict(_drawn_inputs(seed))
    spreads = {'L0_xattn_b_in': (0.0, 0.1),
     'L0_xattn_b_qkv': (0.0, 0.1),
     'L0_xattn_b_o': (0.0, 0.1),
     'L0_xattn_b_prog': (0.0, 0.1),
     'L0_xattn_g1': (1.0, 0.2),
     'L0_xattn_beta1': (0.0, 0.1),
     'L0_xattn_g2': (1.0, 0.2),
     'L0_xattn_beta2': (0.0, 0.1),
     'L1_xattn_bq': (0.0, 0.8),
     'L1_xattn_bk': (0.0, 0.8),
     'L1_xattn_bv': (0.0, 0.1),
     'L1_xattn_bo': (0.0, 0.1),
     'L1_xattn_gamma': (1.0, 0.2),
     'L1_xattn_beta': (0.0, 0.1)}
    factors = {'L1_xattn_Wq': 3.989, 'L1_xattn_Wk': 4.116}
    for name, (base, spread) in spreads.items():
        noise = np.random.default_rng([zlib.crc32(name.encode()), seed]).standard_normal(out[name].shape)
        drawn = base * np.exp(spread * noise) if base else spread * noise
        out[name] = jnp.asarray(drawn.astype(out[name].dtype))
    for name, factor in factors.items():
        out[name] = (out[name] * factor).astype(out[name].dtype)
    return out
```

```python
from collections import Counter
from contextlib import ExitStack

import concourse.bass as bass
from concourse import mybir

F32 = mybir.dt.float32
F32R = mybir.dt.float32r
I32 = mybir.dt.int32
ALU = mybir.AluOpType
ACT = mybir.ActivationFunctionType
AX_X = mybir.AxisListType.X

P = 128
D = 512
KC = D // P
BATCH, SEQ = 2, 2048
TOKENS = BATCH * SEQ
BLOCK = 512
TILES = BLOCK // P
NBLK = TOKENS // BLOCK
BLK_PER_BATCH = SEQ // BLOCK
SLOTS = 2 * TILES
KEYS = 154
MAIN = P
REM = KEYS - MAIN
GAP = 32
CW = 2 * MAIN + 2 * GAP
HD = 64
PAIRW = 2 * KEYS
SECOND = MAIN + GAP
PW = SECOND + KEYS
STATE = 64
EPS = 1e-5
SCALE = 1.0 / 8.0
MASKED = 3.0e38
NO_KEY = 2.0e38
CHUNK = 16
CHUNKS = SEQ // CHUNK
ROUNDS = 2
SETTLED = 2.0 ** -18


def load_row(row):
    return row.rearrange("(a n) -> a n", a=1).broadcast_to([P, row.shape[0]])



PREV, CUR, NEXT = -1, 0, 1


def layer0_items(first=False, last=False):
    out = []
    a = lambda *x: out.append(x)
    steps = TILES * KC
    q_at = {8: 0, 10: 1, 12: 2, 14: 3}
    for g in range(steps):
        t, u = divmod(g, KC)
        tail = (CUR, t - 1) if t else (PREV, TILES - 1)
        has_tail = t > 0 or not first
        if g == 0 and not last:
            for j in range(TILES - 1):
                a("LD", NEXT, j)
        if g + 1 < steps:
            a("S", CUR, g + 1)
        elif not last:
            a("S", NEXT, 0)
        if not last:
            if g < TILES - 1:
                a("LN", NEXT, g)
            if g == 5:
                a("LN", NEXT, TILES - 1)
            if g == 2:
                a("XT", NEXT, 1)
            if g == 6:
                a("XT", NEXT, 3)
            if g in q_at:
                a("Q", NEXT, q_at[g])
        if has_tail and u == 1:
            a("WO", *tail)
        if has_tail and u == 3:
            a("YT", *tail)
        a("PT", CUR, g)
        if has_tail and u == 0:
            a("OT", *tail)
        if not last:
            if g == 1:
                a("XT", NEXT, 0)
            if g == 3:
                a("XT", NEXT, 2)
        a("PV", CUR, g)
        if u == 3:
            a("ON", CUR, t)
        if has_tail and u == 3:
            a("U", *tail)
            a("ST", *tail)
        if g == 3 and not last:
            a("LD", NEXT, TILES - 1)
    return out


def layer0_start():
    out = [("LD", NEXT, j) for j in range(TILES)]
    for j in range(TILES):
        out += [("LN", NEXT, j), ("XT", NEXT, j)]
    return out + [("Q", NEXT, c) for c in range(KC)] + [("S", NEXT, 0)]


def layer0_end():
    return [(k, CUR, TILES - 1) for k in ("OT", "WO", "YT", "U", "ST")]


def layer1_items(first=False, last=False):
    out = []
    a = lambda *x: out.append(x)
    pairs = 2 * KC
    steps = TILES * pairs
    ss_at, xt_at = {2: 0, 3: 1, 6: 2, 10: 3}, {4: 0, 7: 1, 8: 2, 11: 3}
    q_at = {g: c for c, g in enumerate((12, 14, 15, 18, 20, 22, 26, 28))}
    for g in range(steps):
        t, u = divmod(g, pairs)
        tail = (CUR, t - 1) if t else (PREV, TILES - 1)
        has_tail = t > 0 or not first
        if g == 0 and not last:
            for j in range(TILES - 1):
                a("LD", NEXT, j)
        if g + 1 < steps:
            a("S", CUR, g + 1)
        elif not last:
            a("S", NEXT, 0)
        if not last:
            if g in ss_at:
                a("SS", NEXT, ss_at[g])
            if g in xt_at:
                a("XT", NEXT, xt_at[g])
            if g in q_at:
                a("Q", NEXT, q_at[g])
        if u == 5:
            a("WO", CUR, 2 * t)
        if has_tail and u == 1:
            a("WO", tail[0], 2 * tail[1] + 1)
        a("PT", CUR, g)
        if u == 4:
            a("OT", CUR, 2 * t)
        if has_tail and u == 0:
            a("OT", tail[0], 2 * tail[1] + 1)
        a("PV", CUR, g)
        if u % KC == 3:
            a("ON", CUR, g // KC)
        if has_tail and u == 5:
            a("ST", *tail)
        if g == 5 and not last:
            a("LD", NEXT, TILES - 1)
    return out


def layer1_start():
    out = [("LD", NEXT, j) for j in range(TILES)]
    for j in range(TILES):
        out += [("SS", NEXT, j), ("XT", NEXT, j)]
    return out + [("Q", NEXT, c) for c in range(2 * KC)] + [("S", NEXT, 0)]


def layer1_end():
    return [("OT", CUR, 2 * TILES - 1), ("WO", CUR, 2 * TILES - 1), ("ST", CUR, TILES - 1)]


ALSO = {"SS": ("T",), "XT": ("T", "split"), "OT": ("T", "split"), "YT": ("T", "split"),
        "Q": ("G",), "U": ("G", "cat_read"), "WO": ("cat_read",)}


def counted(items, par):
    n = Counter()
    for kind, rel, idx in items:
        n[kind] += 1
        n.update(ALSO.get(kind, ()))
        if kind in ("LD", "ST"):
            n[kind, TILES * ((par + rel) % 2) + idx] += 1
    return n


class Item:

    def __init__(self, kind, blk, par, idx, seen, per=None, trip=0):
        self.kind, self.blk, self.par, self.idx = kind, blk, par, idx
        self.seen, self.per, self.trip = Counter(seen), per or {}, trip

    def done(self, x):
        return self.seen[x] + (self.per[x] * self.trip if self.per.get(x) else 0)

    def side(self, x):
        assert self.per.get(x, 0) % 2 == 0
        return self.seen[x] % 2

    @property
    def batch(self):
        return self.blk // BLK_PER_BATCH

    @property
    def tile(self):
        return self.blk * TILES + self.idx

    @property
    def slot(self):
        return TILES * self.par + self.idx


def walk(eng, start, items, end):
    base = Counter()

    def straight(some, n, par):
        for kind, rel, idx in some:
            yield Item(kind, n + rel, (par + rel) % 2, idx, base)
            base.update(counted([(kind, rel, idx)], par))

    yield from straight(start, -1, 1)
    yield from straight(items(first=True), 0, 0)
    body = items()
    trips = (NBLK - 2) // 2
    per = counted(body, 1) + counted(body, 0)
    with eng.Fori(0, trips, 1) as i:
        seen = Counter(base)
        for half in range(2):
            n, par = 2 * i + (1 + half), (1 + half) % 2
            for kind, rel, idx in body:
                yield Item(kind, n + rel, (par + rel) % 2, idx, seen, per, i)
                seen.update(counted([(kind, rel, idx)], par))
    for x in per:
        base[x] += per[x] * trips
    yield from straight(items(last=True), NBLK - 1, (NBLK - 1) % 2)
    yield from straight(end, NBLK - 1, (NBLK - 1) % 2)


def after(eng, sem, value):
    if isinstance(value, int) and value <= 0:
        return
    eng.wait_ge(sem, value)


class Chain:

    def __init__(self, eng, sem):
        self.eng, self.sem, self.n = eng, sem, 0

    def then(self, ins):
        self.n += 1
        ins.then_inc(self.sem, 1)
        self.eng.wait_ge(self.sem, self.n)


def product(nc, out, stationary, moving, start, stop):
    (sh, sl), (mh, ml) = stationary, moving
    nc.tensor.matmul(out, sh, mh, start=start, stop=False)
    nc.tensor.matmul(out, sh, ml, start=False, stop=False)
    return nc.tensor.matmul(out, sl, mh, start=False, stop=stop)


def build(nc, a, y_dram):
    scratch = nc.dram_tensor("x1_dram", (TOKENS, D), F32, kind="Internal").ap()
    with ExitStack() as ctx:
        sb, sem = makers(nc, ctx)
        keep = dict(
            ident=sb("ident", [P, P], F32),
            hu=sb("hu", [P, BATCH, 1 + SEQ], F32),
            aa=sb("aa", [P, STATE], F32),
            cc=sb("cc", [P, D], F32),
            bank=[ctx.enter_context(nc.psum_tensor(f"bank{i}", [P, 512], F32)) for i in range(8)],
        )
        with ExitStack() as c0:
            sb0, _ = makers(nc, c0)
            l0 = attention_tensors(sb0, "0", KC)
            l0 |= dict(
                wu=[sb0(f"wu_{x}", [P, KC, P], F32R) for x in ("high", "low")],
                ubias=sb0("ubias", [P, 1], F32),
                mod=sb0("mod", [P, BATCH, D], F32),
            )
            with ExitStack() as cp:
                prepare_layer0(nc, cp, sem, a, keep, l0)
            with ExitStack() as cw:
                run_layer(nc, cw, sem, 0, keep, l0, a["x"], scratch)
        with ExitStack() as c1:
            sb1, _ = makers(nc, c1)
            l1 = attention_tensors(sb1, "1", 2 * KC)
            l1 |= dict(
                mask=sb1("mask", [P, BATCH, 2, KEYS], F32),
                gamma=sb1("gamma", [P, D], F32),
                beta=sb1("beta", [P, D], F32),
            )
            with ExitStack() as cs:
                scan_and_prepare_layer1(nc, cs, sem, a, keep, l1)
            with ExitStack() as cw:
                run_layer(nc, cw, sem, 1, keep, l1, scratch, y_dram)


def makers(nc, ctx):
    sb = lambda name, shape, dt: ctx.enter_context(nc.sbuf_tensor(name, shape, dt))
    sem = lambda name: ctx.enter_context(nc.semaphore(name))
    return sb, sem


def attention_tensors(sb, tag, pairs):
    width = pairs * P
    return dict(
        pairs=pairs,
        wq=[sb(f"wq{tag}_{x}", [P, KC, width], F32R) for x in ("high", "low")],
        wo=[sb(f"wo{tag}_{x}", [P, pairs, D], F32R) for x in ("high", "low")],
        nbq=sb(f"nbq{tag}", [P, pairs], F32),
        kbd=sb(f"kbd{tag}", [P, BATCH, pairs, PAIRW], F32),
        vm=sb(f"vm{tag}", [P, BATCH, width], F32),
        vr=sb(f"vr{tag}", [P, BATCH, pairs, P], F32),
        bo=sb(f"bo{tag}", [P, D], F32),
    )


def evacuate_keys(nc, bank, l, u, bias):
    for e, (main, rem) in enumerate(((0, MAIN), (KEYS + REM, KEYS))):
        rows = slice(HD * e, HD * e + HD)
        nc.scalar.activation(l["kbd"][rows, :, u, main:main + MAIN],
                             bank[rows, 0:2 * MAIN].rearrange("p (b k) -> p b k", b=BATCH),
                             ACT.Identity, bias=bias[rows])
        last = nc.scalar.activation(l["kbd"][rows, :, u, rem:rem + REM],
                                    bank[rows, 2 * MAIN:CW].rearrange("p (b k) -> p b k", b=BATCH)[:, :, 0:REM],
                                    ACT.Identity, bias=bias[rows])
    return last


def evacuate_values(nc, bank, l, group, col):
    if group < BATCH:
        return nc.scalar.activation(l["vm"][:, group, col:col + D], bank[:], ACT.Copy)
    first = col // P
    for b in range(BATCH):
        for e in range(2):
            src = bank[GAP * b:GAP * b + REM, :].rearrange("p (u e d) -> p u e d", e=2, d=HD)[:, :, e, :]
            last = nc.scalar.activation(l["vr"][GAP * e:GAP * e + REM, b, first:first + D // P,
                                                HD * e:HD * e + HD], src, ACT.Copy)
    return last


def context_columns(group):
    return slice(group * MAIN, group * MAIN + (MAIN if group < BATCH else 2 * GAP))


def context_transposes(nc, bank, src, group, ident):
    w = MAIN if group < BATCH else 2 * GAP
    for k in range(KC):
        last = nc.tensor.transpose(bank[:, w * k:w * k + w], src[0:w, group, P * k:P * k + P], ident[0:w, 0:w])
    return last


def split_weight(nc, dve, l_pair, src, done):
    high, low = l_pair
    nc.vector.tensor_copy(high, src).then_inc(done[0], 1)
    done[1] += 1
    dve.wait_ge(done[0], done[1])
    nc.vector.tensor_tensor(low, src, high.bitcast(F32), ALU.subtract).then_inc(done[0], 1)
    done[1] += 1



def prepare_layer0(nc, ctx, sem, a, keep, l0):
    sb, _ = makers(nc, ctx)
    bank, ident = keep["bank"], keep["ident"]
    NQKV = 3 * KC
    nat = sb("nat", [P, NQKV + KC, D], F32)
    g1, b1 = sb("g1_row", [P, D], F32), sb("beta1_row", [P, D], F32)
    wt = sb("wt", [P, 4, KC, D], F32)
    product_out = sb("product_out", [P, D], F32)
    vbo = sb("values_bias_through_wo", [P, D], F32)
    wb = sb("wb", [P, NQKV], F32)
    bqkv = sb("bqkv_col", [P, NQKV], F32)
    wbias = sb("wbias", [P, NQKV], F32)
    vb_wide = sb("vb_wide", [P, KC, P], F32)
    cx, cxn = sb("cx", [P, 3, D], F32), sb("cxn", [P, 3, D], F32)
    ct = sb("cnT", [P, KC, CW], F32)
    stats, mv = sb("ctx_stats", [P, 3, 6], F32), sb("ctx_mv", [P, 3, 2], F32)
    half, rstd = sb("ctx_minus_half", [P, 3], F32), sb("ctx_rstd", [P, 3], F32)
    win, bm = sb("win", [P, KC, D], F32), sb("bm", [P, KC, P], F32)
    wur, wug = sb("wu_raw", [P, KC, P], F32), sb("wu_scaled", [P, KC, P], F32)
    g2, b2, b_in = sb("g2_col", [P, KC], F32), sb("beta2_col", [P, KC], F32), sb("b_in_col", [P, KC], F32)
    a2 = sb("a2", [STATE, 2 * STATE], F32)
    pp, ppr = sb("pp", [P, BATCH, 64], F32), sb("pp_rem", [P, BATCH, 64], F32)
    wp, wpt = sb("wprog", [P, KC, 64], F32), sb("wprogT", [64, D], F32)
    bp = sb("bprog_row", [P, D], F32)
    ones = sb("ones", [P, P], F32)
    mean, mean_wide = sb("mean", [64, BATCH], F32), sb("mean_wide", [64, BATCH, P], F32)

    ctx_in, row_in, small_in, win_in = sem("p_ctx_in"), sem("p_row_in"), sem("p_small_in"), sem("p_win_in")
    w_in = [sem(f"p_w_in{i}") for i in range(4)]
    padded, zeroed, consts, pool_step = sem("p_padded"), sem("p_zeroed"), sem("p_consts"), sem("p_pool_step")
    ctx_stats, ctx_normed, dve_step, scaled = sem("p_ctx_stats"), sem("p_ctx_normed"), sem("p_dve_step"), sem("p_scaled")
    biases, filled, drained, split = sem("p_biases"), sem("p_filled"), sem("p_drained"), sem("p_split")
    mean_ready, vb_ready = sem("p_mean_ready"), sem("p_vb_ready")

    jobs = [("ctxT", g) for g in range(3)] + [("wT", r) for r in range(KC, NQKV)]
    jobs += [("keys", u) for u in range(KC)] + [("values", g) for g in range(3)]
    jobs += [("wT", r) for r in list(range(KC)) + list(range(NQKV, NQKV + KC))]
    jobs += [("aa", 0), ("wprogT", 0), ("mean", 0), ("wu", 0), ("ubias", 0), ("mod", 0), ("mod", 1), ("bo", 0)]
    after_job = {job: n + 1 for n, job in enumerate(jobs)}
    rows_order = list(range(KC, NQKV)) + list(range(KC))
    after_row = {r: n + 1 for n, r in enumerate(rows_order)}
    SMALL = 16 * 14

    block = ctx.enter_context(nc.Block())

    @block.sync
    def _(sp):
        sp.wait_ge(padded, 1)
        for b in range(BATCH):
            sp.dma_start(cx[:, b, :], a["ctx"][b, 0:MAIN, :]).then_inc(ctx_in, 16)
            sp.dma_start(cx[GAP * b:GAP * b + REM, 2, :], a["ctx"][b, MAIN:KEYS, :]).then_inc(ctx_in, 16)
        sp.dma_start(g1[:], load_row(a["g1"])).then_inc(row_in, 16)
        sp.dma_start(b1[:], load_row(a["beta1"])).then_inc(row_in, 16)
        wqkv = a["W_qkv"].rearrange("(m r p) n -> m p r n", p=P, r=KC)
        for m in (1, 2, 0):
            sp.dma_start(nat[:, KC * m:KC * m + KC, :], wqkv[m]).then_inc(w_in[m], 16)
        sp.dma_start(nat[:, NQKV:, :], a["W_o"].rearrange("(r p) n -> p r n", p=P)).then_inc(w_in[3], 16)

    @block.scalar
    def _(act):
        act.dma_start(bqkv[:], a["b_qkv"].rearrange("(c p) -> p c", p=P), allow_slow_non_contiguous=True).then_inc(small_in, 16)
        act.dma_start(g2[:], a["g2"].rearrange("(c p) -> p c", p=P), allow_slow_non_contiguous=True).then_inc(small_in, 16)
        act.dma_start(b2[:], a["beta2"].rearrange("(c p) -> p c", p=P), allow_slow_non_contiguous=True).then_inc(small_in, 16)
        act.dma_start(b_in[:], a["b_in"].rearrange("(c p) -> p c", p=P), allow_slow_non_contiguous=True).then_inc(small_in, 16)
        for e in range(2):
            act.dma_start(a2[:, STATE * e:STATE * (e + 1)], a["A"]).then_inc(small_in, 16)
            act.dma_start(keep["cc"][STATE * e:STATE * (e + 1), :], a["Cmat"]).then_inc(small_in, 16)
        act.dma_start(pp[:], a["pp"][:, 0:MAIN, :].rearrange("b p n -> p b n")).then_inc(small_in, 16)
        act.dma_start(wp[:], a["W_prog"].rearrange("(c p) n -> p c n", p=P)).then_inc(small_in, 16)
        act.dma_start(bp[:], load_row(a["b_prog"])).then_inc(small_in, 16)
        act.dma_start(l0["bo"][:], load_row(a["b_o"])).then_inc(small_in, 16)
        act.wait_ge(padded, 3)
        act.dma_start(ppr[0:REM, :, :], a["pp"][:, MAIN:KEYS, :].rearrange("b p n -> p b n")).then_inc(small_in, 16)
        act.dma_start(bm[:, :, STATE:P], a["Bmat"].rearrange("(c p) n -> p c n", p=P)).then_inc(small_in, 16)
        act.dma_start(win[:], a["W_in"].rearrange("(c p) n -> p c n", p=P)).then_inc(win_in, 16)
        for n, (kind, i) in enumerate(jobs):
            act.wait_ge(filled, n + 1)
            x = bank[n % 8]
            if kind == "ctxT":
                cols = context_columns(i)
                w = cols.stop - cols.start
                last = nc.scalar.activation(ct[:, :, cols], x[:, 0:KC * w].rearrange("p (k c) -> p k c", k=KC), ACT.Copy)
            elif kind == "wT":
                m, r = divmod(i, KC)
                last = nc.scalar.activation(wt[:, m, :, P * r:P * r + P], x[:].rearrange("p (k c) -> p k c", k=KC), ACT.Copy)
            elif kind == "keys":
                if i == 0:
                    act.wait_ge(biases, 1)
                    act.wait_ge(zeroed, 2)
                last = evacuate_keys(nc, x, l0, i, wbias[:, KC + i:KC + i + 1])
            elif kind == "values":
                last = evacuate_values(nc, x, l0, i, 0)
            elif kind == "aa":
                last = nc.scalar.activation(keep["aa"][:], x[:, 0:STATE], ACT.Copy)
            elif kind == "wprogT":
                last = nc.scalar.activation(wpt[:], x[0:64, :], ACT.Copy)
            elif kind == "mean":
                last = nc.scalar.activation(mean[:], x[0:64, 0:BATCH], ACT.Copy, scale=1.0 / KEYS)
            elif kind == "wu":
                last = nc.scalar.activation(wur[:], x[:].rearrange("p (c n) -> p c n", c=KC), ACT.Copy)
            elif kind == "ubias":
                last = nc.scalar.activation(l0["ubias"][:], x[:, 0:1], ACT.Copy)
            elif kind == "mod":
                last = nc.scalar.activation(l0["mod"][:, i, :], x[:], ACT.Copy)
            elif kind == "bo":
                last = nc.scalar.activation(vbo[:], x[:], ACT.Copy)
            last.then_inc(drained, 1)

    @block.gpsimd
    def _(pool):
        nc.gpsimd.memset(cx[0:2 * GAP, 2, :], 0.0).then_inc(padded, 1)
        nc.gpsimd.memset(bm[:], 0.0).then_inc(padded, 1)
        nc.gpsimd.memset(ppr[:], 0.0).then_inc(padded, 1)
        nc.gpsimd.memset(ident[:], 0.0).then_inc(pool_step, 1)
        nc.gpsimd.memset(half[:], -0.5).then_inc(pool_step, 1)
        pool.wait_ge(pool_step, 2)
        nc.gpsimd.affine_select(out=ident[:], in_=ident[:], compare_op=ALU.not_equal, fill=1.0, base=0,
                                pattern=[[-1, P]], channel_multiplier=1).then_inc(consts, 1)
        nc.gpsimd.memset(ones[:], 1.0).then_inc(consts, 1)
        nc.gpsimd.memset(l0["kbd"][:], 0.0).then_inc(zeroed, 1)
        nc.gpsimd.memset(l0["vr"][:], 0.0).then_inc(zeroed, 1)
        pool.wait_ge(ctx_stats, 1)
        nc.gpsimd.tensor_tensor(rstd[:], mv[:, :, 1], half[:], ALU.pow).then_inc(pool_step, 1)
        pool.wait_ge(pool_step, 3)
        for g in range(3):
            w = MAIN if g < BATCH else 2 * GAP
            nc.gpsimd.tensor_scalar(cxn[0:w, g, :], cx[0:w, g, :], mv[0:w, g, 0:1], rstd[0:w, g:g + 1],
                                    ALU.subtract, ALU.mult).then_inc(ctx_normed, 1)
        pool.wait_ge(ctx_normed, 3)
        nc.gpsimd.memset(keep["hu"][0:STATE, :, :], 0.0).then_inc(pool_step, 1)
        pool.wait_ge(pool_step, 4)
        nc.gpsimd.memset(keep["hu"][STATE:P, :, 0:1], 0.0)

    @block.vector
    def _(dve):
        step = Chain(dve, dve_step)
        step.then(nc.vector.memset(mv[:], 1.0))
        dve.wait_ge(ctx_in, 64)
        for g in range(3):
            w = MAIN if g < BATCH else 2 * GAP
            step.then(nc.vector.bn_stats(stats[0:w, g, :], cx[0:w, g, :]))
            step.then(nc.vector.bn_aggr(mv[0:w, g, :], stats[0:w, g, :]))
        nc.vector.tensor_scalar(mv[:, :, 1], mv[:, :, 1], EPS, None, ALU.add).then_inc(ctx_stats, 1)
        dve.wait_ge(row_in, 32)
        for r in rows_order:
            dve.wait_ge(w_in[r // KC], 16)
            step.then(nc.vector.tensor_tensor_reduce(out=product_out[:], in0=nat[:, r, :], in1=b1[:], scale=1.0,
                                                     scalar=0.0, op0=ALU.mult, op1=ALU.add,
                                                     accum_out=wb[:, r:r + 1]))
            nc.vector.tensor_tensor(nat[:, r, :], nat[:, r, :], g1[:], ALU.mult).then_inc(scaled, 1)
            if r == NQKV - 1:
                dve.wait_ge(small_in, SMALL)
                nc.vector.tensor_tensor(wbias[:, KC:], bqkv[:, KC:], wb[:, KC:], ALU.add).then_inc(biases, 1)
        step.then(nc.vector.tensor_tensor(wbias[:, 0:KC], bqkv[:, 0:KC], wb[:, 0:KC], ALU.add))
        nc.vector.tensor_scalar(l0["nbq"][:], wbias[:, 0:KC], -SCALE, None, ALU.mult)
        dve.wait_ge(consts, 2)
        dve.wait_ge(biases, 1)
        for k in range(KC):
            nc.vector.tensor_scalar(vb_wide[:, k, :], ones[:], wbias[:, 2 * KC + k:2 * KC + k + 1], None,
                                    ALU.mult).then_inc(vb_ready, 1)
        done = [split, 0]
        dve.wait_ge(drained, after_job["wT", KC - 1])
        split_weight(nc, dve, [w[:] for w in l0["wq"]], wt[:, 0], done)
        dve.wait_ge(drained, after_job["wT", NQKV + KC - 1])
        split_weight(nc, dve, [w[:] for w in l0["wo"]], wt[:, 3], done)
        dve.wait_ge(drained, after_job["mean", 0])
        for b in range(BATCH):
            nc.vector.tensor_scalar(mean_wide[:, b, :], ones[0:64, :], mean[:, b:b + 1], None,
                                    ALU.mult).then_inc(mean_ready, 1)
        dve.wait_ge(drained, after_job["wu", 0])
        for c in range(KC):
            ins = nc.vector.tensor_scalar(wug[:, c, :], wur[:, c, :], g2[:, c:c + 1], None, ALU.mult)
            step.then(ins)
        split_weight(nc, dve, [w[:] for w in l0["wu"]], wug[:], done)
        for b in range(BATCH):
            dve.wait_ge(drained, after_job["mod", b])
            nc.vector.tensor_tensor(l0["mod"][:, b, :], l0["mod"][:, b, :], bp[:], ALU.add)
        dve.wait_ge(drained, after_job["bo", 0])
        nc.vector.tensor_tensor(l0["bo"][:], l0["bo"][:], vbo[:], ALU.add)

    @block.tensor
    def _(pe):
        pe.wait_ge(consts, 2)
        for n, (kind, i) in enumerate(jobs):
            after(pe, drained, n - 7)
            x = bank[n % 8]
            if kind == "ctxT":
                pe.wait_ge(ctx_normed, i + 1)
                last = context_transposes(nc, x, cxn, i, ident)
            elif kind == "wT":
                if i < NQKV:
                    pe.wait_ge(scaled, after_row[i])
                else:
                    pe.wait_ge(w_in[3], 16)
                for k in range(KC):
                    last = nc.tensor.transpose(x[:, P * k:P * k + P], nat[:, i, P * k:P * k + P], ident[:])
            elif kind == "keys":
                if i == 0:
                    pe.wait_ge(drained, after_job["wT", 2 * KC - 1])
                for k in range(KC):
                    last = nc.tensor.matmul(x[:, 0:CW], wt[:, 1, k, P * i:P * i + P], ct[:, k, :],
                                            start=(k == 0), stop=(k == KC - 1))
            elif kind == "values":
                if i == 0:
                    pe.wait_ge(drained, after_job["wT", NQKV - 1])
                cols = context_columns(i)
                for k in range(KC):
                    last = nc.tensor.matmul(x[0:cols.stop - cols.start, :], ct[:, k, cols], wt[:, 2, k, :],
                                            start=(k == 0), stop=(k == KC - 1))
            elif kind == "aa":
                pe.wait_ge(small_in, SMALL)
                last = nc.tensor.transpose(x[:, 0:STATE], a2[:], ident[0:STATE, 0:STATE])
            elif kind == "wprogT":
                for k in range(KC):
                    last = nc.tensor.transpose(x[0:64, P * k:P * k + P], wp[:, k, :], ident[:])
            elif kind == "mean":
                for b in range(BATCH):
                    nc.tensor.matmul(x[0:64, b:b + 1], pp[:, b, :], ones[:, 0:1], start=True, stop=False)
                    last = nc.tensor.matmul(x[0:64, b:b + 1], ppr[:, b, :], ones[:, 0:1], start=False, stop=True)
            elif kind == "wu":
                pe.wait_ge(win_in, 16)
                for c in range(KC):
                    for k in range(KC):
                        last = nc.tensor.matmul(x[:, P * c:P * c + P], win[:, k, P * c:P * c + P], bm[:, k, :],
                                                start=(k == 0), stop=(k == KC - 1))
            elif kind == "ubias":
                pe.wait_ge(drained, after_job["wu", 0])
                for k in range(KC):
                    nc.tensor.matmul(x[:, 0:1], bm[:, k, :], b_in[:, k:k + 1], start=(k == 0), stop=False)
                    last = nc.tensor.matmul(x[:, 0:1], wur[:, k, :], b2[:, k:k + 1], start=False, stop=(k == KC - 1))
            elif kind == "mod":
                pe.wait_ge(mean_ready, i + 1)
                last = nc.tensor.matmul(x[:], mean_wide[:, i, :], wpt[:], start=True, stop=True)
            elif kind == "bo":
                pe.wait_ge(vb_ready, KC)
                for k in range(KC):
                    last = nc.tensor.matmul(x[:], vb_wide[:, k, :], wt[:, 3, k, :], start=(k == 0), stop=(k == KC - 1))
            last.then_inc(filled, 1)



def scan_and_prepare_layer1(nc, ctx, sem, a, keep, l1):
    sb, _ = makers(nc, ctx)
    bank, ident, hu, aa = keep["bank"], keep["ident"], keep["hu"], keep["aa"]
    U = l1["pairs"]
    W = U * P
    stq, stk, sto = sb("wq1_f", [P, KC, W], F32), sb("wk1_f", [P, KC, W], F32), sb("wo1_f", [P, U, D], F32)
    cx, ct = sb("cx1", [P, 3, D], F32), sb("cT", [P, KC, CW], F32)
    bk, bv, bv_wide = sb("bk_col", [P, U], F32), sb("bv_col", [P, U], F32), sb("bv_wide", [P, 4, P], F32)
    vbo = sb("values_bias_through_wo1", [P, D], F32)
    ones = sb("ones1", [P, P], F32)
    mask_in = sb("mask_int", [P, BATCH, KEYS], I32)
    ends = sb("ends", [STATE, BATCH, CHUNKS], F32)
    diff, limit, good = sb("diff", [STATE, BATCH, CHUNKS], F32), sb("limit", [STATE, 1], F32), sb("good", [STATE, 1], F32)
    flag = sb("unsettled", [1, 1], I32)

    wq_in, wk_in, wo_in, small_in, wv_in = (sem(f"s_{x}_in") for x in ("wq", "wk", "wo", "small", "wv"))
    padded, zeroed, consts, dve_step = sem("s_padded"), sem("s_zeroed"), sem("s_consts"), sem("s_dve_step")
    z_ready, h_ready, ends_kept = sem("s_z_ready"), sem("s_h_ready"), sem("s_ends_kept")
    goods_ready, goods_summed, flag_ready = sem("s_goods_ready"), sem("s_goods_summed"), sem("s_flag_ready")
    split, filled, drained, wide_ready = sem("s_split"), sem("s_filled"), sem("s_drained"), sem("s_wide_ready")
    wide_used = sem("s_wide_used")

    jobs = [("ctxT", g) for g in range(3)] + [("keys", u) for u in range(U)]
    jobs += [("values", (g, half)) for half in range(W // D) for g in range(3)] + [("bo", 0)]
    after_job = {job: n + 1 for n, job in enumerate(jobs)}
    SMALL = 16 * (4 + 7)
    SCAN_STEPS = ROUNDS * CHUNK
    before = hu[:, :, 0:SEQ].rearrange("p b (c s) -> p b c s", s=CHUNK)
    state = hu[:, :, 1:1 + SEQ].rearrange("p b (c s) -> p b c s", s=CHUNK)

    block = ctx.enter_context(nc.Block())

    @block.sync
    def _(sp):
        sp.dma_start(stq[:], a["Wq"].rearrange("(k p) n -> p k n", p=P)).then_inc(wq_in, 16)
        sp.dma_start(sto[:], a["Wo"].rearrange("(k p) n -> p k n", p=P)).then_inc(wo_in, 16)
        sp.wait_ge(padded, 1)
        for b in range(BATCH):
            sp.dma_start(cx[:, b, :], a["ctx"][b, 0:MAIN, :]).then_inc(small_in, 16)
            sp.dma_start(cx[GAP * b:GAP * b + REM, 2, :], a["ctx"][b, MAIN:KEYS, :]).then_inc(small_in, 16)
        sp.dma_start(stk[:], a["Wk"].rearrange("(k p) n -> p k n", p=P)).then_inc(wk_in, 16)
        for b in range(BATCH):
            sp.dma_start(mask_in[:, b, :], load_row(a["mask"][b])).then_inc(small_in, 16)
        sp.dma_start(bk[:], a["bk"].rearrange("(c p) -> p c", p=P), allow_slow_non_contiguous=True).then_inc(small_in, 16)
        sp.dma_start(bv[:], a["bv"].rearrange("(c p) -> p c", p=P), allow_slow_non_contiguous=True).then_inc(small_in, 16)
        sp.dma_start(l1["nbq"][:], a["bq"].rearrange("(c p) -> p c", p=P), allow_slow_non_contiguous=True).then_inc(small_in, 16)
        sp.dma_start(l1["bo"][:], load_row(a["bo"])).then_inc(small_in, 16)
        sp.dma_start(l1["gamma"][:], load_row(a["gamma"])).then_inc(small_in, 16)
        sp.wait_ge(split, 2)
        sp.dma_start(stq[:], a["Wv"].rearrange("(k p) n -> p k n", p=P)).then_inc(wv_in, 16)
        sp.dma_start(l1["beta"][:], load_row(a["beta"])).then_inc(wv_in, 16)
        sp.wait_ge(wv_in, 32)

    @block.gpsimd
    def _(pool):
        nc.gpsimd.memset(cx[0:2 * GAP, 2, :], 0.0).then_inc(padded, 1)
        nc.gpsimd.memset(ones[:], 1.0).then_inc(consts, 1)
        nc.gpsimd.memset(l1["kbd"][:], 0.0).then_inc(zeroed, 1)
        nc.gpsimd.memset(l1["vr"][:], 0.0).then_inc(zeroed, 1)

    @block.tensor
    def _(pe):
        def scan_step(t, s):
            for b in range(BATCH):
                pe.wait_ge(h_ready, BATCH * s + b + 1)
                nc.tensor.matmul(bank[b][0:STATE, 0:CHUNKS], aa[:], before[:, b, :, bass.ds(t, 1)],
                                 start=True, stop=True).then_inc(z_ready, 1)

        with pe.Fori(0, ROUNDS, 1) as r:
            with pe.Fori(0, CHUNK, 1) as t:
                scan_step(t, r * CHUNK + t)
        pe.wait_ge(consts, 1)
        pe.wait_ge(goods_ready, 1)
        nc.tensor.matmul(bank[2][0:1, 0:1], good[:], ones[0:STATE, 0:1], start=True, stop=True).then_inc(goods_summed, 1)
        pe.wait_ge(flag_ready, 1)
        unsettled = pe.value_load(flag[0:1, 0:1], min_val=0, max_val=1)
        with pe.If(unsettled > 0):
            with pe.Fori(0, CHUNKS - ROUNDS, 1) as r:
                with pe.Fori(0, CHUNK, 1) as t:
                    scan_step(t, r * CHUNK + t + SCAN_STEPS)
        for n, (kind, i) in enumerate(jobs):
            after(pe, drained, n - 7)
            x = bank[n % 8]
            if kind == "ctxT":
                pe.wait_ge(small_in, SMALL)
                last = context_transposes(nc, x, cx, i, ident)
            elif kind == "keys":
                if i == 0:
                    pe.wait_ge(wk_in, 16)
                    pe.wait_ge(drained, after_job["ctxT", 2])
                for k in range(KC):
                    last = nc.tensor.matmul(x[:, 0:CW], stk[:, k, P * i:P * i + P], ct[:, k, :],
                                            start=(k == 0), stop=(k == KC - 1))
            elif kind == "values":
                group, part = i
                if i == (0, 0):
                    pe.wait_ge(wv_in, 32)
                cols = context_columns(group)
                for k in range(KC):
                    last = nc.tensor.matmul(x[0:cols.stop - cols.start, :], ct[:, k, cols], stq[:, k, D * part:D * part + D],
                                            start=(k == 0), stop=(k == KC - 1))
            elif kind == "bo":
                for k in range(U):
                    pe.wait_ge(wide_ready, k + 1)
                    last = nc.tensor.matmul(x[:], bv_wide[:, k % 4, :], sto[:, k, :], start=(k == 0), stop=(k == U - 1))
                    if k < U - 1:
                        last.then_inc(wide_used, 1)
            last.then_inc(filled, 1)

    @block.scalar
    def _(act):
        def scan_step(t, s):
            for b in range(BATCH):
                act.wait_ge(z_ready, BATCH * s + b + 1)
                nc.scalar.activation(state[0:STATE, b, :, bass.ds(t, 1)], bank[b][0:STATE, 0:CHUNKS].unsqueeze(2),
                                     ACT.Silu).then_inc(h_ready, 1)

        act.sem_inc(h_ready, BATCH)
        for r in range(ROUNDS):
            with act.Fori(0, CHUNK - 1, 1) as t:
                scan_step(t, t + r * CHUNK)
            if r == ROUNDS - 1:
                act.wait_ge(ends_kept, 1)
            scan_step(CHUNK - 1, CHUNK - 1 + r * CHUNK)
        act.wait_ge(flag_ready, 1)
        unsettled = act.value_load(flag[0:1, 0:1], min_val=0, max_val=1)
        with act.If(unsettled > 0):
            with act.Fori(0, CHUNKS - ROUNDS, 1) as r:
                with act.Fori(0, CHUNK, 1) as t:
                    scan_step(t, r * CHUNK + t + SCAN_STEPS)
        for n, (kind, i) in enumerate(jobs):
            act.wait_ge(filled, n + 1)
            x = bank[n % 8]
            if kind == "ctxT":
                cols = context_columns(i)
                w = cols.stop - cols.start
                last = nc.scalar.activation(ct[:, :, cols], x[:, 0:KC * w].rearrange("p (k c) -> p k c", k=KC), ACT.Copy)
            elif kind == "keys":
                if i == 0:
                    act.wait_ge(small_in, SMALL)
                    act.wait_ge(zeroed, 2)
                last = evacuate_keys(nc, x, l1, i, bk[:, i:i + 1])
            elif kind == "values":
                last = evacuate_values(nc, x, l1, i[0], D * i[1])
            elif kind == "bo":
                last = nc.scalar.activation(vbo[:], x[:], ACT.Copy)
            last.then_inc(drained, 1)

    @block.vector
    def _(dve):
        step = Chain(dve, dve_step)
        done = [split, 0]
        dve.wait_ge(wq_in, 16)
        split_weight(nc, dve, [w[:] for w in l1["wq"]], stq[:], done)
        dve.wait_ge(h_ready, BATCH + BATCH * (ROUNDS - 1) * CHUNK)
        nc.vector.tensor_copy(ends[:], state[0:STATE, :, :, CHUNK - 1]).then_inc(ends_kept, 1)
        dve.wait_ge(wo_in, 16)
        split_weight(nc, dve, [w[:] for w in l1["wo"]], sto[:], done)
        dve.wait_ge(small_in, SMALL)
        step.then(nc.vector.tensor_scalar(l1["nbq"][:], l1["nbq"][:], -SCALE, None, ALU.mult))
        for h, (dst, src, n) in enumerate(((0, 0, KEYS), (REM, 0, MAIN), (0, MAIN, REM))):
            nc.vector.tensor_scalar(l1["mask"][:, :, min(h, 1), dst:dst + n], mask_in[:, :, src:src + n], 0, MASKED,
                                    ALU.is_equal, ALU.mult)
        dve.wait_ge(h_ready, BATCH + BATCH * SCAN_STEPS)
        dve.wait_ge(ends_kept, 1)
        now = state[0:STATE, :, :, CHUNK - 1]
        step.then(nc.vector.tensor_tensor(diff[:], now, ends[:], ALU.subtract))
        step.then(nc.vector.tensor_tensor(diff[:], diff[:], diff[:], ALU.mult))
        step.then(nc.vector.tensor_tensor(ends[:], now, now, ALU.mult))
        step.then(nc.vector.tensor_reduce(limit[:], ends[:].rearrange("p b c -> p (b c)"), AX_X, ALU.max))
        step.then(nc.vector.tensor_scalar(limit[:], limit[:], SETTLED * SETTLED, None, ALU.mult))
        step.then(nc.vector.tensor_scalar(diff[:], diff[:], limit[:], None, ALU.is_le))
        nc.vector.tensor_reduce(good[:], diff[:].rearrange("p b c -> p (b c)"), AX_X, ALU.add).then_inc(goods_ready, 1)
        dve.wait_ge(goods_summed, 1)
        nc.vector.tensor_scalar(flag[:], bank[2][0:1, 0:1], float(STATE * BATCH * CHUNKS) - 0.5, None,
                                ALU.is_lt).then_inc(flag_ready, 1)
        dve.wait_ge(consts, 1)
        for k in range(U):
            after(dve, wide_used, k - 3)
            nc.vector.tensor_scalar(bv_wide[:, k % 4, :], ones[:], bv[:, k:k + 1], None, ALU.mult).then_inc(wide_ready, 1)
        dve.wait_ge(drained, after_job["bo", 0])
        nc.vector.tensor_tensor(l1["bo"][:], l1["bo"][:], vbo[:], ALU.add)



def run_layer(nc, ctx, sem, layer, keep, l, src_dram, dst_dram):
    sb, _ = makers(nc, ctx)
    name = lambda x: f"{x}_l{layer}"
    U = l["pairs"]
    hu, cc, ident = keep["hu"], keep["cc"], keep["ident"]
    ring = sb(name("ring"), [P, SLOTS, D], F32)
    xt = [sb(name(f"xT_{x}"), [P, KC, BLOCK], F32R) for x in ("high", "low")]
    qt = [sb(name(f"qT{i}"), [P, U, BLOCK], F32) for i in range(2)]
    probs = sb(name("probs"), [P, 2, PW], F32)
    pt = sb(name("probsT"), [P, 2, 3 * P], F32)
    heads = sb(name("heads"), [P, D], F32)
    cat = [sb(name(f"catT_{x}"), [P, KC, P], F32R) for x in ("high", "low")]
    least = sb(name("least"), [P, 4, 2], F32)
    sums = sb(name("sums"), [P, 2, 2 * KC], F32)
    inv = sb(name("inv"), [P, 2 * KC], F32)
    half = sb(name("minus_half"), [P, 1], F32)
    rstd = sb(name("rstd"), [P, 2], F32)
    stats, mv = sb(name("stats"), [P, 2, 6], F32), sb(name("mv"), [P, 2, 2], F32)
    if layer == 0:
        xn = sb(name("xn"), [P, 2, D], F32)
        yn = sb(name("yn"), [P, D], F32)
    else:
        hs = sb(name("scan_tile"), [P, 2, P], F32)
        mask = sb(name("mask_now"), [P, 2, KEYS], F32)
    S, PT, O, T, G, W = keep["bank"][0:2], keep["bank"][2], keep["bank"][3], keep["bank"][4], keep["bank"][5:7], keep["bank"][7]

    slot_in = [sem(name(f"slot_in{i}")) for i in range(SLOTS)]
    slot_out = [sem(name(f"slot_out{i}")) for i in range(SLOTS)]
    s = {x: sem(name(x)) for x in (
        "pads", "tile_step", "tile_stats", "tile_rstd", "tile_normed", "bias_added", "hs_ready",
        "T_filled", "T_high", "T_drained", "G_filled", "G_drained", "scores_ready", "least_ready",
        "probs_ready", "pt_filled", "pt_drained", "pv_done", "inverses", "heads_ready", "cat_used",
        "W_drained", "out_step", "out_stats", "out_rstd", "out_normed", "out_pool", "out_ready", "mask_ready",
        "passed_dve", "passed_pool")}
    plan = dict(
        start=layer0_start() if layer == 0 else layer1_start(),
        items=layer0_items if layer == 0 else layer1_items,
        end=layer0_end() if layer == 0 else layer1_end(),
    )
    rows = lambda it: bass.ds(it.tile * P, P)
    hu_flat = hu[:].rearrange("p b s -> p (b s)")
    hu_cols = lambda it: bass.ds(it.tile * P + it.batch + 1, P)
    kbd = l["kbd"][:].rearrange("p b u c -> p (b u c)")
    vm = l["vm"][:].rearrange("p b c -> p (b c)")
    vr = l["vr"][:].rearrange("p b u c -> p (b u c)")

    block = ctx.enter_context(nc.Block())

    @block.sync
    def _(sp):
        for it in walk(sp, **plan):
            if it.kind == "LD":
                stored = it.done(("ST", it.slot))
                if not isinstance(stored, int) or stored:
                    sp.wait_ge(slot_out[it.slot], 16 * stored)
                sp.dma_start(ring[:, it.slot, :], src_dram[rows(it), :]).then_inc(slot_in[it.slot], 16)
            elif it.kind == "ST":
                sp.wait_ge(s["out_ready"], it.done("ST") + 1)
                sp.dma_start(dst_dram[rows(it), :], ring[:, it.slot, :]).then_inc(slot_out[it.slot], 16)
        for i in range(SLOTS):
            sp.wait_ge(slot_out[i], 16 * (NBLK // 2))

    @block.tensor
    def _(pe):
        def transposes(it, chunk):
            after(pe, s["T_drained"], it.done("T"))
            for k in range(KC):
                last = nc.tensor.transpose(T[:, P * k:P * k + P], chunk(k), ident[:])
            last.then_inc(s["T_filled"], 1)

        for it in walk(pe, **plan):
            if it.kind == "SS":
                pe.wait_ge(s["hs_ready"], it.done("SS") + 1)
                after(pe, s["T_drained"], it.done("T"))
                nc.tensor.matmul(T[:], hs[:, it.side("SS"), :], cc[:], start=True, stop=True).then_inc(s["T_filled"], 1)
            elif it.kind == "XT":
                if layer == 0:
                    pe.wait_ge(s["tile_normed"], it.done("XT") + 1)
                    transposes(it, lambda k: xn[:, it.idx % 2, P * k:P * k + P])
                else:
                    transposes(it, lambda k: ring[:, it.slot, P * k:P * k + P])
            elif it.kind == "Q":
                after(pe, s["T_drained"], it.done("T"))
                after(pe, s["G_drained"], it.done("G") - 1)
                for k in range(KC):
                    last = product(nc, G[it.side("G")][:], [w[:, k, P * it.idx:P * it.idx + P] for w in l["wq"]],
                                   [x[:, k, :] for x in xt], start=(k == 0), stop=(k == KC - 1))
                last.then_inc(s["G_filled"], 1)
            elif it.kind == "S":
                t, u = divmod(it.idx, U)
                if it.idx == 0:
                    pe.wait_ge(s["G_drained"], it.done("G"))
                after(pe, s["probs_ready"], it.done("S") - 1)
                nc.tensor.matmul(S[it.idx % 2][:, 0:PAIRW], qt[it.par][:, u, P * t:P * t + P],
                                 kbd[:, bass.ds(it.batch * (U * PAIRW) + u * PAIRW, PAIRW)],
                                 start=True, stop=True).then_inc(s["scores_ready"], 1)
            elif it.kind == "PT":
                pe.wait_ge(s["probs_ready"], it.done("PT") + 1)
                after(pe, s["pt_drained"], it.done("PT"))
                side = it.idx % 2
                for n, col in enumerate((0, SECOND + REM, MAIN)):
                    last = nc.tensor.transpose(PT[:, P * n:P * n + P], probs[:, side, col:col + P], ident[:])
                last.then_inc(s["pt_filled"], 1)
            elif it.kind == "PV":
                u, side = it.idx % U, it.idx % 2
                first, col = it.idx % KC == 0, P * (it.idx % KC)
                pe.wait_ge(s["pt_drained"], it.done("PT"))
                if first:
                    after(pe, s["heads_ready"], it.done("ON"))
                nc.tensor.matmul(O[:, col:col + P], pt[:, side, 2 * P:3 * P],
                                 vr[:, bass.ds(it.batch * (U * P) + u * P, P)], start=first, stop=False)
                for h in range(2):
                    last = nc.tensor.matmul(O[:, col + HD * h:col + HD * h + HD], pt[:, side, P * h:P * h + P],
                                            vm[:, bass.ds(it.batch * (U * P) + u * P + HD * h, HD)],
                                            start=False, stop=(it.idx % KC == KC - 1 and h == 1))
                last.then_inc(s["pv_done"], 1)
            elif it.kind == "OT":
                pe.wait_ge(s["heads_ready"], it.done("ON"))
                transposes(it, lambda k: heads[:, P * k:P * k + P])
            elif it.kind == "WO":
                part = it.idx % 2 if layer else 0
                pe.wait_ge(s["T_drained"], it.done("T"))
                if part == 0:
                    tile = it.done("WO") if layer == 0 else it.blk * TILES + it.idx // 2
                    after(pe, s["W_drained"], tile)
                for k in range(KC):
                    last = product(nc, W[:], [x[:, k, :] for x in cat], [w[:, KC * part + k, :] for w in l["wo"]],
                                   start=(k == 0 and part == 0), stop=(k == KC - 1 and (part == 1 or layer == 0)))
                last.then_inc(s["cat_used"], 1)
            elif it.kind == "YT":
                pe.wait_ge(s["out_normed"], it.done("YT") + 1)
                transposes(it, lambda k: yn[:, P * k:P * k + P])
            elif it.kind == "U":
                pe.wait_ge(s["T_drained"], it.done("T"))
                after(pe, s["G_drained"], it.done("G") - 1)
                for k in range(KC):
                    last = product(nc, G[it.side("G")][:, 0:P], [w[:, k, :] for w in l["wu"]],
                                   [x[:, k, :] for x in cat], start=(k == 0), stop=(k == KC - 1))
                last.then_inc(s["cat_used"], 1)

    @block.scalar
    def _(act):
        bank_T = T[:].rearrange("p (k c) -> p k c", k=KC)
        act.wait_ge(s["pads"], 1)
        for it in walk(act, **plan):
            if it.kind in ("XT", "OT", "YT"):
                act.wait_ge(s["T_filled"], it.done("T") + 1)
                if it.kind == "XT":
                    after(act, s["G_filled"], it.done("Q"))
                    dst = xt[0][:, :, P * it.idx:P * it.idx + P]
                else:
                    after(act, s["cat_used"], it.done("cat_read"))
                    dst = cat[0][:]
                nc.scalar.activation(dst, bank_T, ACT.Copy).then_inc(s["T_high"], 1)
            elif it.kind == "Q":
                act.wait_ge(s["G_filled"], it.done("Q") + 1)
                nc.scalar.activation(qt[it.par][:, it.idx, :], G[it.side("G")][:], ACT.Identity, scale=-SCALE,
                                     bias=l["nbq"][:, it.idx:it.idx + 1]).then_inc(s["G_drained"], 1)
            elif it.kind == "U":
                act.wait_ge(s["cat_used"], it.done("cat_read") + 1)
                nc.scalar.activation(hu_flat[STATE:P, hu_cols(it)], G[it.side("G")][STATE:P, 0:P], ACT.Identity,
                                     bias=l["ubias"][STATE:P]).then_inc(s["G_drained"], 1)
            elif it.kind == "S":
                side, o = it.idx % 2, it.idx // KC
                act.wait_ge(s["least_ready"], it.done("S") + 1)
                after(act, s["pt_filled"], it.done("S") - 1)
                for h in range(2):
                    col = 2 * (it.idx % KC) + h
                    last = nc.scalar.activation(probs[:, side, SECOND * h:SECOND * h + KEYS], S[side][:, KEYS * h:KEYS * h + KEYS],
                                                ACT.Exp, scale=-1.0, bias=least[:, it.idx % 4, h:h + 1],
                                                accum_out=sums[:, o % 2, col:col + 1])
                last.then_inc(s["probs_ready"], 1)

    @block.vector
    def _(dve):
        bank_T = T[:].rearrange("p (k c) -> p k c", k=KC)

        def statistics(which, x, step, count, ready):
            nc.vector.bn_stats(stats[:, which, :], x).then_inc(step, 1)
            dve.wait_ge(step, 2 * count + 1)
            dve.sem_inc(s["passed_dve"], 1)
            nc.vector.bn_aggr(mv[:, which, :], stats[:, which, :]).then_inc(step, 1)
            dve.wait_ge(step, 2 * count + 2)
            nc.vector.tensor_scalar(mv[:, which, 1:2], mv[:, which, 1:2], EPS, None, ALU.add).then_inc(ready, 1)

        for it in walk(dve, **plan):
            if it.kind == "LN":
                dve.wait_ge(slot_in[it.slot], 16 * it.done(("LD", it.slot)))
                after(dve, s["tile_normed"], it.done("LN"))
                statistics(0, ring[:, it.slot, :], s["tile_step"], it.done("LN"), s["tile_stats"])
            elif it.kind == "SS":
                dve.wait_ge(slot_in[it.slot], 16 * it.done(("LD", it.slot)))
                dve.wait_ge(s["T_filled"], it.done("T") + 1)
                nc.vector.tensor_tensor(ring[:, it.slot, :], T[:], ring[:, it.slot, :], ALU.add).then_inc(s["T_drained"], 1)
            elif it.kind in ("XT", "OT", "YT"):
                dve.wait_ge(s["T_high"], it.done("split") + 1)
                high, low = ([x[:, :, P * it.idx:P * it.idx + P] for x in xt] if it.kind == "XT" else [x[:] for x in cat])
                nc.vector.tensor_tensor(low, bank_T, high.bitcast(F32), ALU.subtract).then_inc(s["T_drained"], 1)
            elif it.kind == "S":
                if layer == 1 and it.idx == 0:
                    after(dve, s["least_ready"], it.done("S"))
                    nc.vector.tensor_copy(mask[:].rearrange("p h k -> p (h k)"), l["mask"][:].rearrange("p b h k -> p (b h k)")[
                        :, bass.ds(it.batch * PAIRW, PAIRW)]).then_inc(s["mask_ready"], 1)
                    dve.wait_ge(s["mask_ready"], it.blk + 1)
                dve.wait_ge(s["scores_ready"], it.done("S") + 1)
                after(dve, s["probs_ready"], it.done("S") - 3)
                dve.sem_inc(s["passed_dve"], 1)
                bank_S = S[it.idx % 2]
                if layer == 0:
                    nc.vector.tensor_reduce(least[:, it.idx % 4, :], bank_S[:, 0:PAIRW].rearrange("p (h k) -> p h k", h=2),
                                            AX_X, ALU.min).then_inc(s["least_ready"], 1)
                else:
                    for h in range(2):
                        cols = bank_S[:, KEYS * h:KEYS * h + KEYS]
                        last = nc.vector.tensor_tensor_reduce(out=cols, in0=cols, in1=mask[:, h, :], scale=1.0, scalar=NO_KEY,
                                                              op0=ALU.add, op1=ALU.min, accum_out=least[:, it.idx % 4, h:h + 1])
                    last.then_inc(s["least_ready"], 1)
            elif it.kind == "PT":
                dve.wait_ge(s["pt_filled"], it.done("PT") + 1)
                after(dve, s["pv_done"], it.done("PT") - 1)
                nc.vector.tensor_copy(pt[:, it.idx % 2, :], PT[:, 0:3 * P]).then_inc(s["pt_drained"], 1)
            elif it.kind == "ON":
                dve.wait_ge(s["pv_done"], KC * (it.done("ON") + 1))
                nc.vector.reciprocal(inv[:], sums[:, it.idx % 2, :]).then_inc(s["inverses"], 1)
                dve.wait_ge(s["inverses"], it.done("ON") + 1)
                nc.vector.tensor_tensor(heads[:].rearrange("p (h d) -> p h d", d=HD), O[:].rearrange("p (h d) -> p h d", d=HD),
                                        inv[:].unsqueeze(2).to_broadcast([P, 2 * KC, HD]), ALU.mult).then_inc(s["heads_ready"], 1)
            elif it.kind == "WO" and (layer == 0 or it.idx % 2 == 1):
                tile = it.blk * TILES + (it.idx if layer == 0 else it.idx // 2)
                slot = TILES * it.par + (it.idx if layer == 0 else it.idx // 2)
                x = ring[:, slot, :]
                dve.wait_ge(s["cat_used"], it.done("cat_read") + 1)
                dve.wait_ge(s["bias_added"], tile + 1)
                nc.vector.tensor_tensor(x, W[:], x, ALU.add).then_inc(s["W_drained"], 1)
                dve.wait_ge(s["W_drained"], tile + 1)
                after(dve, s["out_normed"], tile)
                statistics(1, x, s["out_step"], tile, s["out_stats"])

    @block.gpsimd
    def _(pool):
        nc.gpsimd.memset(probs[:], 0.0)
        nc.gpsimd.memset(half[:], -0.5).then_inc(s["pads"], 1)
        pool.wait_ge(s["pads"], 1)
        for it in walk(pool, **plan):
            if it.kind == "LN":
                x = ring[:, it.slot, :]
                pool.wait_ge(s["tile_stats"], it.done("LN") + 1)
                nc.gpsimd.tensor_tensor(rstd[:, 0:1], mv[:, 0, 1:2], half[:], ALU.pow).then_inc(s["tile_rstd"], 1)
                pool.wait_ge(s["tile_rstd"], it.done("LN") + 1)
                after(pool, s["T_filled"], it.done("T"))
                pool.sem_inc(s["passed_pool"], 1)
                nc.gpsimd.tensor_scalar(xn[:, it.idx % 2, :], x, mv[:, 0, 0:1], rstd[:, 0:1], ALU.subtract,
                                        ALU.mult).then_inc(s["tile_normed"], 1)
                pool.wait_ge(s["tile_normed"], it.done("LN") + 1)
                nc.gpsimd.tensor_tensor(x, x, l["bo"][:], ALU.add).then_inc(s["bias_added"], 1)
            elif it.kind == "SS":
                after(pool, s["T_filled"], it.done("T"))
                nc.gpsimd.tensor_copy(hs[:, it.side("SS"), :], hu_flat[:, hu_cols(it)]).then_inc(s["hs_ready"], 1)
            elif it.kind == "XT" and layer == 1:
                x = ring[:, it.slot, :]
                pool.wait_ge(s["T_filled"], it.done("T") + 1)
                nc.gpsimd.tensor_tensor(x, x, l["bo"][:], ALU.add).then_inc(s["bias_added"], 1)
            elif it.kind == "WO" and (layer == 0 or it.idx % 2 == 1):
                tile = it.blk * TILES + (it.idx if layer == 0 else it.idx // 2)
                x = ring[:, TILES * it.par + (it.idx if layer == 0 else it.idx // 2), :]
                pool.wait_ge(s["out_stats"], tile + 1)
                nc.gpsimd.tensor_tensor(rstd[:, 1:2], mv[:, 1, 1:2], half[:], ALU.pow).then_inc(s["out_rstd"], 1)
                pool.wait_ge(s["out_rstd"], tile + 1)
                if layer == 0:
                    after(pool, s["T_filled"], it.done("T"))
                pool.sem_inc(s["passed_pool"], 1)
                nc.gpsimd.tensor_scalar(yn[:] if layer == 0 else x, x, mv[:, 1, 0:1], rstd[:, 1:2], ALU.subtract,
                                        ALU.mult).then_inc(s["out_normed"], 1)
                pool.wait_ge(s["out_normed"], tile + 1)
                if layer == 0:
                    pool.sem_inc(s["passed_pool"], 1)
                    nc.gpsimd.tensor_tensor(x, x, l["mod"][:].rearrange("p b n -> p (b n)")[:, bass.ds(it.batch * D, D)],
                                            ALU.add).then_inc(s["out_ready"], 1)
                else:
                    nc.gpsimd.tensor_tensor(x, x, l["gamma"][:], ALU.mult).then_inc(s["out_pool"], 1)
                    pool.wait_ge(s["out_pool"], tile + 1)
                    nc.gpsimd.tensor_tensor(x, x, l["beta"][:], ALU.add).then_inc(s["out_ready"], 1)


_INS = {
    "x": "x", "ctx": "ctx_1024", "pp": "ctxb_2048x64", "mask": "mask_BxS2_ik0",
    "A": "L0_xattn_A", "Bmat": "L0_xattn_Bmat", "Cmat": "L0_xattn_Cmat", "W_in": "L0_xattn_W_in",
    "b_in": "L0_xattn_b_in", "W_qkv": "L0_xattn_W_qkv", "b_qkv": "L0_xattn_b_qkv", "W_o": "L0_xattn_W_o",
    "b_o": "L0_xattn_b_o", "W_prog": "L0_xattn_W_prog", "b_prog": "L0_xattn_b_prog", "g1": "L0_xattn_g1",
    "beta1": "L0_xattn_beta1", "g2": "L0_xattn_g2", "beta2": "L0_xattn_beta2",
    "Wq": "L1_xattn_Wq", "bq": "L1_xattn_bq", "Wk": "L1_xattn_Wk", "bk": "L1_xattn_bk", "Wv": "L1_xattn_Wv",
    "bv": "L1_xattn_bv", "Wo": "L1_xattn_Wo", "bo": "L1_xattn_bo", "gamma": "L1_xattn_gamma", "beta": "L1_xattn_beta",
}


def kernel(**inputs):
    import numpy as _np
    import concourse.bacc as _bacc
    from concourse import mybir as _mybir
    from concourse.bass_utils import run_bass_kernel_spmd as _run

    nc = _bacc.Bacc("TRN2", target_bir_lowering=False, num_devices=1)
    arrays, args = {}, {}
    for short, name in _INS.items():
        x = _np.ascontiguousarray(inputs[name])
        if short == "x":
            x = x.reshape(TOKENS, D)
        arrays[f"in_{short}_dram"] = x
        args[short] = nc.dram_tensor(f"in_{short}_dram", x.shape, _mybir.dt.from_np(x.dtype), kind="ExternalInput").ap()
    y = nc.dram_tensor("y_dram", (TOKENS, D), _mybir.dt.float32, kind="ExternalOutput").ap()
    build(nc, args, y)
    got = _run(nc, [arrays], core_ids=[0])
    return got.results[0]["y_dram"].reshape(BATCH, SEQ, D)
```

```python
from collections import Counter
from contextlib import ExitStack

import concourse.bass as bass
from concourse import mybir

F32 = mybir.dt.float32
F32R = mybir.dt.float32r
I32 = mybir.dt.int32
ALU = mybir.AluOpType
ACT = mybir.ActivationFunctionType
AX_X = mybir.AxisListType.X

P = 128
D = 512
KC = D // P
BATCH, SEQ = 2, 2048
TOKENS = BATCH * SEQ
BLOCK = 512
TILES = BLOCK // P
NBLK = TOKENS // BLOCK
BLK_PER_BATCH = SEQ // BLOCK
SLOTS = 2 * TILES
KEYS = 154
MAIN = P
REM = KEYS - MAIN
GAP = 32
CW = 2 * MAIN + 2 * GAP
HD = 64
PAIRW = 2 * KEYS
SECOND = MAIN + GAP
PW = SECOND + KEYS
STATE = 64
EPS = 1e-5
SCALE = 1.0 / 8.0
MASKED = 3.0e38
NO_KEY = 2.0e38
CHUNK = 16
CHUNKS = SEQ // CHUNK
ROUNDS = 2
SETTLED = 2.0 ** -18


def load_row(row):
    return row.rearrange("(a n) -> a n", a=1).broadcast_to([P, row.shape[0]])



PREV, CUR, NEXT = -1, 0, 1
TURN, AHEAD, VALUES, LOW_X, LOW_CAT, FILL, DRAIN, REFILL, STORE = range(9)


def layer0_places():
    steps = TILES * KC
    put = [(g - 2, AHEAD, "S", g) for g in range(steps)] + [(g, TURN, "PT", g) for g in range(steps)]
    put += [(g + 1, VALUES, "PV", g) for g in range(steps)]
    for t in range(TILES):
        end = KC * (t + 1)
        put += [(end, DRAIN, "ON", t), (end + 1, REFILL, "OT", t), (end + 2, LOW_CAT, "OL", t), (end + 3, FILL, "WO", t),
                (end + 4, DRAIN, "RD", t), (end + 5, DRAIN, "RN", t), (end + 5, STORE, "ST", t),
                (end + 7, REFILL, "YT", t), (end + 8, LOW_CAT, "YL", t), (end + 9, FILL, "U", t)]
    for j, (load, norm, turn) in enumerate(((0, 0, 1), (0, 1, 3), (1, 5, 6), (5, 8, 9))):
        put += [(load - steps, STORE, "LD", j), (norm - steps, STORE, "LN", j)]
        put += [(turn - steps, FILL, "XT", j), (turn + 1 - steps, LOW_X, "XL", j)]
    put += [(g, FILL, "Q", c) for c, g in enumerate((10 - steps, 12 - steps, 14 - steps, 0))]
    return steps, put


def layer1_places():
    pairs = 2 * KC
    steps = TILES * pairs
    put = [(g - 2, AHEAD, "S", g) for g in range(steps)] + [(g, TURN, "PT", g) for g in range(steps)]
    put += [(g + 1, VALUES, "PV", g) for g in range(steps)]
    for o in range(2 * TILES):
        end = KC * (o + 1)
        put += [(end, DRAIN, "ON", o), (end + 1, REFILL, "OT", o), (end + 2, LOW_CAT, "OL", o), (end + 3, FILL, "WO", o)]
        if o % 2:
            put += [(end + 4, DRAIN, "RD", o // 2), (end + 5, DRAIN, "RN", o // 2), (end + 7, STORE, "ST", o // 2)]
    for j, (load, add, turn) in enumerate(((0, 4, 5), (0, 6, 7), (0, 8, 9), (7, 11, 12))):
        put += [(load - steps, STORE, "LD", j), (j - steps, TURN, "HS", j), (add - steps, FILL, "SS", j)]
        put += [(turn - steps, FILL, "XT", j), (turn + 1 - steps, LOW_X, "XL", j)]
    put += [(g, FILL, "Q", c) for c, g in enumerate((13 - steps, 17 - steps, 21 - steps, 25 - steps, 29 - steps, 0, 2, 4))]
    return steps, put


class Plan:

    def __init__(self, steps, put):
        self.steps, self.put = steps, sorted(put, key=lambda x: (x[0], x[1]))

    def start(self):
        return [(kind, NEXT, idx) for step, _, kind, idx in self.put if step < 0]

    def items(self, first=False, last=False):
        at = []
        for rel in (PREV, CUR, NEXT):
            if (rel == PREV and first) or (rel == NEXT and last):
                continue
            for step, phase, kind, idx in self.put:
                here = step + rel * self.steps
                if 0 <= here < self.steps:
                    at.append((here, phase, kind, rel, idx))
        return [(kind, rel, idx) for _, _, kind, rel, idx in sorted(at, key=lambda x: (x[0], x[1]))]

    def end(self):
        return [(kind, CUR, idx) for step, _, kind, idx in self.put if step >= self.steps]


ALSO = {"SS": ("T", "drained"), "XT": ("T",), "OT": ("T",), "YT": ("T",),
        "XL": ("split", "drained"), "OL": ("split", "drained"), "YL": ("split", "drained"),
        "Q": ("G",), "U": ("G", "cat_read"), "WO": ("cat_read",)}


def counted(items, par):
    n = Counter()
    for kind, rel, idx in items:
        n[kind] += 1
        n.update(ALSO.get(kind, ()))
        if kind in ("LD", "ST"):
            n[kind, TILES * ((par + rel) % 2) + idx] += 1
    return n


class Item:

    def __init__(self, kind, blk, par, idx, seen, per=None, trip=0):
        self.kind, self.blk, self.par, self.idx = kind, blk, par, idx
        self.seen, self.per, self.trip = Counter(seen), per or {}, trip

    def done(self, x):
        return self.seen[x] + (self.per[x] * self.trip if self.per.get(x) else 0)

    def side(self, x):
        assert self.per.get(x, 0) % 2 == 0
        return self.seen[x] % 2

    @property
    def batch(self):
        return self.blk // BLK_PER_BATCH

    @property
    def tile(self):
        return self.blk * TILES + self.idx

    @property
    def slot(self):
        return TILES * self.par + self.idx


def walk(eng, plan):
    base = Counter()

    def straight(some, n, par):
        for kind, rel, idx in some:
            yield Item(kind, n + rel, (par + rel) % 2, idx, base)
            base.update(counted([(kind, rel, idx)], par))

    yield from straight(plan.start(), -1, 1)
    yield from straight(plan.items(first=True), 0, 0)
    body = plan.items()
    trips = (NBLK - 2) // 2
    per = counted(body, 1) + counted(body, 0)
    with eng.Fori(0, trips, 1) as i:
        seen = Counter(base)
        for half in range(2):
            n, par = 2 * i + (1 + half), (1 + half) % 2
            for kind, rel, idx in body:
                yield Item(kind, n + rel, (par + rel) % 2, idx, seen, per, i)
                seen.update(counted([(kind, rel, idx)], par))
    for x in per:
        base[x] += per[x] * trips
    yield from straight(plan.items(last=True), NBLK - 1, (NBLK - 1) % 2)
    yield from straight(plan.end(), NBLK - 1, (NBLK - 1) % 2)


def after(eng, sem, value):
    if isinstance(value, int) and value <= 0:
        return
    eng.wait_ge(sem, value)


class Chain:

    def __init__(self, eng, sem):
        self.eng, self.sem, self.n = eng, sem, 0

    def then(self, ins):
        self.n += 1
        ins.then_inc(self.sem, 1)
        self.eng.wait_ge(self.sem, self.n)


def product(nc, out, stationary, moving, start, stop):
    (sh, sl), (mh, ml) = stationary, moving
    nc.tensor.matmul(out, sh, mh, start=start, stop=False)
    nc.tensor.matmul(out, sh, ml, start=False, stop=False)
    return nc.tensor.matmul(out, sl, mh, start=False, stop=stop)


def build(nc, a, y_dram):
    scratch = nc.dram_tensor("x1_dram", (TOKENS, D), F32, kind="Internal").ap()
    with ExitStack() as ctx:
        sb, sem = makers(nc, ctx)
        keep = dict(
            ident=sb("ident", [P, P], F32),
            hu=sb("hu", [P, BATCH, 1 + SEQ], F32),
            aa=sb("aa", [P, STATE], F32),
            cc=sb("cc", [P, D], F32),
            bank=[ctx.enter_context(nc.psum_tensor(f"bank{i}", [P, 512], F32)) for i in range(8)],
        )
        with ExitStack() as c0:
            sb0, _ = makers(nc, c0)
            l0 = attention_tensors(sb0, "0", KC)
            l0 |= dict(
                wu=[sb0(f"wu_{x}", [P, KC, P], F32R) for x in ("high", "low")],
                ubias=sb0("ubias", [P, 1], F32),
                mod=sb0("mod", [P, BATCH, D], F32),
            )
            with ExitStack() as cp:
                prepare_layer0(nc, cp, sem, a, keep, l0)
            with ExitStack() as cw:
                run_layer(nc, cw, sem, 0, keep, l0, a["x"], scratch)
        with ExitStack() as c1:
            sb1, _ = makers(nc, c1)
            l1 = attention_tensors(sb1, "1", 2 * KC)
            l1 |= dict(
                mask=sb1("mask", [P, BATCH, 2, KEYS], F32),
                gamma=sb1("gamma", [P, D], F32),
                beta=sb1("beta", [P, D], F32),
            )
            with ExitStack() as cs:
                scan_and_prepare_layer1(nc, cs, sem, a, keep, l1)
            with ExitStack() as cw:
                run_layer(nc, cw, sem, 1, keep, l1, scratch, y_dram)


def makers(nc, ctx):
    sb = lambda name, shape, dt: ctx.enter_context(nc.sbuf_tensor(name, shape, dt))
    sem = lambda name: ctx.enter_context(nc.semaphore(name))
    return sb, sem


def attention_tensors(sb, tag, pairs):
    width = pairs * P
    return dict(
        pairs=pairs,
        wq=[sb(f"wq{tag}_{x}", [P, KC, width], F32R) for x in ("high", "low")],
        wo=[sb(f"wo{tag}_{x}", [P, pairs, D], F32R) for x in ("high", "low")],
        nbq=sb(f"nbq{tag}", [P, pairs], F32),
        kbd=sb(f"kbd{tag}", [P, BATCH, pairs, PAIRW], F32),
        vm=sb(f"vm{tag}", [P, BATCH, width], F32),
        vr=sb(f"vr{tag}", [P, BATCH, pairs, P], F32),
        bo=sb(f"bo{tag}", [P, D], F32),
    )


def evacuate_keys(nc, bank, l, u, bias):
    for e, (main, rem) in enumerate(((0, MAIN), (KEYS + REM, KEYS))):
        rows = slice(HD * e, HD * e + HD)
        nc.scalar.activation(l["kbd"][rows, :, u, main:main + MAIN],
                             bank[rows, 0:2 * MAIN].rearrange("p (b k) -> p b k", b=BATCH),
                             ACT.Identity, bias=bias[rows])
        last = nc.scalar.activation(l["kbd"][rows, :, u, rem:rem + REM],
                                    bank[rows, 2 * MAIN:CW].rearrange("p (b k) -> p b k", b=BATCH)[:, :, 0:REM],
                                    ACT.Identity, bias=bias[rows])
    return last


def evacuate_values(nc, bank, l, group, col):
    if group < BATCH:
        return nc.scalar.activation(l["vm"][:, group, col:col + D], bank[:], ACT.Copy)
    first = col // P
    for b in range(BATCH):
        for e in range(2):
            src = bank[GAP * b:GAP * b + REM, :].rearrange("p (u e d) -> p u e d", e=2, d=HD)[:, :, e, :]
            last = nc.scalar.activation(l["vr"][GAP * e:GAP * e + REM, b, first:first + D // P,
                                                HD * e:HD * e + HD], src, ACT.Copy)
    return last


def context_columns(group):
    return slice(group * MAIN, group * MAIN + (MAIN if group < BATCH else 2 * GAP))


def context_transposes(nc, bank, src, group, ident):
    w = MAIN if group < BATCH else 2 * GAP
    for k in range(KC):
        last = nc.tensor.transpose(bank[:, w * k:w * k + w], src[0:w, group, P * k:P * k + P], ident[0:w, 0:w])
    return last


def split_weight(nc, dve, l_pair, src, done):
    high, low = l_pair
    nc.vector.tensor_copy(high, src).then_inc(done[0], 1)
    done[1] += 1
    dve.wait_ge(done[0], done[1])
    nc.vector.tensor_tensor(low, src, high.bitcast(F32), ALU.subtract).then_inc(done[0], 1)
    done[1] += 1



def prepare_layer0(nc, ctx, sem, a, keep, l0):
    sb, _ = makers(nc, ctx)
    bank, ident = keep["bank"], keep["ident"]
    NQKV = 3 * KC
    nat = sb("nat", [P, NQKV + KC, D], F32)
    g1, b1 = sb("g1_row", [P, D], F32), sb("beta1_row", [P, D], F32)
    wt = sb("wt", [P, 4, KC, D], F32)
    product_out = sb("product_out", [P, D], F32)
    vbo = sb("values_bias_through_wo", [P, D], F32)
    wb = sb("wb", [P, NQKV], F32)
    bqkv = sb("bqkv_col", [P, NQKV], F32)
    wbias = sb("wbias", [P, NQKV], F32)
    vb_wide = sb("vb_wide", [P, KC, P], F32)
    cx, cxn = sb("cx", [P, 3, D], F32), sb("cxn", [P, 3, D], F32)
    ct = sb("cnT", [P, KC, CW], F32)
    stats, mv = sb("ctx_stats", [P, 3, 6], F32), sb("ctx_mv", [P, 3, 2], F32)
    half, rstd = sb("ctx_minus_half", [P, 3], F32), sb("ctx_rstd", [P, 3], F32)
    win, bm = sb("win", [P, KC, D], F32), sb("bm", [P, KC, P], F32)
    wur, wug = sb("wu_raw", [P, KC, P], F32), sb("wu_scaled", [P, KC, P], F32)
    g2, b2, b_in = sb("g2_col", [P, KC], F32), sb("beta2_col", [P, KC], F32), sb("b_in_col", [P, KC], F32)
    a2 = sb("a2", [STATE, 2 * STATE], F32)
    pp, ppr = sb("pp", [P, BATCH, 64], F32), sb("pp_rem", [P, BATCH, 64], F32)
    wp, wpt = sb("wprog", [P, KC, 64], F32), sb("wprogT", [64, D], F32)
    bp = sb("bprog_row", [P, D], F32)
    ones = sb("ones", [P, P], F32)
    mean, mean_wide = sb("mean", [64, BATCH], F32), sb("mean_wide", [64, BATCH, P], F32)

    ctx_in, row_in, small_in, win_in = sem("p_ctx_in"), sem("p_row_in"), sem("p_small_in"), sem("p_win_in")
    w_in = [sem(f"p_w_in{i}") for i in range(4)]
    padded, zeroed, consts, pool_step = sem("p_padded"), sem("p_zeroed"), sem("p_consts"), sem("p_pool_step")
    ctx_stats, ctx_normed, dve_step, scaled = sem("p_ctx_stats"), sem("p_ctx_normed"), sem("p_dve_step"), sem("p_scaled")
    biases, filled, drained, split = sem("p_biases"), sem("p_filled"), sem("p_drained"), sem("p_split")
    mean_ready, vb_ready = sem("p_mean_ready"), sem("p_vb_ready")

    jobs = [("ctxT", g) for g in range(3)] + [("wT", r) for r in range(KC, NQKV)]
    jobs += [("keys", u) for u in range(KC)] + [("values", g) for g in range(3)]
    jobs += [("wT", r) for r in list(range(KC)) + list(range(NQKV, NQKV + KC))]
    jobs += [("aa", 0), ("wprogT", 0), ("mean", 0), ("wu", 0), ("ubias", 0), ("mod", 0), ("mod", 1), ("bo", 0)]
    after_job = {job: n + 1 for n, job in enumerate(jobs)}
    rows_order = list(range(KC, NQKV)) + list(range(KC))
    after_row = {r: n + 1 for n, r in enumerate(rows_order)}
    SMALL = 16 * 14

    block = ctx.enter_context(nc.Block())

    @block.sync
    def _(sp):
        sp.wait_ge(padded, 1)
        for b in range(BATCH):
            sp.dma_start(cx[:, b, :], a["ctx"][b, 0:MAIN, :]).then_inc(ctx_in, 16)
            sp.dma_start(cx[GAP * b:GAP * b + REM, 2, :], a["ctx"][b, MAIN:KEYS, :]).then_inc(ctx_in, 16)
        sp.dma_start(g1[:], load_row(a["g1"])).then_inc(row_in, 16)
        sp.dma_start(b1[:], load_row(a["beta1"])).then_inc(row_in, 16)
        wqkv = a["W_qkv"].rearrange("(m r p) n -> m p r n", p=P, r=KC)
        for m in (1, 2, 0):
            sp.dma_start(nat[:, KC * m:KC * m + KC, :], wqkv[m]).then_inc(w_in[m], 16)
        sp.dma_start(nat[:, NQKV:, :], a["W_o"].rearrange("(r p) n -> p r n", p=P)).then_inc(w_in[3], 16)

    @block.scalar
    def _(act):
        act.dma_start(bqkv[:], a["b_qkv"].rearrange("(c p) -> p c", p=P), allow_slow_non_contiguous=True).then_inc(small_in, 16)
        act.dma_start(g2[:], a["g2"].rearrange("(c p) -> p c", p=P), allow_slow_non_contiguous=True).then_inc(small_in, 16)
        act.dma_start(b2[:], a["beta2"].rearrange("(c p) -> p c", p=P), allow_slow_non_contiguous=True).then_inc(small_in, 16)
        act.dma_start(b_in[:], a["b_in"].rearrange("(c p) -> p c", p=P), allow_slow_non_contiguous=True).then_inc(small_in, 16)
        for e in range(2):
            act.dma_start(a2[:, STATE * e:STATE * (e + 1)], a["A"]).then_inc(small_in, 16)
            act.dma_start(keep["cc"][STATE * e:STATE * (e + 1), :], a["Cmat"]).then_inc(small_in, 16)
        act.dma_start(pp[:], a["pp"][:, 0:MAIN, :].rearrange("b p n -> p b n")).then_inc(small_in, 16)
        act.dma_start(wp[:], a["W_prog"].rearrange("(c p) n -> p c n", p=P)).then_inc(small_in, 16)
        act.dma_start(bp[:], load_row(a["b_prog"])).then_inc(small_in, 16)
        act.dma_start(l0["bo"][:], load_row(a["b_o"])).then_inc(small_in, 16)
        act.wait_ge(padded, 3)
        act.dma_start(ppr[0:REM, :, :], a["pp"][:, MAIN:KEYS, :].rearrange("b p n -> p b n")).then_inc(small_in, 16)
        act.dma_start(bm[:, :, STATE:P], a["Bmat"].rearrange("(c p) n -> p c n", p=P)).then_inc(small_in, 16)
        act.dma_start(win[:], a["W_in"].rearrange("(c p) n -> p c n", p=P)).then_inc(win_in, 16)
        for n, (kind, i) in enumerate(jobs):
            act.wait_ge(filled, n + 1)
            x = bank[n % 8]
            if kind == "ctxT":
                cols = context_columns(i)
                w = cols.stop - cols.start
                last = nc.scalar.activation(ct[:, :, cols], x[:, 0:KC * w].rearrange("p (k c) -> p k c", k=KC), ACT.Copy)
            elif kind == "wT":
                m, r = divmod(i, KC)
                last = nc.scalar.activation(wt[:, m, :, P * r:P * r + P], x[:].rearrange("p (k c) -> p k c", k=KC), ACT.Copy)
            elif kind == "keys":
                if i == 0:
                    act.wait_ge(biases, 1)
                    act.wait_ge(zeroed, 2)
                last = evacuate_keys(nc, x, l0, i, wbias[:, KC + i:KC + i + 1])
            elif kind == "values":
                last = evacuate_values(nc, x, l0, i, 0)
            elif kind == "aa":
                last = nc.scalar.activation(keep["aa"][:], x[:, 0:STATE], ACT.Copy)
            elif kind == "wprogT":
                last = nc.scalar.activation(wpt[:], x[0:64, :], ACT.Copy)
            elif kind == "mean":
                last = nc.scalar.activation(mean[:], x[0:64, 0:BATCH], ACT.Copy, scale=1.0 / KEYS)
            elif kind == "wu":
                last = nc.scalar.activation(wur[:], x[:].rearrange("p (c n) -> p c n", c=KC), ACT.Copy)
            elif kind == "ubias":
                last = nc.scalar.activation(l0["ubias"][:], x[:, 0:1], ACT.Copy)
            elif kind == "mod":
                last = nc.scalar.activation(l0["mod"][:, i, :], x[:], ACT.Copy)
            elif kind == "bo":
                last = nc.scalar.activation(vbo[:], x[:], ACT.Copy)
            last.then_inc(drained, 1)

    @block.gpsimd
    def _(pool):
        nc.gpsimd.memset(cx[0:2 * GAP, 2, :], 0.0).then_inc(padded, 1)
        nc.gpsimd.memset(bm[:], 0.0).then_inc(padded, 1)
        nc.gpsimd.memset(ppr[:], 0.0).then_inc(padded, 1)
        nc.gpsimd.memset(ident[:], 0.0).then_inc(pool_step, 1)
        nc.gpsimd.memset(half[:], -0.5).then_inc(pool_step, 1)
        pool.wait_ge(pool_step, 2)
        nc.gpsimd.affine_select(out=ident[:], in_=ident[:], compare_op=ALU.not_equal, fill=1.0, base=0,
                                pattern=[[-1, P]], channel_multiplier=1).then_inc(consts, 1)
        nc.gpsimd.memset(ones[:], 1.0).then_inc(consts, 1)
        nc.gpsimd.memset(l0["kbd"][:], 0.0).then_inc(zeroed, 1)
        nc.gpsimd.memset(l0["vr"][:], 0.0).then_inc(zeroed, 1)
        pool.wait_ge(ctx_stats, 1)
        nc.gpsimd.tensor_tensor(rstd[:], mv[:, :, 1], half[:], ALU.pow).then_inc(pool_step, 1)
        pool.wait_ge(pool_step, 3)
        for g in range(3):
            w = MAIN if g < BATCH else 2 * GAP
            nc.gpsimd.tensor_scalar(cxn[0:w, g, :], cx[0:w, g, :], mv[0:w, g, 0:1], rstd[0:w, g:g + 1],
                                    ALU.subtract, ALU.mult).then_inc(ctx_normed, 1)
        pool.wait_ge(ctx_normed, 3)
        nc.gpsimd.memset(keep["hu"][0:STATE, :, :], 0.0).then_inc(pool_step, 1)
        pool.wait_ge(pool_step, 4)
        nc.gpsimd.memset(keep["hu"][STATE:P, :, 0:1], 0.0)

    @block.vector
    def _(dve):
        step = Chain(dve, dve_step)
        step.then(nc.vector.memset(mv[:], 1.0))
        dve.wait_ge(ctx_in, 64)
        for g in range(3):
            w = MAIN if g < BATCH else 2 * GAP
            step.then(nc.vector.bn_stats(stats[0:w, g, :], cx[0:w, g, :]))
            step.then(nc.vector.bn_aggr(mv[0:w, g, :], stats[0:w, g, :]))
        nc.vector.tensor_scalar(mv[:, :, 1], mv[:, :, 1], EPS, None, ALU.add).then_inc(ctx_stats, 1)
        dve.wait_ge(row_in, 32)
        for r in rows_order:
            dve.wait_ge(w_in[r // KC], 16)
            step.then(nc.vector.tensor_tensor_reduce(out=product_out[:], in0=nat[:, r, :], in1=b1[:], scale=1.0,
                                                     scalar=0.0, op0=ALU.mult, op1=ALU.add,
                                                     accum_out=wb[:, r:r + 1]))
            nc.vector.tensor_tensor(nat[:, r, :], nat[:, r, :], g1[:], ALU.mult).then_inc(scaled, 1)
            if r == NQKV - 1:
                dve.wait_ge(small_in, SMALL)
                nc.vector.tensor_tensor(wbias[:, KC:], bqkv[:, KC:], wb[:, KC:], ALU.add).then_inc(biases, 1)
        step.then(nc.vector.tensor_tensor(wbias[:, 0:KC], bqkv[:, 0:KC], wb[:, 0:KC], ALU.add))
        nc.vector.tensor_scalar(l0["nbq"][:], wbias[:, 0:KC], -SCALE, None, ALU.mult)
        dve.wait_ge(consts, 2)
        dve.wait_ge(biases, 1)
        for k in range(KC):
            nc.vector.tensor_scalar(vb_wide[:, k, :], ones[:], wbias[:, 2 * KC + k:2 * KC + k + 1], None,
                                    ALU.mult).then_inc(vb_ready, 1)
        done = [split, 0]
        dve.wait_ge(drained, after_job["wT", KC - 1])
        split_weight(nc, dve, [w[:] for w in l0["wq"]], wt[:, 0], done)
        dve.wait_ge(drained, after_job["wT", NQKV + KC - 1])
        split_weight(nc, dve, [w[:] for w in l0["wo"]], wt[:, 3], done)
        dve.wait_ge(drained, after_job["mean", 0])
        for b in range(BATCH):
            nc.vector.tensor_scalar(mean_wide[:, b, :], ones[0:64, :], mean[:, b:b + 1], None,
                                    ALU.mult).then_inc(mean_ready, 1)
        dve.wait_ge(drained, after_job["wu", 0])
        for c in range(KC):
            ins = nc.vector.tensor_scalar(wug[:, c, :], wur[:, c, :], g2[:, c:c + 1], None, ALU.mult)
            step.then(ins)
        split_weight(nc, dve, [w[:] for w in l0["wu"]], wug[:], done)
        for b in range(BATCH):
            dve.wait_ge(drained, after_job["mod", b])
            nc.vector.tensor_tensor(l0["mod"][:, b, :], l0["mod"][:, b, :], bp[:], ALU.add)
        dve.wait_ge(drained, after_job["bo", 0])
        nc.vector.tensor_tensor(l0["bo"][:], l0["bo"][:], vbo[:], ALU.add)

    @block.tensor
    def _(pe):
        pe.wait_ge(consts, 2)
        for n, (kind, i) in enumerate(jobs):
            after(pe, drained, n - 7)
            x = bank[n % 8]
            if kind == "ctxT":
                pe.wait_ge(ctx_normed, i + 1)
                last = context_transposes(nc, x, cxn, i, ident)
            elif kind == "wT":
                if i < NQKV:
                    pe.wait_ge(scaled, after_row[i])
                else:
                    pe.wait_ge(w_in[3], 16)
                for k in range(KC):
                    last = nc.tensor.transpose(x[:, P * k:P * k + P], nat[:, i, P * k:P * k + P], ident[:])
            elif kind == "keys":
                if i == 0:
                    pe.wait_ge(drained, after_job["wT", 2 * KC - 1])
                for k in range(KC):
                    last = nc.tensor.matmul(x[:, 0:CW], wt[:, 1, k, P * i:P * i + P], ct[:, k, :],
                                            start=(k == 0), stop=(k == KC - 1))
            elif kind == "values":
                if i == 0:
                    pe.wait_ge(drained, after_job["wT", NQKV - 1])
                cols = context_columns(i)
                for k in range(KC):
                    last = nc.tensor.matmul(x[0:cols.stop - cols.start, :], ct[:, k, cols], wt[:, 2, k, :],
                                            start=(k == 0), stop=(k == KC - 1))
            elif kind == "aa":
                pe.wait_ge(small_in, SMALL)
                last = nc.tensor.transpose(x[:, 0:STATE], a2[:], ident[0:STATE, 0:STATE])
            elif kind == "wprogT":
                for k in range(KC):
                    last = nc.tensor.transpose(x[0:64, P * k:P * k + P], wp[:, k, :], ident[:])
            elif kind == "mean":
                for b in range(BATCH):
                    nc.tensor.matmul(x[0:64, b:b + 1], pp[:, b, :], ones[:, 0:1], start=True, stop=False)
                    last = nc.tensor.matmul(x[0:64, b:b + 1], ppr[:, b, :], ones[:, 0:1], start=False, stop=True)
            elif kind == "wu":
                pe.wait_ge(win_in, 16)
                for c in range(KC):
                    for k in range(KC):
                        last = nc.tensor.matmul(x[:, P * c:P * c + P], win[:, k, P * c:P * c + P], bm[:, k, :],
                                                start=(k == 0), stop=(k == KC - 1))
            elif kind == "ubias":
                pe.wait_ge(drained, after_job["wu", 0])
                for k in range(KC):
                    nc.tensor.matmul(x[:, 0:1], bm[:, k, :], b_in[:, k:k + 1], start=(k == 0), stop=False)
                    last = nc.tensor.matmul(x[:, 0:1], wur[:, k, :], b2[:, k:k + 1], start=False, stop=(k == KC - 1))
            elif kind == "mod":
                pe.wait_ge(mean_ready, i + 1)
                last = nc.tensor.matmul(x[:], mean_wide[:, i, :], wpt[:], start=True, stop=True)
            elif kind == "bo":
                pe.wait_ge(vb_ready, KC)
                for k in range(KC):
                    last = nc.tensor.matmul(x[:], vb_wide[:, k, :], wt[:, 3, k, :], start=(k == 0), stop=(k == KC - 1))
            last.then_inc(filled, 1)



def scan_and_prepare_layer1(nc, ctx, sem, a, keep, l1):
    sb, _ = makers(nc, ctx)
    bank, ident, hu, aa = keep["bank"], keep["ident"], keep["hu"], keep["aa"]
    U = l1["pairs"]
    W = U * P
    stq, stk, sto = sb("wq1_f", [P, KC, W], F32), sb("wk1_f", [P, KC, W], F32), sb("wo1_f", [P, U, D], F32)
    cx, ct = sb("cx1", [P, 3, D], F32), sb("cT", [P, KC, CW], F32)
    bk, bv, bv_wide = sb("bk_col", [P, U], F32), sb("bv_col", [P, U], F32), sb("bv_wide", [P, 4, P], F32)
    vbo = sb("values_bias_through_wo1", [P, D], F32)
    ones = sb("ones1", [P, P], F32)
    mask_in = sb("mask_int", [P, BATCH, KEYS], I32)
    ends = sb("ends", [STATE, BATCH, CHUNKS], F32)
    diff, limit, good = sb("diff", [STATE, BATCH, CHUNKS], F32), sb("limit", [STATE, 1], F32), sb("good", [STATE, 1], F32)
    flag = sb("unsettled", [1, 1], I32)

    wq_in, wk_in, wo_in, small_in, wv_in = (sem(f"s_{x}_in") for x in ("wq", "wk", "wo", "small", "wv"))
    padded, zeroed, consts, dve_step = sem("s_padded"), sem("s_zeroed"), sem("s_consts"), sem("s_dve_step")
    z_ready, h_ready, ends_kept = sem("s_z_ready"), sem("s_h_ready"), sem("s_ends_kept")
    goods_ready, goods_summed, flag_ready = sem("s_goods_ready"), sem("s_goods_summed"), sem("s_flag_ready")
    split, filled, drained, wide_ready = sem("s_split"), sem("s_filled"), sem("s_drained"), sem("s_wide_ready")
    wide_used = sem("s_wide_used")

    jobs = [("ctxT", g) for g in range(3)] + [("keys", u) for u in range(U)]
    jobs += [("values", (g, half)) for half in range(W // D) for g in range(3)] + [("bo", 0)]
    after_job = {job: n + 1 for n, job in enumerate(jobs)}
    SMALL = 16 * (4 + 7)
    SCAN_STEPS = ROUNDS * CHUNK
    before = hu[:, :, 0:SEQ].rearrange("p b (c s) -> p b c s", s=CHUNK)
    state = hu[:, :, 1:1 + SEQ].rearrange("p b (c s) -> p b c s", s=CHUNK)

    block = ctx.enter_context(nc.Block())

    @block.sync
    def _(sp):
        sp.dma_start(stq[:], a["Wq"].rearrange("(k p) n -> p k n", p=P)).then_inc(wq_in, 16)
        sp.dma_start(sto[:], a["Wo"].rearrange("(k p) n -> p k n", p=P)).then_inc(wo_in, 16)
        sp.wait_ge(padded, 1)
        for b in range(BATCH):
            sp.dma_start(cx[:, b, :], a["ctx"][b, 0:MAIN, :]).then_inc(small_in, 16)
            sp.dma_start(cx[GAP * b:GAP * b + REM, 2, :], a["ctx"][b, MAIN:KEYS, :]).then_inc(small_in, 16)
        sp.dma_start(stk[:], a["Wk"].rearrange("(k p) n -> p k n", p=P)).then_inc(wk_in, 16)
        for b in range(BATCH):
            sp.dma_start(mask_in[:, b, :], load_row(a["mask"][b])).then_inc(small_in, 16)
        sp.dma_start(bk[:], a["bk"].rearrange("(c p) -> p c", p=P), allow_slow_non_contiguous=True).then_inc(small_in, 16)
        sp.dma_start(bv[:], a["bv"].rearrange("(c p) -> p c", p=P), allow_slow_non_contiguous=True).then_inc(small_in, 16)
        sp.dma_start(l1["nbq"][:], a["bq"].rearrange("(c p) -> p c", p=P), allow_slow_non_contiguous=True).then_inc(small_in, 16)
        sp.dma_start(l1["bo"][:], load_row(a["bo"])).then_inc(small_in, 16)
        sp.dma_start(l1["gamma"][:], load_row(a["gamma"])).then_inc(small_in, 16)
        sp.wait_ge(split, 2)
        sp.dma_start(stq[:], a["Wv"].rearrange("(k p) n -> p k n", p=P)).then_inc(wv_in, 16)
        sp.dma_start(l1["beta"][:], load_row(a["beta"])).then_inc(wv_in, 16)
        sp.wait_ge(wv_in, 32)

    @block.gpsimd
    def _(pool):
        nc.gpsimd.memset(cx[0:2 * GAP, 2, :], 0.0).then_inc(padded, 1)
        nc.gpsimd.memset(ones[:], 1.0).then_inc(consts, 1)
        nc.gpsimd.memset(l1["kbd"][:], 0.0).then_inc(zeroed, 1)
        nc.gpsimd.memset(l1["vr"][:], 0.0).then_inc(zeroed, 1)

    @block.tensor
    def _(pe):
        def scan_step(t, s):
            for b in range(BATCH):
                pe.wait_ge(h_ready, BATCH * s + b + 1)
                nc.tensor.matmul(bank[b][0:STATE, 0:CHUNKS], aa[:], before[:, b, :, bass.ds(t, 1)],
                                 start=True, stop=True).then_inc(z_ready, 1)

        with pe.Fori(0, ROUNDS, 1) as r:
            with pe.Fori(0, CHUNK, 1) as t:
                scan_step(t, r * CHUNK + t)
        pe.wait_ge(consts, 1)
        pe.wait_ge(goods_ready, 1)
        nc.tensor.matmul(bank[2][0:1, 0:1], good[:], ones[0:STATE, 0:1], start=True, stop=True).then_inc(goods_summed, 1)
        pe.wait_ge(flag_ready, 1)
        unsettled = pe.value_load(flag[0:1, 0:1], min_val=0, max_val=1)
        with pe.If(unsettled > 0):
            with pe.Fori(0, CHUNKS - ROUNDS, 1) as r:
                with pe.Fori(0, CHUNK, 1) as t:
                    scan_step(t, r * CHUNK + t + SCAN_STEPS)
        for n, (kind, i) in enumerate(jobs):
            after(pe, drained, n - 7)
            x = bank[n % 8]
            if kind == "ctxT":
                pe.wait_ge(small_in, SMALL)
                last = context_transposes(nc, x, cx, i, ident)
            elif kind == "keys":
                if i == 0:
                    pe.wait_ge(wk_in, 16)
                    pe.wait_ge(drained, after_job["ctxT", 2])
                for k in range(KC):
                    last = nc.tensor.matmul(x[:, 0:CW], stk[:, k, P * i:P * i + P], ct[:, k, :],
                                            start=(k == 0), stop=(k == KC - 1))
            elif kind == "values":
                group, part = i
                if i == (0, 0):
                    pe.wait_ge(wv_in, 32)
                cols = context_columns(group)
                for k in range(KC):
                    last = nc.tensor.matmul(x[0:cols.stop - cols.start, :], ct[:, k, cols], stq[:, k, D * part:D * part + D],
                                            start=(k == 0), stop=(k == KC - 1))
            elif kind == "bo":
                for k in range(U):
                    pe.wait_ge(wide_ready, k + 1)
                    last = nc.tensor.matmul(x[:], bv_wide[:, k % 4, :], sto[:, k, :], start=(k == 0), stop=(k == U - 1))
                    if k < U - 1:
                        last.then_inc(wide_used, 1)
            last.then_inc(filled, 1)

    @block.scalar
    def _(act):
        def scan_step(t, s):
            for b in range(BATCH):
                act.wait_ge(z_ready, BATCH * s + b + 1)
                nc.scalar.activation(state[0:STATE, b, :, bass.ds(t, 1)], bank[b][0:STATE, 0:CHUNKS].unsqueeze(2),
                                     ACT.Silu).then_inc(h_ready, 1)

        act.sem_inc(h_ready, BATCH)
        for r in range(ROUNDS):
            with act.Fori(0, CHUNK - 1, 1) as t:
                scan_step(t, t + r * CHUNK)
            if r == ROUNDS - 1:
                act.wait_ge(ends_kept, 1)
            scan_step(CHUNK - 1, CHUNK - 1 + r * CHUNK)
        act.wait_ge(flag_ready, 1)
        unsettled = act.value_load(flag[0:1, 0:1], min_val=0, max_val=1)
        with act.If(unsettled > 0):
            with act.Fori(0, CHUNKS - ROUNDS, 1) as r:
                with act.Fori(0, CHUNK, 1) as t:
                    scan_step(t, r * CHUNK + t + SCAN_STEPS)
        for n, (kind, i) in enumerate(jobs):
            act.wait_ge(filled, n + 1)
            x = bank[n % 8]
            if kind == "ctxT":
                cols = context_columns(i)
                w = cols.stop - cols.start
                last = nc.scalar.activation(ct[:, :, cols], x[:, 0:KC * w].rearrange("p (k c) -> p k c", k=KC), ACT.Copy)
            elif kind == "keys":
                if i == 0:
                    act.wait_ge(small_in, SMALL)
                    act.wait_ge(zeroed, 2)
                last = evacuate_keys(nc, x, l1, i, bk[:, i:i + 1])
            elif kind == "values":
                last = evacuate_values(nc, x, l1, i[0], D * i[1])
            elif kind == "bo":
                last = nc.scalar.activation(vbo[:], x[:], ACT.Copy)
            last.then_inc(drained, 1)

    @block.vector
    def _(dve):
        step = Chain(dve, dve_step)
        done = [split, 0]
        dve.wait_ge(wq_in, 16)
        split_weight(nc, dve, [w[:] for w in l1["wq"]], stq[:], done)
        dve.wait_ge(h_ready, BATCH + BATCH * (ROUNDS - 1) * CHUNK)
        nc.vector.tensor_copy(ends[:], state[0:STATE, :, :, CHUNK - 1]).then_inc(ends_kept, 1)
        dve.wait_ge(wo_in, 16)
        split_weight(nc, dve, [w[:] for w in l1["wo"]], sto[:], done)
        dve.wait_ge(small_in, SMALL)
        step.then(nc.vector.tensor_scalar(l1["nbq"][:], l1["nbq"][:], -SCALE, None, ALU.mult))
        for h, (dst, src, n) in enumerate(((0, 0, KEYS), (REM, 0, MAIN), (0, MAIN, REM))):
            nc.vector.tensor_scalar(l1["mask"][:, :, min(h, 1), dst:dst + n], mask_in[:, :, src:src + n], 0, MASKED,
                                    ALU.is_equal, ALU.mult)
        dve.wait_ge(h_ready, BATCH + BATCH * SCAN_STEPS)
        dve.wait_ge(ends_kept, 1)
        now = state[0:STATE, :, :, CHUNK - 1]
        step.then(nc.vector.tensor_tensor(diff[:], now, ends[:], ALU.subtract))
        step.then(nc.vector.tensor_tensor(diff[:], diff[:], diff[:], ALU.mult))
        step.then(nc.vector.tensor_tensor(ends[:], now, now, ALU.mult))
        step.then(nc.vector.tensor_reduce(limit[:], ends[:].rearrange("p b c -> p (b c)"), AX_X, ALU.max))
        step.then(nc.vector.tensor_scalar(limit[:], limit[:], SETTLED * SETTLED, None, ALU.mult))
        step.then(nc.vector.tensor_scalar(diff[:], diff[:], limit[:], None, ALU.is_le))
        nc.vector.tensor_reduce(good[:], diff[:].rearrange("p b c -> p (b c)"), AX_X, ALU.add).then_inc(goods_ready, 1)
        dve.wait_ge(goods_summed, 1)
        nc.vector.tensor_scalar(flag[:], bank[2][0:1, 0:1], float(STATE * BATCH * CHUNKS) - 0.5, None,
                                ALU.is_lt).then_inc(flag_ready, 1)
        dve.wait_ge(consts, 1)
        for k in range(U):
            after(dve, wide_used, k - 3)
            nc.vector.tensor_scalar(bv_wide[:, k % 4, :], ones[:], bv[:, k:k + 1], None, ALU.mult).then_inc(wide_ready, 1)
        dve.wait_ge(drained, after_job["bo", 0])
        nc.vector.tensor_tensor(l1["bo"][:], l1["bo"][:], vbo[:], ALU.add)



def run_layer(nc, ctx, sem, layer, keep, l, src_dram, dst_dram):
    sb, _ = makers(nc, ctx)
    name = lambda x: f"{x}_l{layer}"
    U = l["pairs"]
    hu, cc, ident = keep["hu"], keep["cc"], keep["ident"]
    ring = sb(name("ring"), [P, SLOTS, D], F32)
    xt = [sb(name(f"xT_{x}"), [P, KC, BLOCK], F32R) for x in ("high", "low")]
    qt = [sb(name(f"qT{i}"), [P, U, BLOCK], F32) for i in range(2)]
    probs = sb(name("probs"), [P, 2, PW], F32)
    pt = sb(name("probsT"), [P, 2, 3 * P], F32)
    heads = sb(name("heads"), [P, D], F32)
    cat = [sb(name(f"catT_{x}"), [P, KC, P], F32R) for x in ("high", "low")]
    least = sb(name("least"), [P, 4, 2], F32)
    sums = sb(name("sums"), [P, 2, 2 * KC], F32)
    inv = sb(name("inv"), [P, 2 * KC], F32)
    fix = sb(name("ln_constants"), [P, 2, 2], F32)
    rstd = sb(name("rstd"), [P, 2, 2], F32)
    stats, mv = sb(name("stats"), [P, 2, 6], F32), sb(name("mv"), [P, 2, 2], F32)
    if layer == 0:
        xn = sb(name("xn"), [P, 2, D], F32)
        yn = sb(name("yn"), [P, D], F32)
        out = sb(name("out"), [P, 2, D], F32)
    else:
        hs = sb(name("scan_tile"), [P, TILES, P], F32)
        mask = sb(name("mask_now"), [P, 2, KEYS], F32)
    S, PT, O, T, G, W = keep["bank"][0:2], keep["bank"][2], keep["bank"][3], keep["bank"][4:6], keep["bank"][6], keep["bank"][7]

    slot_in = [sem(name(f"slot_in{i}")) for i in range(SLOTS)]
    slot_out = [sem(name(f"slot_out{i}")) for i in range(2 if layer == 0 else SLOTS)]
    s = {x: sem(name(x)) for x in (
        "pads", "tile_step", "tile_stats", "tile_rstd", "tile_normed", "bias_added", "hs_ready",
        "SS_filled", "XT_filled", "OT_filled", "YT_filled", "T_high", "T_drained", "G_filled", "G_drained", "scores_ready", "least_ready",
        "probs_ready", "pt_filled", "pt_drained", "pv_done", "inverses", "heads_ready", "cat_used",
        "W_drained", "out_step", "out_stats", "out_rstd", "out_normed", "out_pool", "out_ready", "mask_ready",
        "passed_dve", "passed_pool")}
    plan = Plan(*(layer0_places() if layer == 0 else layer1_places()))
    rows = lambda it: bass.ds(it.tile * P, P)
    hu_flat = hu[:].rearrange("p b s -> p (b s)")
    hu_cols = lambda it: bass.ds(it.tile * P + it.batch + 1, P)
    kbd = l["kbd"][:].rearrange("p b u c -> p (b u c)")
    vm = l["vm"][:].rearrange("p b c -> p (b c)")
    vr = l["vr"][:].rearrange("p b u c -> p (b u c)")

    block = ctx.enter_context(nc.Block())

    @block.sync
    def _(sp):
        for it in walk(sp, plan):
            if it.kind == "LD":
                if layer == 0:
                    after(sp, s["out_ready"], it.done("RN"))
                else:
                    after(sp, slot_out[it.slot], 16 * it.done(("ST", it.slot)))
                sp.dma_start(ring[:, it.slot, :], src_dram[rows(it), :]).then_inc(slot_in[it.slot], 16)
            elif it.kind == "ST":
                sp.wait_ge(s["out_ready"], it.done("ST") + 1)
                if layer == 0:
                    sp.dma_start(dst_dram[rows(it), :], out[:, it.idx % 2, :]).then_inc(slot_out[it.idx % 2], 16)
                else:
                    sp.dma_start(dst_dram[rows(it), :], ring[:, it.slot, :]).then_inc(slot_out[it.slot], 16)
        for i in range(len(slot_out)):
            sp.wait_ge(slot_out[i], 16 * (NBLK * TILES // len(slot_out)))

    @block.tensor
    def _(pe):
        def transposes(it, chunk):
            after(pe, s["T_drained"], it.done("T") - 1)
            for k in range(KC):
                last = nc.tensor.transpose(T[it.side("T")][:, P * k:P * k + P], chunk(k), ident[:])
            last.then_inc(s[it.kind + "_filled"], 1)

        for it in walk(pe, plan):
            if it.kind == "SS":
                pe.wait_ge(s["hs_ready"], it.done("SS") + 1)
                after(pe, s["T_drained"], it.done("T") - 1)
                nc.tensor.matmul(T[it.side("T")][:], hs[:, it.idx, :], cc[:], start=True, stop=True).then_inc(
                    s["SS_filled"], 1)
            elif it.kind == "XT":
                if layer == 0:
                    pe.wait_ge(s["tile_normed"], it.done("XT") + 1)
                    transposes(it, lambda k: xn[:, it.idx % 2, P * k:P * k + P])
                else:
                    pe.wait_ge(s["T_drained"], it.done("drained"))
                    transposes(it, lambda k: ring[:, it.slot, P * k:P * k + P])
            elif it.kind == "Q":
                if it.idx == 0:
                    pe.wait_ge(s["T_drained"], it.done("drained"))
                after(pe, s["G_drained"], it.done("G"))
                for k in range(KC):
                    last = product(nc, G[:], [w[:, k, P * it.idx:P * it.idx + P] for w in l["wq"]],
                                   [x[:, k, :] for x in xt], start=(k == 0), stop=(k == KC - 1))
                last.then_inc(s["G_filled"], 1)
            elif it.kind == "S":
                t, u = divmod(it.idx, U)
                if it.idx < U:
                    pe.wait_ge(s["G_drained"], it.done("G"))
                after(pe, s["probs_ready"], it.done("S") - 1)
                nc.tensor.matmul(S[it.idx % 2][:, 0:PAIRW], qt[it.par][:, u, P * t:P * t + P],
                                 kbd[:, bass.ds(it.batch * (U * PAIRW) + u * PAIRW, PAIRW)],
                                 start=True, stop=True).then_inc(s["scores_ready"], 1)
            elif it.kind == "PT":
                pe.wait_ge(s["probs_ready"], it.done("PT") + 1)
                after(pe, s["pt_drained"], it.done("PT"))
                side = it.idx % 2
                for n, col in enumerate((0, SECOND + REM, MAIN)):
                    last = nc.tensor.transpose(PT[:, P * n:P * n + P], probs[:, side, col:col + P], ident[:])
                last.then_inc(s["pt_filled"], 1)
            elif it.kind == "PV":
                u, side = it.idx % U, it.idx % 2
                first, col = it.idx % KC == 0, P * (it.idx % KC)
                pe.wait_ge(s["pt_drained"], it.done("PV") + 1)
                if first:
                    after(pe, s["heads_ready"], it.done("ON"))
                nc.tensor.matmul(O[:, col:col + P], pt[:, side, 2 * P:3 * P],
                                 vr[:, bass.ds(it.batch * (U * P) + u * P, P)], start=first, stop=False)
                for h in range(2):
                    last = nc.tensor.matmul(O[:, col + HD * h:col + HD * h + HD], pt[:, side, P * h:P * h + P],
                                            vm[:, bass.ds(it.batch * (U * P) + u * P + HD * h, HD)],
                                            start=False, stop=(it.idx % KC == KC - 1 and h == 1))
                last.then_inc(s["pv_done"], 1)
            elif it.kind == "OT":
                pe.wait_ge(s["heads_ready"], it.done("ON"))
                transposes(it, lambda k: heads[:, P * k:P * k + P])
            elif it.kind == "WO":
                part = it.idx % 2 if layer else 0
                pe.wait_ge(s["T_drained"], it.done("drained"))
                if part == 0:
                    tile = it.done("WO") if layer == 0 else it.blk * TILES + it.idx // 2
                    after(pe, s["W_drained"], tile)
                for k in range(KC):
                    last = product(nc, W[:], [x[:, k, :] for x in cat], [w[:, KC * part + k, :] for w in l["wo"]],
                                   start=(k == 0 and part == 0), stop=(k == KC - 1 and (part == 1 or layer == 0)))
                last.then_inc(s["cat_used"], 1)
            elif it.kind == "YT":
                pe.wait_ge(s["out_normed"], it.done("YT") + 1)
                transposes(it, lambda k: yn[:, P * k:P * k + P])
            elif it.kind == "U":
                pe.wait_ge(s["T_drained"], it.done("drained"))
                after(pe, s["G_drained"], it.done("G"))
                for k in range(KC):
                    last = product(nc, G[:, 0:P], [w[:, k, :] for w in l["wu"]],
                                   [x[:, k, :] for x in cat], start=(k == 0), stop=(k == KC - 1))
                last.then_inc(s["cat_used"], 1)

    @block.scalar
    def _(act):
        bank_T = [t[:].rearrange("p (k c) -> p k c", k=KC) for t in T]
        act.wait_ge(s["pads"], 4)
        for it in walk(act, plan):
            if it.kind in ("XT", "OT", "YT"):
                act.wait_ge(s[it.kind + "_filled"], it.done(it.kind) + 1)
                if it.kind == "XT":
                    after(act, s["G_filled"], it.done("Q"))
                    dst = xt[0][:, :, P * it.idx:P * it.idx + P]
                else:
                    after(act, s["cat_used"], it.done("cat_read"))
                    dst = cat[0][:]
                nc.scalar.activation(dst, bank_T[it.side("T")], ACT.Copy).then_inc(s["T_high"], 1)
            elif it.kind == "Q":
                act.wait_ge(s["G_filled"], it.done("Q") + 1)
                nc.scalar.activation(qt[it.par][:, it.idx, :], G[:], ACT.Identity, scale=-SCALE,
                                     bias=l["nbq"][:, it.idx:it.idx + 1]).then_inc(s["G_drained"], 1)
            elif it.kind == "U":
                act.wait_ge(s["cat_used"], it.done("cat_read") + 1)
                nc.scalar.activation(hu_flat[STATE:P, hu_cols(it)], G[STATE:P, 0:P], ACT.Identity,
                                     bias=l["ubias"][STATE:P]).then_inc(s["G_drained"], 1)
            elif it.kind == "S":
                side, o = it.idx % 2, it.idx // KC
                act.wait_ge(s["least_ready"], it.done("S") + 1)
                after(act, s["pt_filled"], it.done("S") - 1)
                for h in range(2):
                    col = 2 * (it.idx % KC) + h
                    last = nc.scalar.activation(probs[:, side, SECOND * h:SECOND * h + KEYS], S[side][:, KEYS * h:KEYS * h + KEYS],
                                                ACT.Exp, scale=-1.0, bias=least[:, it.idx % 4, h:h + 1],
                                                accum_out=sums[:, o % 2, col:col + 1])
                last.then_inc(s["probs_ready"], 1)

    @block.vector
    def _(dve):
        bank_T = [t[:].rearrange("p (k c) -> p k c", k=KC) for t in T]

        def statistics(which, x, step, count, ready):
            nc.vector.bn_stats(stats[:, which, :], x).then_inc(step, 1)
            dve.wait_ge(step, count + 1)
            dve.sem_inc(s["passed_dve"], 1)
            nc.vector.bn_aggr(mv[:, which, :], stats[:, which, :]).then_inc(ready, 1)

        for it in walk(dve, plan):
            if it.kind == "LN":
                dve.wait_ge(slot_in[it.slot], 16 * it.done(("LD", it.slot)))
                after(dve, s["tile_normed"], it.done("LN"))
                statistics(0, ring[:, it.slot, :], s["tile_step"], it.done("LN"), s["tile_stats"])
            elif it.kind == "SS":
                dve.wait_ge(slot_in[it.slot], 16 * it.done(("LD", it.slot)))
                dve.wait_ge(s["SS_filled"], it.done("SS") + 1)
                nc.vector.tensor_tensor(ring[:, it.slot, :], T[it.side("T")][:], ring[:, it.slot, :], ALU.add).then_inc(s["T_drained"], 1)
            elif it.kind in ("XL", "OL", "YL"):
                dve.wait_ge(s["T_high"], it.done("split") + 1)
                high, low = ([x[:, :, P * it.idx:P * it.idx + P] for x in xt] if it.kind == "XL" else [x[:] for x in cat])
                nc.vector.tensor_tensor(low, bank_T[it.side("drained")], high.bitcast(F32), ALU.subtract).then_inc(s["T_drained"], 1)
            elif it.kind == "S":
                if layer == 1 and it.idx == 0:
                    after(dve, s["least_ready"], it.done("S"))
                    nc.vector.tensor_copy(mask[:].rearrange("p h k -> p (h k)"), l["mask"][:].rearrange("p b h k -> p (b h k)")[
                        :, bass.ds(it.batch * PAIRW, PAIRW)]).then_inc(s["mask_ready"], 1)
                    dve.wait_ge(s["mask_ready"], it.blk + 1)
                dve.wait_ge(s["scores_ready"], it.done("S") + 1)
                after(dve, s["probs_ready"], it.done("S") - 3)
                dve.sem_inc(s["passed_dve"], 1)
                bank_S = S[it.idx % 2]
                if layer == 0:
                    nc.vector.tensor_reduce(least[:, it.idx % 4, :], bank_S[:, 0:PAIRW].rearrange("p (h k) -> p h k", h=2),
                                            AX_X, ALU.min).then_inc(s["least_ready"], 1)
                else:
                    for h in range(2):
                        cols = bank_S[:, KEYS * h:KEYS * h + KEYS]
                        last = nc.vector.tensor_tensor_reduce(out=cols, in0=cols, in1=mask[:, h, :], scale=1.0, scalar=NO_KEY,
                                                              op0=ALU.add, op1=ALU.min, accum_out=least[:, it.idx % 4, h:h + 1])
                    last.then_inc(s["least_ready"], 1)
            elif it.kind == "PT":
                dve.wait_ge(s["pt_filled"], it.done("PT") + 1)
                after(dve, s["pv_done"], it.done("PT") - 1)
                nc.vector.tensor_copy(pt[:, it.idx % 2, :], PT[:, 0:3 * P]).then_inc(s["pt_drained"], 1)
            elif it.kind == "ON":
                dve.wait_ge(s["pv_done"], KC * (it.done("ON") + 1))
                nc.vector.reciprocal(inv[:], sums[:, it.idx % 2, :]).then_inc(s["inverses"], 1)
                dve.wait_ge(s["inverses"], it.done("ON") + 1)
                nc.vector.tensor_tensor(heads[:].rearrange("p (h d) -> p h d", d=HD), O[:].rearrange("p (h d) -> p h d", d=HD),
                                        inv[:].unsqueeze(2).to_broadcast([P, 2 * KC, HD]), ALU.mult).then_inc(s["heads_ready"], 1)
            elif it.kind == "RD":
                tile, x = it.done("RD"), ring[:, it.slot, :]
                dve.wait_ge(s["cat_used"], it.done("cat_read"))
                dve.wait_ge(s["bias_added"], tile + 1)
                nc.vector.tensor_tensor(x, W[:], x, ALU.add).then_inc(s["W_drained"], 1)
            elif it.kind == "RN":
                tile, x = it.done("RN"), ring[:, it.slot, :]
                dve.wait_ge(s["W_drained"], tile + 1)
                after(dve, s["out_normed"], tile)
                statistics(1, x, s["out_step"], tile, s["out_stats"])

    @block.gpsimd
    def _(pool):
        nc.gpsimd.memset(probs[:], 0.0)
        for row, col, value in ((0, 0, 0.0), (0, 1, EPS), (1, 0, -1.0), (1, 1, -0.5)):
            nc.gpsimd.memset(fix[:, row, col:col + 1], value).then_inc(s["pads"], 1)
        pool.wait_ge(s["pads"], 4)
        def normalised(which, out, x, step, count, done):
            nc.gpsimd.tensor_tensor(rstd[:, which, :], mv[:, which, :], fix[:, 0, :], ALU.add).then_inc(step, 1)
            pool.wait_ge(step, 4 * count + 1)
            nc.gpsimd.tensor_tensor(rstd[:, which, 1:2], rstd[:, which, 1:2], fix[:, 1, 1:2], ALU.pow).then_inc(step, 1)
            pool.wait_ge(step, 4 * count + 2)
            nc.gpsimd.tensor_tensor(rstd[:, which, 0:1], rstd[:, which, 0:1], rstd[:, which, 1:2], ALU.mult).then_inc(step, 1)
            pool.wait_ge(step, 4 * count + 3)
            nc.gpsimd.tensor_tensor(rstd[:, which, 0:1], rstd[:, which, 0:1], fix[:, 1, 0:1], ALU.mult).then_inc(step, 1)
            pool.wait_ge(step, 4 * count + 4)
            if layer == 0:
                after(pool, *((s["YT_filled"], it.done("RN")) if which else (s["XT_filled"], it.done("LN") - 1)))
            pool.sem_inc(s["passed_pool"], 1)
            nc.gpsimd.tensor_scalar(out, x, rstd[:, which, 1:2], rstd[:, which, 0:1], ALU.mult, ALU.add).then_inc(done, 1)

        for it in walk(pool, plan):
            if it.kind == "LN":
                x = ring[:, it.slot, :]
                pool.wait_ge(s["tile_stats"], it.done("LN") + 1)
                normalised(0, xn[:, it.idx % 2, :], x, s["tile_rstd"], it.done("LN"), s["tile_normed"])
                pool.wait_ge(s["tile_normed"], it.done("LN") + 1)
                nc.gpsimd.tensor_tensor(x, x, l["bo"][:], ALU.add).then_inc(s["bias_added"], 1)
            elif it.kind == "HS":
                after(pool, s["SS_filled"], it.done("SS"))
                nc.gpsimd.tensor_copy(hs[:, it.idx, :], hu_flat[:, hu_cols(it)]).then_inc(s["hs_ready"], 1)
            elif it.kind == "XT" and layer == 1:
                x = ring[:, it.slot, :]
                pool.wait_ge(s["XT_filled"], it.done("XT") + 1)
                nc.gpsimd.tensor_tensor(x, x, l["bo"][:], ALU.add).then_inc(s["bias_added"], 1)
            elif it.kind == "RN":
                tile, x = it.done("RN"), ring[:, it.slot, :]
                pool.wait_ge(s["out_stats"], tile + 1)
                normalised(1, yn[:] if layer == 0 else x, x, s["out_rstd"], tile, s["out_normed"])
                pool.wait_ge(s["out_normed"], tile + 1)
                if layer == 0:
                    after(pool, slot_out[it.idx % 2], (2 * it.blk + it.idx // 2) * 16)
                    pool.sem_inc(s["passed_pool"], 1)
                    nc.gpsimd.tensor_tensor(out[:, it.idx % 2, :], x, l["mod"][:].rearrange("p b n -> p (b n)")[:, bass.ds(it.batch * D, D)],
                                            ALU.add).then_inc(s["out_ready"], 1)
                else:
                    nc.gpsimd.tensor_tensor(x, x, l["gamma"][:], ALU.mult).then_inc(s["out_pool"], 1)
                    pool.wait_ge(s["out_pool"], tile + 1)
                    nc.gpsimd.tensor_tensor(x, x, l["beta"][:], ALU.add).then_inc(s["out_ready"], 1)


_INS = {
    "x": "x", "ctx": "ctx_1024", "pp": "ctxb_2048x64", "mask": "mask_BxS2_ik0",
    "A": "L0_xattn_A", "Bmat": "L0_xattn_Bmat", "Cmat": "L0_xattn_Cmat", "W_in": "L0_xattn_W_in",
    "b_in": "L0_xattn_b_in", "W_qkv": "L0_xattn_W_qkv", "b_qkv": "L0_xattn_b_qkv", "W_o": "L0_xattn_W_o",
    "b_o": "L0_xattn_b_o", "W_prog": "L0_xattn_W_prog", "b_prog": "L0_xattn_b_prog", "g1": "L0_xattn_g1",
    "beta1": "L0_xattn_beta1", "g2": "L0_xattn_g2", "beta2": "L0_xattn_beta2",
    "Wq": "L1_xattn_Wq", "bq": "L1_xattn_bq", "Wk": "L1_xattn_Wk", "bk": "L1_xattn_bk", "Wv": "L1_xattn_Wv",
    "bv": "L1_xattn_bv", "Wo": "L1_xattn_Wo", "bo": "L1_xattn_bo", "gamma": "L1_xattn_gamma", "beta": "L1_xattn_beta",
}


def kernel(**inputs):
    import numpy as _np
    import concourse.bacc as _bacc
    from concourse import mybir as _mybir
    from concourse.bass_utils import run_bass_kernel_spmd as _run

    nc = _bacc.Bacc("TRN2", target_bir_lowering=False, num_devices=1)
    arrays, args = {}, {}
    for short, name in _INS.items():
        x = _np.ascontiguousarray(inputs[name])
        if short == "x":
            x = x.reshape(TOKENS, D)
        arrays[f"in_{short}_dram"] = x
        args[short] = nc.dram_tensor(f"in_{short}_dram", x.shape, _mybir.dt.from_np(x.dtype), kind="ExternalInput").ap()
    y = nc.dram_tensor("y_dram", (TOKENS, D), _mybir.dt.float32, kind="ExternalOutput").ap()
    build(nc, args, y)
    got = _run(nc, [arrays], core_ids=[0])
    return got.results[0]["y_dram"].reshape(BATCH, SEQ, D)
```

```python
from collections import Counter
from contextlib import ExitStack

import concourse.bass as bass
from concourse import mybir

F32 = mybir.dt.float32
F32R = mybir.dt.float32r
I32 = mybir.dt.int32
ALU = mybir.AluOpType
ACT = mybir.ActivationFunctionType
AX_X = mybir.AxisListType.X

P = 128
D = 512
KC = D // P
BATCH, SEQ = 2, 2048
TOKENS = BATCH * SEQ
BLOCK = 512
TILES = BLOCK // P
NBLK = TOKENS // BLOCK
BLK_PER_BATCH = SEQ // BLOCK
SLOTS = 2 * TILES
KEYS = 154
MAIN = P
REM = KEYS - MAIN
GAP = 32
CW = 2 * MAIN + 2 * GAP
HD = 64
PAIRW = 2 * KEYS
SECOND = MAIN + GAP
PW = SECOND + KEYS
STATE = 64
EPS = 1e-5
SCALE = 1.0 / 8.0
MASKED = 3.0e38
NO_KEY = 2.0e38
CHUNK = 16
CHUNKS = SEQ // CHUNK
ROUNDS = 2
SETTLED = 2.0 ** -18


def load_row(row):
    return row.rearrange("(a n) -> a n", a=1).broadcast_to([P, row.shape[0]])



PREV, CUR, NEXT = -1, 0, 1
TURN, AHEAD, VALUES, LOW_X, LOW_CAT, FILL, DRAIN, REFILL, STORE = range(9)


TAIL = (
    dict(ON=(0, DRAIN), OT=(2, REFILL), OL=(3, LOW_CAT), WO=(4, REFILL), RD=(5, TURN), RN=(5, STORE), ST=(5, STORE),
         YT=(8, REFILL), YL=(9, LOW_CAT)),
    dict(ON=(0, DRAIN), OT=(2, REFILL), OL=(3, LOW_CAT), WO=(4, DRAIN), RD=(6, LOW_X), RN=(7, DRAIN), ST=(8, STORE)),
)
HEAD = (
    dict(LD=((0, STORE), (0, STORE), (1, STORE), (5, STORE)),
         LN=((0, STORE), (0, STORE), (4, STORE), (8, STORE)),
         BI=((2, FILL), (4, STORE), (7, STORE), (11, STORE)),
         XT=((1, FILL), (3, FILL), (7, FILL), (10, FILL)),
         XL=((2, LOW_X), (4, LOW_X), (8, LOW_X), (11, LOW_X)),
         Q=((12, FILL), (13, FILL), (14, FILL), (15, FILL))),
    dict(LD=((0, STORE), (0, STORE), (0, STORE), (8, STORE)),
         HS=((0, TURN), (1, TURN), (2, TURN), (4, TURN)),
         SS=((3, FILL), (6, FILL), (8, FILL), (12, FILL)),
         XT=((5, FILL), (7, FILL), (10, FILL), (13, FILL)),
         BI=((5, DRAIN), (7, DRAIN), (10, DRAIN), (13, DRAIN)),
         XL=((6, TURN), (8, LOW_X), (11, LOW_X), (14, LOW_X)),
         Q=((15, FILL), (18, FILL), (22, FILL), (26, FILL), (30, FILL), (31, FILL), (34, STORE), (35, FILL))),
)
UTILES = 2
U_STEP = 10
OF_TILE = ("RD", "RN", "ST")


def places(layer):
    pairs = KC if layer == 0 else 2 * KC
    steps = TILES * pairs
    put = [(g - 2, AHEAD, "S", g) for g in range(steps)] + [(g, TURN, "PT", g) for g in range(steps)]
    put += [(g + 1, VALUES, "PV", g) for g in range(steps)]
    for o in range(steps // KC):
        for kind, (step, phase) in TAIL[layer].items():
            if kind not in OF_TILE or layer == 0:
                put.append((KC * (o + 1) + step, phase, kind, o))
            elif o % 2:
                put.append((KC * (o + 1) + step, phase, kind, o // 2))
    if layer == 0:
        put += [(KC * (UTILES * (i + 1)) + U_STEP, FILL, "U", i) for i in range(TILES // UTILES)]
    for kind, at in HEAD[layer].items():
        put += [(step - steps, phase, kind, j) for j, (step, phase) in enumerate(at)]
    return steps, put


class Plan:

    def __init__(self, steps, put):
        self.steps, self.put = steps, sorted(put, key=lambda x: (x[0], x[1]))

    def start(self):
        def turn(item):
            kind, _, j = item
            turns = {"LD": -3, "HS": -2, "LN": -1, "SS": max(0, 3 * j - 2), "XT": 3 * j + 2, "XL": 3 * j + 3}
            return turns.get(kind, len(self.put))
        return sorted([(kind, NEXT, idx) for step, _, kind, idx in self.put if step < 0], key=turn)

    def items(self, first=False, last=False):
        at = []
        for rel in (PREV, CUR, NEXT):
            if (rel == PREV and first) or (rel == NEXT and last):
                continue
            for step, phase, kind, idx in self.put:
                here = step + rel * self.steps
                if 0 <= here < self.steps:
                    at.append((here, phase, kind, rel, idx))
        return [(kind, rel, idx) for _, _, kind, rel, idx in sorted(at, key=lambda x: (x[0], x[1]))]

    def end(self):
        return [(kind, CUR, idx) for step, _, kind, idx in self.put if step >= self.steps]


ALSO = {"SS": ("T", "drained"), "XT": ("T",), "OT": ("T",), "YT": ("T",),
        "XL": ("split", "drained"), "OL": ("split", "drained"), "YL": ("split", "drained")}


def counted(items, par):
    n = Counter()
    for kind, rel, idx in items:
        n[kind] += 1
        n.update(ALSO.get(kind, ()))
        if kind in ("LD", "ST"):
            n[kind, TILES * ((par + rel) % 2) + idx] += 1
    return n


WHOLE = {"XL": "x_split", "OL": "cat_split", "YL": "y_split"}


def noted(seen, kind, idx):
    if kind in WHOLE:
        seen[WHOLE[kind]] = seen["drained"]
    if kind == "SS":
        seen["x2", idx] = seen["drained"]


class Item:

    def __init__(self, kind, blk, par, idx, seen, per=None, trip=0):
        self.kind, self.blk, self.par, self.idx = kind, blk, par, idx
        self.seen, self.per, self.trip = Counter(seen), per or {}, trip

    def done(self, x):
        return self.seen[x] + (self.per[x] * self.trip if self.per.get(x) else 0)

    def drained_for(self, x):
        return self.seen[x] + (self.per["drained"] * self.trip if self.per.get("drained") else 0)

    def side(self, x):
        assert self.per.get(x, 0) % 2 == 0
        return self.seen[x] % 2

    @property
    def batch(self):
        return self.blk // BLK_PER_BATCH

    @property
    def tile(self):
        return self.blk * TILES + self.idx

    @property
    def slot(self):
        return TILES * self.par + self.idx


def walk(eng, plan):
    base = Counter()

    def straight(some, n, par):
        for kind, rel, idx in some:
            yield Item(kind, n + rel, (par + rel) % 2, idx, base)
            base.update(counted([(kind, rel, idx)], par))
            noted(base, kind, idx)

    yield from straight(plan.start(), -1, 1)
    yield from straight(plan.items(first=True), 0, 0)
    body = plan.items()
    trips = (NBLK - 2) // 2
    per = counted(body, 1) + counted(body, 0)
    with eng.Fori(0, trips, 1) as i:
        seen = Counter(base)
        for half in range(2):
            n, par = 2 * i + (1 + half), (1 + half) % 2
            for kind, rel, idx in body:
                yield Item(kind, n + rel, (par + rel) % 2, idx, seen, per, i)
                seen.update(counted([(kind, rel, idx)], par))
                noted(seen, kind, idx)
    for x in per:
        base[x] += per[x] * trips
    for x in [*set(WHOLE.values()), *(("x2", j) for j in range(TILES))]:
        base[x] += per["drained"] * trips
    yield from straight(plan.items(last=True), NBLK - 1, (NBLK - 1) % 2)
    yield from straight(plan.end(), NBLK - 1, (NBLK - 1) % 2)


def after(eng, sem, value):
    if isinstance(value, int) and value <= 0:
        return
    eng.wait_ge(sem, value)


class Chain:

    def __init__(self, eng, sem):
        self.eng, self.sem, self.n = eng, sem, 0

    def then(self, ins):
        self.n += 1
        ins.then_inc(self.sem, 1)
        self.eng.wait_ge(self.sem, self.n)


def product(nc, out, stationary, moving, start, stop):
    (sh, sl), (mh, ml) = stationary, moving
    nc.tensor.matmul(out, sh, mh, start=start, stop=False)
    nc.tensor.matmul(out, sh, ml, start=False, stop=False)
    return nc.tensor.matmul(out, sl, mh, start=False, stop=stop)


def build(nc, a, y_dram):
    scratch = nc.dram_tensor("x1_dram", (TOKENS, D), F32, kind="Internal").ap()
    with ExitStack() as ctx:
        sb, sem = makers(nc, ctx)
        keep = dict(
            ident=sb("ident", [P, P], F32),
            hu=sb("hu", [P, BATCH, 1 + SEQ], F32),
            aa=sb("aa", [P, STATE], F32),
            cc=sb("cc", [P, D], F32),
            room=sb("room", [P, 3, KC * 2 * D], F32),
            room_in=sem("room_in"),
            bank=[ctx.enter_context(nc.psum_tensor(f"bank{i}", [P, 512], F32)) for i in range(8)],
        )
        with ExitStack() as c0:
            sb0, _ = makers(nc, c0)
            l0 = attention_tensors(sb0, "0", KC)
            l0 |= dict(
                wu=[sb0(f"wu_{x}", [P, KC, P], F32R) for x in ("high", "low")],
                ubias=sb0("ubias", [P, 1], F32),
                mod=sb0("mod", [P, BATCH, D], F32),
            )
            with ExitStack() as cp:
                prepare_layer0(nc, cp, sem, a, keep, l0)
            with ExitStack() as cw:
                run_layer(nc, cw, sem, 0, keep, l0, a["x"], scratch,
                          [a[w].rearrange("(k p) n -> p k n", p=P) for w in ("Wk", "Wv", "Wo")])
        with ExitStack() as c1:
            sb1, _ = makers(nc, c1)
            l1 = attention_tensors(sb1, "1", 2 * KC)
            l1 |= dict(
                mask=sb1("mask", [P, BATCH, 2, KEYS], F32),
                gamma=sb1("gamma", [P, D], F32),
                beta=sb1("beta", [P, D], F32),
            )
            with ExitStack() as cs:
                scan_and_prepare_layer1(nc, cs, sem, a, keep, l1)
            with ExitStack() as cw:
                run_layer(nc, cw, sem, 1, keep, l1, scratch, y_dram, gain=(a["gamma"], a["beta"]))


def makers(nc, ctx):
    sb = lambda name, shape, dt: ctx.enter_context(nc.sbuf_tensor(name, shape, dt))
    sem = lambda name: ctx.enter_context(nc.semaphore(name))
    return sb, sem


def attention_tensors(sb, tag, pairs):
    width = pairs * P
    return dict(
        pairs=pairs,
        wq=[sb(f"wq{tag}_{x}", [P, KC, width], F32R) for x in ("high", "low")],
        wo=[sb(f"wo{tag}_{x}", [P, pairs, D], F32R) for x in ("high", "low")],
        nbq=sb(f"nbq{tag}", [P, pairs], F32),
        kbd=sb(f"kbd{tag}", [P, BATCH, pairs, PAIRW], F32),
        vm=sb(f"vm{tag}", [P, BATCH, width], F32),
        vr=sb(f"vr{tag}", [P, BATCH, pairs, P], F32),
        bo=sb(f"bo{tag}", [P, D], F32),
    )


def evacuate_keys(nc, bank, l, u, bias):
    for e, (main, rem) in enumerate(((0, MAIN), (KEYS + REM, KEYS))):
        rows = slice(HD * e, HD * e + HD)
        nc.scalar.activation(l["kbd"][rows, :, u, main:main + MAIN],
                             bank[rows, 0:2 * MAIN].rearrange("p (b k) -> p b k", b=BATCH),
                             ACT.Identity, bias=bias[rows])
        last = nc.scalar.activation(l["kbd"][rows, :, u, rem:rem + REM],
                                    bank[rows, 2 * MAIN:CW].rearrange("p (b k) -> p b k", b=BATCH)[:, :, 0:REM],
                                    ACT.Identity, bias=bias[rows])
    return last


def evacuate_values(nc, bank, l, group, col):
    if group < BATCH:
        return nc.scalar.activation(l["vm"][:, group, col:col + D], bank[:], ACT.Copy)
    first = col // P
    for b in range(BATCH):
        for e in range(2):
            src = bank[GAP * b:GAP * b + REM, :].rearrange("p (u e d) -> p u e d", e=2, d=HD)[:, :, e, :]
            last = nc.scalar.activation(l["vr"][GAP * e:GAP * e + REM, b, first:first + D // P,
                                                HD * e:HD * e + HD], src, ACT.Copy)
    return last


def context_columns(group):
    return slice(group * MAIN, group * MAIN + (MAIN if group < BATCH else 2 * GAP))


def context_transposes(nc, bank, src, group, ident):
    w = MAIN if group < BATCH else 2 * GAP
    for k in range(KC):
        last = nc.tensor.transpose(bank[:, w * k:w * k + w], src[0:w, group, P * k:P * k + P], ident[0:w, 0:w])
    return last


def split_weight(nc, dve, l_pair, src, done):
    high, low = l_pair
    nc.vector.tensor_copy(high, src).then_inc(done[0], 1)
    done[1] += 1
    dve.wait_ge(done[0], done[1])
    nc.vector.tensor_tensor(low, src, high.bitcast(F32), ALU.subtract).then_inc(done[0], 1)
    done[1] += 1



def prepare_layer0(nc, ctx, sem, a, keep, l0):
    sb, _ = makers(nc, ctx)
    bank, ident = keep["bank"], keep["ident"]
    NQKV = 3 * KC
    nat = keep["room"][:, 0:2, :].rearrange("p a (r n) -> p (a r) n", n=D)
    g1, b1 = sb("g1_row", [P, D], F32), sb("beta1_row", [P, D], F32)
    wt = sb("wt", [P, 4, KC, D], F32)
    product_out = sb("product_out", [P, D], F32)
    vbo = sb("values_bias_through_wo", [P, D], F32)
    wb = sb("wb", [P, NQKV], F32)
    bqkv = sb("bqkv_col", [P, NQKV], F32)
    wbias = sb("wbias", [P, NQKV], F32)
    vb_wide = sb("vb_wide", [P, KC, P], F32)
    cx, cxn = sb("cx", [P, 3, D], F32), sb("cxn", [P, 3, D], F32)
    ct = sb("cnT", [P, KC, CW], F32)
    stats, mv = sb("ctx_stats", [P, 3, 6], F32), sb("ctx_mv", [P, 3, 2], F32)
    half, rstd, shift = sb("ctx_minus_half", [P, 3], F32), sb("ctx_rstd", [P, 3], F32), sb("ctx_shift", [P, 3], F32)
    win, bm = keep["room"][:, 2, 0:KC * D].rearrange("p (k n) -> p k n", n=D), sb("bm", [P, KC, P], F32)
    wur, wug = sb("wu_raw", [P, KC, P], F32), sb("wu_scaled", [P, KC, P], F32)
    g2, b2, b_in = sb("g2_col", [P, KC], F32), sb("beta2_col", [P, KC], F32), sb("b_in_col", [P, KC], F32)
    a2 = sb("a2", [STATE, 2 * STATE], F32)
    pp, ppr = sb("pp", [P, BATCH, 64], F32), sb("pp_rem", [P, BATCH, 64], F32)
    wp, wpt = sb("wprog", [P, KC, 64], F32), sb("wprogT", [64, D], F32)
    bp = sb("bprog_row", [P, D], F32)
    ones = sb("ones", [P, P], F32)
    mean, mean_wide = sb("mean", [64, BATCH], F32), sb("mean_wide", [64, BATCH, P], F32)

    ctx_in, row_in, small_in, win_in = sem("p_ctx_in"), sem("p_row_in"), sem("p_small_in"), sem("p_win_in")
    w_in = [sem(f"p_w_in{i}") for i in range(4)]
    padded, zeroed, consts, pool_step = sem("p_padded"), sem("p_zeroed"), sem("p_consts"), sem("p_pool_step")
    ctx_stats, ctx_normed, dve_step, scaled = sem("p_ctx_stats"), sem("p_ctx_normed"), sem("p_dve_step"), sem("p_scaled")
    biases, filled, drained, split = sem("p_biases"), sem("p_filled"), sem("p_drained"), sem("p_split")
    mean_ready, vb_ready, bqkv_in = sem("p_mean_ready"), sem("p_vb_ready"), sem("p_bqkv_in")

    jobs = [("ctxT", g) for g in range(3)] + [("wT", r) for r in range(KC, 2 * KC)] + [("keys", u) for u in range(KC)]
    jobs += [("wT", r) for r in list(range(2 * KC, NQKV)) + list(range(KC)) + list(range(NQKV, NQKV + KC))]
    jobs += [("values", g) for g in range(3)]
    jobs += [("aa", 0), ("wprogT", 0), ("mean", 0), ("wu", 0), ("bo", 0), ("ubias", 0), ("mod", 0), ("mod", 1)]
    after_job = {job: n + 1 for n, job in enumerate(jobs)}
    rows_order = list(range(KC, NQKV)) + list(range(KC))
    after_row = {r: n + 1 for n, r in enumerate(rows_order)}
    SMALL = 16 * 13

    block = ctx.enter_context(nc.Block())

    @block.sync
    def _(sp):
        sp.wait_ge(padded, 1)
        for b in range(BATCH):
            sp.dma_start(cx[:, b, :], a["ctx"][b, 0:MAIN, :]).then_inc(ctx_in, 16)
            sp.dma_start(cx[GAP * b:GAP * b + REM, 2, :], a["ctx"][b, MAIN:KEYS, :]).then_inc(ctx_in, 16)
        sp.dma_start(g1[:], load_row(a["g1"])).then_inc(row_in, 16)
        sp.dma_start(b1[:], load_row(a["beta1"])).then_inc(row_in, 16)
        wqkv = a["W_qkv"].rearrange("(m r p) n -> m p r n", p=P, r=KC)
        for m in (1, 2, 0):
            sp.dma_start(nat[:, KC * m:KC * m + KC, :], wqkv[m]).then_inc(w_in[m], 16)
        sp.dma_start(nat[:, NQKV:, :], a["W_o"].rearrange("(r p) n -> p r n", p=P)).then_inc(w_in[3], 16)

    @block.scalar
    def _(act):
        act.dma_start(bqkv[:], a["b_qkv"].rearrange("(c p) -> p c", p=P), allow_slow_non_contiguous=True).then_inc(bqkv_in, 16)
        act.dma_start(g2[:], a["g2"].rearrange("(c p) -> p c", p=P), allow_slow_non_contiguous=True).then_inc(small_in, 16)
        act.dma_start(b2[:], a["beta2"].rearrange("(c p) -> p c", p=P), allow_slow_non_contiguous=True).then_inc(small_in, 16)
        act.dma_start(b_in[:], a["b_in"].rearrange("(c p) -> p c", p=P), allow_slow_non_contiguous=True).then_inc(small_in, 16)
        for e in range(2):
            act.dma_start(a2[:, STATE * e:STATE * (e + 1)], a["A"]).then_inc(small_in, 16)
            act.dma_start(keep["cc"][STATE * e:STATE * (e + 1), :], a["Cmat"]).then_inc(small_in, 16)
        act.dma_start(pp[:], a["pp"][:, 0:MAIN, :].rearrange("b p n -> p b n")).then_inc(small_in, 16)
        act.dma_start(wp[:], a["W_prog"].rearrange("(c p) n -> p c n", p=P)).then_inc(small_in, 16)
        act.dma_start(bp[:], load_row(a["b_prog"])).then_inc(small_in, 16)
        act.dma_start(l0["bo"][:], load_row(a["b_o"])).then_inc(small_in, 16)
        act.wait_ge(padded, 3)
        act.dma_start(ppr[0:REM, :, :], a["pp"][:, MAIN:KEYS, :].rearrange("b p n -> p b n")).then_inc(small_in, 16)
        act.dma_start(bm[:, :, STATE:P], a["Bmat"].rearrange("(c p) n -> p c n", p=P)).then_inc(small_in, 16)
        act.dma_start(win, a["W_in"].rearrange("(c p) n -> p c n", p=P)).then_inc(win_in, 16)
        for n, (kind, i) in enumerate(jobs):
            act.wait_ge(filled, n + 1)
            x = bank[n % 8]
            if kind == "ctxT":
                cols = context_columns(i)
                w = cols.stop - cols.start
                last = nc.scalar.activation(ct[:, :, cols], x[:, 0:KC * w].rearrange("p (k c) -> p k c", k=KC), ACT.Copy)
            elif kind == "wT":
                m, r = divmod(i, KC)
                last = nc.scalar.activation(wt[:, m, :, P * r:P * r + P], x[:].rearrange("p (k c) -> p k c", k=KC), ACT.Copy)
            elif kind == "keys":
                if i == 0:
                    act.wait_ge(biases, 1)
                    act.wait_ge(zeroed, 2)
                last = evacuate_keys(nc, x, l0, i, wbias[:, KC + i:KC + i + 1])
            elif kind == "values":
                last = evacuate_values(nc, x, l0, i, 0)
            elif kind == "aa":
                last = nc.scalar.activation(keep["aa"][:], x[:, 0:STATE], ACT.Copy)
            elif kind == "wprogT":
                last = nc.scalar.activation(wpt[:], x[0:64, :], ACT.Copy)
            elif kind == "mean":
                last = nc.scalar.activation(mean[:], x[0:64, 0:BATCH], ACT.Copy, scale=1.0 / KEYS)
            elif kind == "wu":
                last = nc.scalar.activation(wur[:], x[:].rearrange("p (c n) -> p c n", c=KC), ACT.Copy)
            elif kind == "ubias":
                last = nc.scalar.activation(l0["ubias"][:], x[:, 0:1], ACT.Copy)
            elif kind == "mod":
                last = nc.scalar.activation(l0["mod"][:, i, :], x[:], ACT.Copy)
            elif kind == "bo":
                last = nc.scalar.activation(vbo[:], x[:], ACT.Copy)
            last.then_inc(drained, 1)

    @block.gpsimd
    def _(pool):
        nc.gpsimd.memset(cx[0:2 * GAP, 2, :], 0.0).then_inc(padded, 1)
        nc.gpsimd.memset(bm[:], 0.0).then_inc(padded, 1)
        nc.gpsimd.memset(ppr[:], 0.0).then_inc(padded, 1)
        nc.gpsimd.memset(ident[:], 0.0).then_inc(pool_step, 1)
        nc.gpsimd.memset(half[:], -0.5).then_inc(pool_step, 1)
        pool.wait_ge(pool_step, 2)
        nc.gpsimd.affine_select(out=ident[:], in_=ident[:], compare_op=ALU.not_equal, fill=1.0, base=0,
                                pattern=[[-1, P]], channel_multiplier=1).then_inc(consts, 1)
        nc.gpsimd.memset(ones[:], 1.0).then_inc(consts, 1)
        nc.gpsimd.memset(l0["kbd"][:], 0.0).then_inc(zeroed, 1)
        nc.gpsimd.memset(l0["vr"][:], 0.0).then_inc(zeroed, 1)
        pool.wait_ge(ctx_stats, 2)
        nc.gpsimd.tensor_tensor(rstd[:], mv[:, :, 1], half[:], ALU.pow).then_inc(pool_step, 1)
        pool.wait_ge(pool_step, 3)
        nc.gpsimd.tensor_tensor(shift[:], mv[:, :, 0], rstd[:], ALU.mult).then_inc(pool_step, 1)
        pool.wait_ge(pool_step, 4)
        for g in range(3):
            w = MAIN if g < BATCH else 2 * GAP
            nc.gpsimd.tensor_scalar(cxn[0:w, g, :], cx[0:w, g, :], rstd[0:w, g:g + 1], shift[0:w, g:g + 1],
                                    ALU.mult, ALU.add).then_inc(ctx_normed, 1)
        pool.wait_ge(ctx_normed, 3)
        nc.gpsimd.memset(keep["hu"][0:STATE, :, :], 0.0).then_inc(pool_step, 1)
        pool.wait_ge(pool_step, 5)
        nc.gpsimd.memset(keep["hu"][STATE:P, :, 0:1], 0.0)

    @block.vector
    def _(dve):
        step = Chain(dve, dve_step)
        step.then(nc.vector.memset(mv[:], 1.0))
        dve.wait_ge(ctx_in, 64)
        for g in range(3):
            w = MAIN if g < BATCH else 2 * GAP
            step.then(nc.vector.bn_stats(stats[0:w, g, :], cx[0:w, g, :]))
            step.then(nc.vector.bn_aggr(mv[0:w, g, :], stats[0:w, g, :]))
        nc.vector.tensor_scalar(mv[:, :, 0], mv[:, :, 0], -1.0, None, ALU.mult).then_inc(ctx_stats, 1)
        nc.vector.tensor_scalar(mv[:, :, 1], mv[:, :, 1], EPS, None, ALU.add).then_inc(ctx_stats, 1)
        dve.wait_ge(row_in, 32)
        for r in rows_order:
            dve.wait_ge(w_in[r // KC], 16)
            step.then(nc.vector.tensor_tensor_reduce(out=product_out[:], in0=nat[:, r, :], in1=b1[:], scale=1.0,
                                                     scalar=0.0, op0=ALU.mult, op1=ALU.add,
                                                     accum_out=wb[:, r:r + 1]))
            nc.vector.tensor_tensor(nat[:, r, :], nat[:, r, :], g1[:], ALU.mult).then_inc(scaled, 1)
            if r % KC == KC - 1 and r >= KC:
                dve.wait_ge(bqkv_in, 16)
                nc.vector.tensor_tensor(wbias[:, r - KC + 1:r + 1], bqkv[:, r - KC + 1:r + 1], wb[:, r - KC + 1:r + 1],
                                        ALU.add).then_inc(biases, 1)
        step.then(nc.vector.tensor_tensor(wbias[:, 0:KC], bqkv[:, 0:KC], wb[:, 0:KC], ALU.add))
        nc.vector.tensor_scalar(l0["nbq"][:], wbias[:, 0:KC], -SCALE, None, ALU.mult)
        dve.wait_ge(consts, 2)
        dve.wait_ge(biases, 2)
        for k in range(KC):
            nc.vector.tensor_scalar(vb_wide[:, k, :], ones[:], wbias[:, 2 * KC + k:2 * KC + k + 1], None,
                                    ALU.mult).then_inc(vb_ready, 1)
        done = [split, 0]
        dve.wait_ge(drained, after_job["wT", KC - 1])
        split_weight(nc, dve, [w[:] for w in l0["wq"]], wt[:, 0], done)
        dve.wait_ge(drained, after_job["wT", NQKV + KC - 1])
        split_weight(nc, dve, [w[:] for w in l0["wo"]], wt[:, 3], done)
        dve.wait_ge(drained, after_job["mean", 0])
        for b in range(BATCH):
            nc.vector.tensor_scalar(mean_wide[:, b, :], ones[0:64, :], mean[:, b:b + 1], None,
                                    ALU.mult).then_inc(mean_ready, 1)
        dve.wait_ge(drained, after_job["wu", 0])
        for c in range(KC):
            ins = nc.vector.tensor_scalar(wug[:, c, :], wur[:, c, :], g2[:, c:c + 1], None, ALU.mult)
            step.then(ins)
        split_weight(nc, dve, [w[:] for w in l0["wu"]], wug[:], done)
        dve.wait_ge(drained, after_job["bo", 0])
        nc.vector.tensor_tensor(l0["bo"][:], l0["bo"][:], vbo[:], ALU.add)
        for b in range(BATCH):
            dve.wait_ge(drained, after_job["mod", b])
            nc.vector.tensor_tensor(l0["mod"][:, b, :], l0["mod"][:, b, :], bp[:], ALU.add)

    @block.tensor
    def _(pe):
        pe.wait_ge(consts, 2)
        for n, (kind, i) in enumerate(jobs):
            after(pe, drained, n - 7)
            x = bank[n % 8]
            if kind == "ctxT":
                pe.wait_ge(ctx_normed, i + 1)
                last = context_transposes(nc, x, cxn, i, ident)
            elif kind == "wT":
                if i < NQKV:
                    pe.wait_ge(scaled, after_row[i])
                else:
                    pe.wait_ge(w_in[3], 16)
                for k in range(KC):
                    last = nc.tensor.transpose(x[:, P * k:P * k + P], nat[:, i, P * k:P * k + P], ident[:])
            elif kind == "keys":
                if i == 0:
                    pe.wait_ge(drained, after_job["wT", 2 * KC - 1])
                for k in range(KC):
                    last = nc.tensor.matmul(x[:, 0:CW], wt[:, 1, k, P * i:P * i + P], ct[:, k, :],
                                            start=(k == 0), stop=(k == KC - 1))
            elif kind == "values":
                if i == 0:
                    pe.wait_ge(drained, after_job["wT", NQKV - 1])
                cols = context_columns(i)
                for k in range(KC):
                    last = nc.tensor.matmul(x[0:cols.stop - cols.start, :], ct[:, k, cols], wt[:, 2, k, :],
                                            start=(k == 0), stop=(k == KC - 1))
            elif kind == "aa":
                pe.wait_ge(small_in, SMALL)
                last = nc.tensor.transpose(x[:, 0:STATE], a2[:], ident[0:STATE, 0:STATE])
            elif kind == "wprogT":
                for k in range(KC):
                    last = nc.tensor.transpose(x[0:64, P * k:P * k + P], wp[:, k, :], ident[:])
            elif kind == "mean":
                for b in range(BATCH):
                    nc.tensor.matmul(x[0:64, b:b + 1], pp[:, b, :], ones[:, 0:1], start=True, stop=False)
                    last = nc.tensor.matmul(x[0:64, b:b + 1], ppr[:, b, :], ones[:, 0:1], start=False, stop=True)
            elif kind == "wu":
                pe.wait_ge(win_in, 16)
                for c in range(KC):
                    for k in range(KC):
                        last = nc.tensor.matmul(x[:, P * c:P * c + P], win[:, k, P * c:P * c + P], bm[:, k, :],
                                                start=(k == 0), stop=(k == KC - 1))
            elif kind == "ubias":
                pe.wait_ge(drained, after_job["wu", 0])
                for k in range(KC):
                    nc.tensor.matmul(x[:, 0:1], bm[:, k, :], b_in[:, k:k + 1], start=(k == 0), stop=False)
                    last = nc.tensor.matmul(x[:, 0:1], wur[:, k, :], b2[:, k:k + 1], start=False, stop=(k == KC - 1))
            elif kind == "mod":
                pe.wait_ge(mean_ready, i + 1)
                last = nc.tensor.matmul(x[:], mean_wide[:, i, :], wpt[:], start=True, stop=True)
            elif kind == "bo":
                pe.wait_ge(vb_ready, KC)
                for k in range(KC):
                    last = nc.tensor.matmul(x[:], vb_wide[:, k, :], wt[:, 3, k, :], start=(k == 0), stop=(k == KC - 1))
            last.then_inc(filled, 1)



def scan_and_prepare_layer1(nc, ctx, sem, a, keep, l1):
    sb, _ = makers(nc, ctx)
    bank, ident, hu, aa = keep["bank"], keep["ident"], keep["hu"], keep["aa"]
    U = l1["pairs"]
    W = U * P
    room = keep["room"]
    stk, stv = (room[:, i, :].rearrange("p (k n) -> p k n", n=W) for i in range(2))
    sto = room[:, 2, :].rearrange("p (k n) -> p k n", n=D)
    stq = sb("wq1_f", [P, KC, W], F32)
    cx, ct = sb("cx1", [P, 3, D], F32), sb("cT", [P, KC, CW], F32)
    bk = sb("bk_col", [P, U], F32)
    bv = [l1["gamma"], l1["beta"]]
    ones = sb("ones1", [P, P], F32)
    mask_in = sb("mask_int", [P, BATCH, KEYS], I32)
    ends = sb("ends", [STATE, BATCH, CHUNKS], F32)
    diff, limit, good = sb("diff", [STATE, BATCH, CHUNKS], F32), sb("limit", [STATE, 1], F32), sb("good", [STATE, 1], F32)
    flag = sb("unsettled", [1, 1], I32)

    wq_in, small_in = sem("s_wq_in"), sem("s_small_in")
    padded, zeroed, consts, dve_step = sem("s_padded"), sem("s_zeroed"), sem("s_consts"), sem("s_dve_step")
    z_ready, h_ready, ends_kept = sem("s_z_ready"), sem("s_h_ready"), sem("s_ends_kept")
    goods_ready, goods_summed, flag_ready = sem("s_goods_ready"), sem("s_goods_summed"), sem("s_flag_ready")
    split, filled, drained, values_kept = sem("s_split"), sem("s_filled"), sem("s_drained"), sem("s_values_kept")

    jobs = [("ctxT", g) for g in range(3)] + [("keys", u) for u in range(U)]
    jobs += [("values", (g, half)) for half in range(W // D) for g in range(3)]
    FIRST_VALUES = 3 + U
    after_job = {job: n + 1 for n, job in enumerate(jobs)}
    SMALL = 16 * (4 + 2 + 1 + 2 + 1 + 1)
    SCAN_STEPS = ROUNDS * CHUNK
    JOB_BANKS = 5
    FIRST_JOB = 4

    def jobs_after(step):
        if step is None:
            return range((SCAN_STEPS - FIRST_JOB + 1) // 2, len(jobs))
        n, odd = divmod(step - FIRST_JOB, 2)
        return [n] if n >= 0 and not odd and n < len(jobs) else []

    before = hu[:, :, 0:SEQ].rearrange("p b (c s) -> p b c s", s=CHUNK)
    state = hu[:, :, 1:1 + SEQ].rearrange("p b (c s) -> p b c s", s=CHUNK)

    block = ctx.enter_context(nc.Block())

    @block.sync
    def _(sp):
        sp.wait_ge(padded, 1)
        for b in range(BATCH):
            sp.dma_start(cx[:, b, :], a["ctx"][b, 0:MAIN, :]).then_inc(small_in, 16)
            sp.dma_start(cx[GAP * b:GAP * b + REM, 2, :], a["ctx"][b, MAIN:KEYS, :]).then_inc(small_in, 16)
        for b in range(BATCH):
            sp.dma_start(mask_in[:, b, :], load_row(a["mask"][b])).then_inc(small_in, 16)
        sp.dma_start(bk[:], a["bk"].rearrange("(c p) -> p c", p=P), allow_slow_non_contiguous=True).then_inc(small_in, 16)
        for half in range(2):
            sp.dma_start(bv[half][:], load_row(a["bv"][D * half:D * half + D])).then_inc(small_in, 16)
        sp.dma_start(l1["nbq"][:], a["bq"].rearrange("(c p) -> p c", p=P), allow_slow_non_contiguous=True).then_inc(small_in, 16)
        sp.dma_start(l1["bo"][:], load_row(a["bo"])).then_inc(small_in, 16)
        sp.dma_start(stq[:], a["Wq"].rearrange("(k p) n -> p k n", p=P)).then_inc(wq_in, 16)

    @block.gpsimd
    def _(pool):
        nc.gpsimd.memset(cx[0:2 * GAP, 2, :], 0.0).then_inc(padded, 1)
        nc.gpsimd.memset(ones[:], 1.0).then_inc(consts, 1)
        nc.gpsimd.memset(l1["kbd"][:], 0.0).then_inc(zeroed, 1)
        nc.gpsimd.memset(l1["vr"][:], 0.0).then_inc(zeroed, 1)

    @block.tensor
    def _(pe):
        def scan_step(t, s):
            for b in range(BATCH):
                pe.wait_ge(h_ready, BATCH * s + b + 1)
                nc.tensor.matmul(bank[b][0:STATE, 0:CHUNKS], aa[:], before[:, b, :, bass.ds(t, 1)],
                                 start=True, stop=True).then_inc(z_ready, 1)

        def run_job(n):
            kind, i = jobs[n]
            before = n - JOB_BANKS
            if before < FIRST_VALUES:
                after(pe, drained, before + 1)
            else:
                pe.wait_ge(values_kept, before - FIRST_VALUES + 1)
            x = bank[3 + n % JOB_BANKS]
            if kind == "ctxT":
                pe.wait_ge(small_in, SMALL)
                last = context_transposes(nc, x, cx, i, ident)
            elif kind == "keys":
                if i == 0:
                    pe.wait_ge(keep["room_in"], 16 * 3)
                    pe.wait_ge(drained, after_job["ctxT", 2])
                for k in range(KC):
                    last = nc.tensor.matmul(x[:, 0:CW], stk[:, k, P * i:P * i + P], ct[:, k, :],
                                            start=(k == 0), stop=(k == KC - 1))
            elif kind == "values":
                group, part = i
                cols = context_columns(group)
                for k in range(KC):
                    last = nc.tensor.matmul(x[0:cols.stop - cols.start, :], ct[:, k, cols], stv[:, k, D * part:D * part + D],
                                            start=(k == 0), stop=(k == KC - 1))
            last.then_inc(filled, 1)

        for step in range(SCAN_STEPS):
            scan_step(step % CHUNK, step)
            for n in jobs_after(step):
                run_job(n)
        for n in jobs_after(None):
            run_job(n)
        pe.wait_ge(consts, 1)
        pe.wait_ge(goods_ready, 1)
        nc.tensor.matmul(bank[2][0:1, 0:1], good[:], ones[0:STATE, 0:1], start=True, stop=True).then_inc(goods_summed, 1)
        pe.wait_ge(flag_ready, 1)
        unsettled = pe.value_load(flag[0:1, 0:1], min_val=0, max_val=1)
        with pe.If(unsettled > 0):
            with pe.Fori(0, CHUNKS - ROUNDS, 1) as r:
                with pe.Fori(0, CHUNK, 1) as t:
                    scan_step(t, r * CHUNK + t + SCAN_STEPS)

    @block.scalar
    def _(act):
        def scan_step(t, s):
            for b in range(BATCH):
                act.wait_ge(z_ready, BATCH * s + b + 1)
                nc.scalar.activation(state[0:STATE, b, :, bass.ds(t, 1)], bank[b][0:STATE, 0:CHUNKS].unsqueeze(2),
                                     ACT.Silu).then_inc(h_ready, 1)

        act.sem_inc(h_ready, BATCH)
        def empty_bank(n):
            kind, i = jobs[n]
            act.wait_ge(filled, n + 1)
            x = bank[3 + n % JOB_BANKS]
            if kind == "ctxT":
                cols = context_columns(i)
                w = cols.stop - cols.start
                last = nc.scalar.activation(ct[:, :, cols], x[:, 0:KC * w].rearrange("p (k c) -> p k c", k=KC), ACT.Copy)
            elif kind == "keys":
                if i == 0:
                    act.wait_ge(small_in, SMALL)
                    act.wait_ge(zeroed, 2)
                last = evacuate_keys(nc, x, l1, i, bk[:, i:i + 1])
            last.then_inc(drained, 1)

        for step in range(SCAN_STEPS):
            if step == SCAN_STEPS - 1:
                act.wait_ge(ends_kept, 1)
            scan_step(step % CHUNK, step)
            for n in jobs_after(step - 1):
                if n < FIRST_VALUES:
                    empty_bank(n)
        act.wait_ge(flag_ready, 1)
        unsettled = act.value_load(flag[0:1, 0:1], min_val=0, max_val=1)
        with act.If(unsettled > 0):
            with act.Fori(0, CHUNKS - ROUNDS, 1) as r:
                with act.Fori(0, CHUNK, 1) as t:
                    scan_step(t, r * CHUNK + t + SCAN_STEPS)

    @block.vector
    def _(dve):
        step = Chain(dve, dve_step)
        done = [split, 0]
        dve.wait_ge(keep["room_in"], 16 * 3)
        split_weight(nc, dve, [w[:] for w in l1["wo"]], sto, done)
        dve.wait_ge(h_ready, BATCH + BATCH * (ROUNDS - 1) * CHUNK)
        nc.vector.tensor_copy(ends[:], state[0:STATE, :, :, CHUNK - 1]).then_inc(ends_kept, 1)
        dve.wait_ge(wq_in, 16)
        split_weight(nc, dve, [w[:] for w in l1["wq"]], stq[:], done)
        dve.wait_ge(small_in, SMALL)
        step.then(nc.vector.tensor_scalar(l1["nbq"][:], l1["nbq"][:], -SCALE, None, ALU.mult))
        for h, (dst, src, n) in enumerate(((0, 0, KEYS), (REM, 0, MAIN), (0, MAIN, REM))):
            nc.vector.tensor_scalar(l1["mask"][:, :, min(h, 1), dst:dst + n], mask_in[:, :, src:src + n], 0, MASKED,
                                    ALU.is_equal, ALU.mult)
        def keep_values(n):
            group, half = jobs[n][1]
            dve.wait_ge(filled, n + 1)
            x, bias = bank[3 + n % JOB_BANKS], bv[half]
            if group < BATCH:
                last = nc.vector.tensor_tensor(l1["vm"][:, group, D * half:D * half + D], x[:], bias[:], ALU.add)
            else:
                for b in range(BATCH):
                    for e in range(2):
                        rows = slice(GAP * b, GAP * b + REM)
                        src, add = (y[rows, :].rearrange("p (u e d) -> p u e d", e=2, d=HD)[:, :, e, :] for y in (x, bias))
                        last = nc.vector.tensor_tensor(
                            l1["vr"][GAP * e:GAP * e + REM, b, D // P * half:D // P * (half + 1), HD * e:HD * e + HD],
                            src, add, ALU.add)
            last.then_inc(values_kept, 1)

        dve.wait_ge(zeroed, 2)
        early = [n for step in range(SCAN_STEPS) for n in jobs_after(step) if n >= FIRST_VALUES]
        for n in early:
            keep_values(n)
        dve.wait_ge(h_ready, BATCH + BATCH * SCAN_STEPS)
        dve.wait_ge(ends_kept, 1)
        now = state[0:STATE, :, :, CHUNK - 1]
        step.then(nc.vector.tensor_tensor(diff[:], now, ends[:], ALU.subtract))
        step.then(nc.vector.tensor_tensor(diff[:], diff[:], diff[:], ALU.mult))
        step.then(nc.vector.tensor_tensor(ends[:], now, now, ALU.mult))
        step.then(nc.vector.tensor_reduce(limit[:], ends[:].rearrange("p b c -> p (b c)"), AX_X, ALU.max))
        step.then(nc.vector.tensor_scalar(limit[:], limit[:], SETTLED * SETTLED, None, ALU.mult))
        step.then(nc.vector.tensor_scalar(diff[:], diff[:], limit[:], None, ALU.is_le))
        nc.vector.tensor_reduce(good[:], diff[:].rearrange("p b c -> p (b c)"), AX_X, ALU.add).then_inc(goods_ready, 1)
        for n in jobs_after(None):
            keep_values(n)
        dve.wait_ge(goods_summed, 1)
        nc.vector.tensor_scalar(flag[:], bank[2][0:1, 0:1], float(STATE * BATCH * CHUNKS) - 0.5, None,
                                ALU.is_lt).then_inc(flag_ready, 1)



def run_layer(nc, ctx, sem, layer, keep, l, src_dram, dst_dram, next_weights=(), gain=None):
    sb, _ = makers(nc, ctx)
    name = lambda x: f"{x}_l{layer}"
    U = l["pairs"]
    hu, cc, ident = keep["hu"], keep["cc"], keep["ident"]
    if layer == 0:
        ring = sb(name("ring"), [P, SLOTS, D], F32)
        qt = [sb(name(f"qT{i}"), [P, U, BLOCK], F32) for i in range(2)]
    else:
        ring = keep["room"][:, 0, :].rearrange("p (s n) -> p s n", n=D)
        qt = [keep["room"][:, 1 + i, :].rearrange("p (u n) -> p u n", n=BLOCK) for i in range(2)]
    xt = [sb(name(f"xT_{x}"), [P, KC, BLOCK], F32R) for x in ("high", "low")]
    probs = sb(name("probs"), [P, 2, PW], F32)
    pt = sb(name("probsT"), [P, 2, 3 * P], F32)
    heads = sb(name("heads"), [P, D], F32)
    cat = [sb(name(f"catT_{x}"), [P, KC, P], F32R) for x in ("high", "low")]
    least = sb(name("least"), [P, 4, 2], F32)
    sums = sb(name("sums"), [P, 2, 2 * KC], F32)
    inv = sb(name("inv"), [P, 2 * KC], F32)
    fix = sb(name("ln_constants"), [P, 2, 2], F32)
    rstd = sb(name("rstd"), [P, 3, 2], F32)
    stats, mv = sb(name("stats"), [P, 3, 6], F32), sb(name("mv"), [P, 3, 2], F32)
    if layer == 0:
        xn = sb(name("xn"), [P, 2, D], F32)
        yn = sb(name("yn"), [P, D], F32)
        yt = [sb(name(f"yT_{x}"), [P, KC, UTILES * P], F32R) for x in ("high", "low")]
        out = sb(name("out"), [P, D], F32)
    else:
        hs = sb(name("scan_tile"), [P, TILES, P], F32)
        mask = sb(name("mask_now"), [P, 2, KEYS], F32)
    S, PT, O, T, G, W = keep["bank"][0:2], keep["bank"][2], keep["bank"][3], keep["bank"][4:6], keep["bank"][6], keep["bank"][7]

    slot_in = [sem(name(f"slot_in{i}")) for i in range(SLOTS)]
    slot_out = [sem(name(f"slot_out{i}")) for i in range(1 if layer == 0 else SLOTS)]
    s = {x: sem(name(x)) for x in (
        "pads", "gain_in", "tile_step", "tile_stats", "tile_rstd", "tile_normed", "bias_added", "hs_ready",
        "SS_filled", "XT_filled", "OT_filled", "YT_filled", "T_high", "T_drained", "G_filled", "Q_drained",
        "U_filled", "U_drained", "scores_ready", "least_ready",
        "probs_ready", "pt_filled", "pt_drained", "pv_done", "inverses", "heads_ready", "cat_used",
        "W_drained", "out_step", "out_stats", "out_rstd", "out_normed", "out_pool", "out_ready", "mask_ready",
        "passed_dve", "passed_pool")}
    plan = Plan(*places(layer))
    in_start = lambda it: isinstance(it.blk, int) and it.blk == 0
    query_bank = lambda it: W if in_start(it) and it.idx % 2 else G
    rows = lambda it: bass.ds(it.tile * P, P)
    hu_flat = hu[:].rearrange("p b s -> p (b s)")
    hu_cols = lambda it: bass.ds(it.tile * P + it.batch + 1, P)
    kbd = l["kbd"][:].rearrange("p b u c -> p (b u c)")
    vm = l["vm"][:].rearrange("p b c -> p (b c)")
    vr = l["vr"][:].rearrange("p b u c -> p (b u c)")

    block = ctx.enter_context(nc.Block())

    @block.sync
    def _(sp):
        for it in walk(sp, plan):
            if it.kind == "LD":
                if layer == 0:
                    after(sp, s["out_ready"], it.done("RD"))
                    after(sp, s["out_normed"], it.done("RN"))
                else:
                    after(sp, slot_out[it.slot], 16 * it.done(("ST", it.slot)))
                sp.dma_start(ring[:, it.slot, :], src_dram[rows(it), :]).then_inc(slot_in[it.slot], 16)
                if gain and in_start(it) and it.idx == TILES - 1:
                    for row_name, row in zip(("gamma", "beta"), gain):
                        sp.dma_start(l[row_name][:], load_row(row)).then_inc(s["gain_in"], 16)
                if next_weights and isinstance(it.blk, int) and it.blk == 1 and it.idx < 3:
                    weight = next_weights[it.idx]
                    place = keep["room"][:, it.idx, :].rearrange("p (k n) -> p k n", n=weight.shape[2])
                    sp.dma_start(place, weight).then_inc(keep["room_in"], 16)
            elif it.kind == "ST":
                sp.wait_ge(s["out_ready"], it.done("ST") + 1)
                if layer == 0:
                    sp.dma_start(dst_dram[rows(it), :], out[:]).then_inc(slot_out[0], 16)
                else:
                    sp.dma_start(dst_dram[rows(it), :], ring[:, it.slot, :]).then_inc(slot_out[it.slot], 16)
        for i in range(len(slot_out)):
            sp.wait_ge(slot_out[i], 16 * (NBLK * TILES // len(slot_out)))

    @block.tensor
    def _(pe):
        def transposes(it, chunk):
            after(pe, s["T_drained"], it.done("T") - 1)
            for k in range(KC):
                last = nc.tensor.transpose(T[it.side("T")][:, P * k:P * k + P], chunk(k), ident[:])
            last.then_inc(s[it.kind + "_filled"], 1)

        pe.sem_inc(s["U_filled"], 1)
        for it in walk(pe, plan):
            if it.kind == "SS":
                pe.wait_ge(s["hs_ready"], it.done("SS") + 1)
                after(pe, s["T_drained"], it.done("T") - 1)
                nc.tensor.matmul(T[it.side("T")][:], hs[:, it.idx, :], cc[:], start=True, stop=True).then_inc(
                    s["SS_filled"], 1)
            elif it.kind == "XT":
                if layer == 0:
                    pe.wait_ge(s["tile_normed"], it.done("XT") + 1)
                    transposes(it, lambda k: xn[:, it.idx % 2, P * k:P * k + P])
                else:
                    pe.wait_ge(s["T_drained"], it.drained_for(("x2", it.idx)))
                    transposes(it, lambda k: ring[:, it.slot, P * k:P * k + P])
            elif it.kind == "Q":
                if it.idx == 0:
                    pe.wait_ge(s["T_drained"], it.drained_for("x_split"))
                bank_Q = query_bank(it)
                if in_start(it):
                    after(pe, s["Q_drained"], it.idx - 1)
                else:
                    after(pe, s["Q_drained"], it.done("Q"))
                    if layer == 0:
                        pe.wait_ge(s["U_drained"], it.done("U") + 1)
                for k in range(KC):
                    last = product(nc, bank_Q[:], [w[:, k, P * it.idx:P * it.idx + P] for w in l["wq"]],
                                   [x[:, k, :] for x in xt], start=(k == 0), stop=(k == KC - 1))
                last.then_inc(s["G_filled"], 1)
            elif it.kind == "S":
                t, u = divmod(it.idx, U)
                if it.idx < U:
                    pe.wait_ge(s["Q_drained"], it.blk * U + it.idx + 1)
                after(pe, s["probs_ready"], it.done("S") - 1)
                nc.tensor.matmul(S[it.idx % 2][:, 0:PAIRW], qt[it.par][:, u, P * t:P * t + P],
                                 kbd[:, bass.ds(it.batch * (U * PAIRW) + u * PAIRW, PAIRW)],
                                 start=True, stop=True).then_inc(s["scores_ready"], 1)
            elif it.kind == "PT":
                pe.wait_ge(s["probs_ready"], it.done("PT") + 1)
                after(pe, s["pt_drained"], it.done("PT"))
                side = it.idx % 2
                for n, col in enumerate((0, SECOND + REM, MAIN)):
                    last = nc.tensor.transpose(PT[:, P * n:P * n + P], probs[:, side, col:col + P], ident[:])
                last.then_inc(s["pt_filled"], 1)
            elif it.kind == "PV":
                u, side = it.idx % U, it.idx % 2
                first, col = it.idx % KC == 0, P * (it.idx % KC)
                pe.wait_ge(s["pt_drained"], it.done("PV") + 1)
                if first:
                    after(pe, s["heads_ready"], it.done("ON"))
                nc.tensor.matmul(O[:, col:col + P], pt[:, side, 2 * P:3 * P],
                                 vr[:, bass.ds(it.batch * (U * P) + u * P, P)], start=first, stop=False)
                for h in range(2):
                    last = nc.tensor.matmul(O[:, col + HD * h:col + HD * h + HD], pt[:, side, P * h:P * h + P],
                                            vm[:, bass.ds(it.batch * (U * P) + u * P + HD * h, HD)],
                                            start=False, stop=(it.idx % KC == KC - 1 and h == 1))
                last.then_inc(s["pv_done"], 1)
            elif it.kind == "OT":
                pe.wait_ge(s["heads_ready"], it.done("ON"))
                transposes(it, lambda k: heads[:, P * k:P * k + P])
            elif it.kind == "WO":
                part = it.idx % 2 if layer else 0
                pe.wait_ge(s["T_drained"], it.drained_for("cat_split"))
                if part == 0:
                    tile = it.done("WO") if layer == 0 else it.blk * TILES + it.idx // 2
                    after(pe, s["W_drained"], tile)
                for k in range(KC):
                    last = product(nc, W[:], [x[:, k, :] for x in cat], [w[:, KC * part + k, :] for w in l["wo"]],
                                   start=(k == 0 and part == 0), stop=(k == KC - 1 and (part == 1 or layer == 0)))
                last.then_inc(s["cat_used"], 1)
            elif it.kind == "YT":
                pe.wait_ge(s["out_normed"], it.done("YT") + 1)
                transposes(it, lambda k: yn[:, P * k:P * k + P])
            elif it.kind == "U":
                pe.wait_ge(s["T_drained"], it.drained_for("y_split"))
                after(pe, s["Q_drained"], it.done("Q"))
                pe.wait_ge(s["U_drained"], it.done("U") + 1)
                for k in range(KC):
                    last = product(nc, G[:, 0:UTILES * P], [w[:, k, :] for w in l["wu"]],
                                   [x[:, k, :] for x in yt], start=(k == 0), stop=(k == KC - 1))
                last.then_inc(s["U_filled"], 1)

    @block.scalar
    def _(act):
        bank_T = [t[:].rearrange("p (k c) -> p k c", k=KC) for t in T]
        act.wait_ge(s["pads"], 4)
        act.sem_inc(s["U_drained"], 1)
        for it in walk(act, plan):
            if it.kind in ("XT", "OT", "YT"):
                act.wait_ge(s[it.kind + "_filled"], it.done(it.kind) + 1)
                if it.kind == "XT":
                    after(act, s["G_filled"], it.done("Q"))
                    dst = xt[0][:, :, P * it.idx:P * it.idx + P]
                elif it.kind == "OT":
                    after(act, s["cat_used"], it.done("WO"))
                    dst = cat[0][:]
                else:
                    act.wait_ge(s["U_filled"], it.done("U") + 1)
                    dst = yt[0][:, :, P * (it.idx % UTILES):P * (it.idx % UTILES) + P]
                nc.scalar.activation(dst, bank_T[it.side("T")], ACT.Copy).then_inc(s["T_high"], 1)
            elif it.kind == "Q":
                act.wait_ge(s["G_filled"], it.done("Q") + 1)
                nc.scalar.activation(qt[it.par][:, it.idx, :], query_bank(it)[:], ACT.Identity, scale=-SCALE,
                                     bias=l["nbq"][:, it.idx:it.idx + 1]).then_inc(s["Q_drained"], 1)
            elif it.kind == "U":
                act.wait_ge(s["U_filled"], it.done("U") + 2)
                cols = bass.ds(it.blk * BLOCK + it.idx * UTILES * P + it.batch + 1, UTILES * P)
                nc.scalar.activation(hu_flat[STATE:P, cols], G[STATE:P, 0:UTILES * P], ACT.Identity,
                                     bias=l["ubias"][STATE:P]).then_inc(s["U_drained"], 1)
            elif it.kind == "S":
                side, o = it.idx % 2, it.idx // KC
                act.wait_ge(s["least_ready"], it.done("S") + 1)
                after(act, s["pt_filled"], it.done("S") - 1)
                for h in range(2):
                    col = 2 * (it.idx % KC) + h
                    last = nc.scalar.activation(probs[:, side, SECOND * h:SECOND * h + KEYS], S[side][:, KEYS * h:KEYS * h + KEYS],
                                                ACT.Exp, scale=-1.0, bias=least[:, it.idx % 4, h:h + 1],
                                                accum_out=sums[:, o % 2, col:col + 1])
                last.then_inc(s["probs_ready"], 1)

    @block.vector
    def _(dve):
        bank_T = [t[:].rearrange("p (k c) -> p k c", k=KC) for t in T]

        nc.vector.memset(probs[:], 0.0)
        for row, col, value in ((0, 0, 0.0), (0, 1, EPS), (1, 0, -1.0), (1, 1, -0.5)):
            nc.vector.memset(fix[:, row, col:col + 1], value).then_inc(s["pads"], 1)

        def statistics(which, x, step, count, ready):
            nc.vector.bn_stats(stats[:, which, :], x).then_inc(step, 1)
            dve.wait_ge(step, count + 1)
            dve.sem_inc(s["passed_dve"], 1)
            nc.vector.bn_aggr(mv[:, which, :], stats[:, which, :]).then_inc(ready, 1)

        for it in walk(dve, plan):
            if it.kind == "LN":
                dve.wait_ge(slot_in[it.slot], 16 * it.done(("LD", it.slot)))
                after(dve, s["tile_normed"], it.done("LN") - 1)
                statistics(it.idx % 2, ring[:, it.slot, :], s["tile_step"], it.done("LN"), s["tile_stats"])
            elif it.kind == "SS":
                dve.wait_ge(slot_in[it.slot], 16 * it.done(("LD", it.slot)))
                dve.wait_ge(s["SS_filled"], it.done("SS") + 1)
                nc.vector.tensor_tensor(ring[:, it.slot, :], T[it.side("T")][:], ring[:, it.slot, :], ALU.add).then_inc(s["T_drained"], 1)
            elif it.kind in ("XL", "OL", "YL"):
                dve.wait_ge(s["T_high"], it.done("split") + 1)
                if it.kind == "OL":
                    high, low = (x[:] for x in cat)
                else:
                    at = it.idx if it.kind == "XL" else it.idx % UTILES
                    high, low = (x[:, :, P * at:P * at + P] for x in (xt if it.kind == "XL" else yt))
                nc.vector.tensor_tensor(low, bank_T[it.side("drained")], high.bitcast(F32), ALU.subtract).then_inc(s["T_drained"], 1)
            elif it.kind == "S":
                if layer == 1 and it.idx == 0:
                    after(dve, s["least_ready"], it.done("S"))
                    nc.vector.tensor_copy(mask[:].rearrange("p h k -> p (h k)"), l["mask"][:].rearrange("p b h k -> p (b h k)")[
                        :, bass.ds(it.batch * PAIRW, PAIRW)]).then_inc(s["mask_ready"], 1)
                    dve.wait_ge(s["mask_ready"], it.blk + 1)
                dve.wait_ge(s["scores_ready"], it.done("S") + 1)
                after(dve, s["probs_ready"], it.done("S") - 3)
                dve.sem_inc(s["passed_dve"], 1)
                bank_S = S[it.idx % 2]
                if layer == 0:
                    nc.vector.tensor_reduce(least[:, it.idx % 4, :], bank_S[:, 0:PAIRW].rearrange("p (h k) -> p h k", h=2),
                                            AX_X, ALU.min).then_inc(s["least_ready"], 1)
                else:
                    for h in range(2):
                        cols = bank_S[:, KEYS * h:KEYS * h + KEYS]
                        last = nc.vector.tensor_tensor_reduce(out=cols, in0=cols, in1=mask[:, h, :], scale=1.0, scalar=NO_KEY,
                                                              op0=ALU.add, op1=ALU.min, accum_out=least[:, it.idx % 4, h:h + 1])
                    last.then_inc(s["least_ready"], 1)
            elif it.kind == "PT":
                dve.wait_ge(s["pt_filled"], it.done("PT") + 1)
                after(dve, s["pv_done"], it.done("PT") - 1)
                nc.vector.tensor_copy(pt[:, it.idx % 2, :], PT[:, 0:3 * P]).then_inc(s["pt_drained"], 1)
            elif it.kind == "ON":
                dve.wait_ge(s["pv_done"], KC * (it.done("ON") + 1))
                nc.vector.reciprocal(inv[:], sums[:, it.idx % 2, :]).then_inc(s["inverses"], 1)
                dve.wait_ge(s["inverses"], it.done("ON") + 1)
                nc.vector.tensor_tensor(heads[:].rearrange("p (h d) -> p h d", d=HD), O[:].rearrange("p (h d) -> p h d", d=HD),
                                        inv[:].unsqueeze(2).to_broadcast([P, 2 * KC, HD]), ALU.mult).then_inc(s["heads_ready"], 1)
            elif it.kind == "RD":
                tile, x = it.done("RD"), ring[:, it.slot, :]
                dve.wait_ge(s["cat_used"], it.done("WO"))
                dve.wait_ge(s["bias_added"], tile + 1)
                nc.vector.tensor_tensor(x, W[:], x, ALU.add).then_inc(s["W_drained"], 1)
            elif it.kind == "RN":
                tile, x = it.done("RN"), ring[:, it.slot, :]
                dve.wait_ge(s["W_drained"], tile + 1)
                after(dve, s["out_normed"], tile)
                statistics(2, x, s["out_step"], tile, s["out_stats"])

    @block.gpsimd
    def _(pool):
        pool.wait_ge(s["pads"], 4)
        def normalised(which, out, x, step, count, done):
            nc.gpsimd.tensor_tensor(rstd[:, which, :], mv[:, which, :], fix[:, 0, :], ALU.add).then_inc(step, 1)
            pool.wait_ge(step, 4 * count + 1)
            nc.gpsimd.tensor_tensor(rstd[:, which, 1:2], rstd[:, which, 1:2], fix[:, 1, 1:2], ALU.pow).then_inc(step, 1)
            pool.wait_ge(step, 4 * count + 2)
            nc.gpsimd.tensor_tensor(rstd[:, which, 0:1], rstd[:, which, 0:1], rstd[:, which, 1:2], ALU.mult).then_inc(step, 1)
            pool.wait_ge(step, 4 * count + 3)
            nc.gpsimd.tensor_tensor(rstd[:, which, 0:1], rstd[:, which, 0:1], fix[:, 1, 0:1], ALU.mult).then_inc(step, 1)
            pool.wait_ge(step, 4 * count + 4)
            if layer == 0:
                after(pool, *((s["YT_filled"], it.done("RN")) if which == 2 else (s["XT_filled"], it.done("LN") - 1)))
            pool.sem_inc(s["passed_pool"], 1)
            nc.gpsimd.tensor_scalar(out, x, rstd[:, which, 1:2], rstd[:, which, 0:1], ALU.mult, ALU.add).then_inc(done, 1)

        for it in walk(pool, plan):
            if it.kind == "LN":
                x = ring[:, it.slot, :]
                pool.wait_ge(s["tile_stats"], it.done("LN") + 1)
                normalised(it.idx % 2, xn[:, it.idx % 2, :], x, s["tile_rstd"], it.done("LN"), s["tile_normed"])
            elif it.kind == "BI":
                x = ring[:, it.slot, :]
                pool.wait_ge(s["tile_normed" if layer == 0 else "XT_filled"], it.done("BI") + 1)
                nc.gpsimd.tensor_tensor(x, x, l["bo"][:], ALU.add).then_inc(s["bias_added"], 1)
            elif it.kind == "HS":
                after(pool, s["SS_filled"], it.done("SS"))
                nc.gpsimd.tensor_copy(hs[:, it.idx, :], hu_flat[:, hu_cols(it)]).then_inc(s["hs_ready"], 1)
            elif it.kind == "RD" and layer == 0:
                pool.wait_ge(s["W_drained"], it.done("RD") + 1)
                after(pool, slot_out[0], it.tile * 16)
                pool.sem_inc(s["passed_pool"], 1)
                nc.gpsimd.tensor_tensor(out[:], ring[:, it.slot, :], l["mod"][:].rearrange(
                    "p b n -> p (b n)")[:, bass.ds(it.batch * D, D)], ALU.add).then_inc(s["out_ready"], 1)
            elif it.kind == "RN":
                tile, x = it.done("RN"), ring[:, it.slot, :]
                pool.wait_ge(s["out_stats"], tile + 1)
                normalised(2, yn[:] if layer == 0 else x, x, s["out_rstd"], tile, s["out_normed"])
                if layer == 1:
                    pool.wait_ge(s["gain_in"], 32)
                    pool.wait_ge(s["out_normed"], tile + 1)
                    nc.gpsimd.tensor_tensor(x, x, l["gamma"][:], ALU.mult).then_inc(s["out_pool"], 1)
                    pool.wait_ge(s["out_pool"], tile + 1)
                    nc.gpsimd.tensor_tensor(x, x, l["beta"][:], ALU.add).then_inc(s["out_ready"], 1)


_INS = {
    "x": "x", "ctx": "ctx_1024", "pp": "ctxb_2048x64", "mask": "mask_BxS2_ik0",
    "A": "L0_xattn_A", "Bmat": "L0_xattn_Bmat", "Cmat": "L0_xattn_Cmat", "W_in": "L0_xattn_W_in",
    "b_in": "L0_xattn_b_in", "W_qkv": "L0_xattn_W_qkv", "b_qkv": "L0_xattn_b_qkv", "W_o": "L0_xattn_W_o",
    "b_o": "L0_xattn_b_o", "W_prog": "L0_xattn_W_prog", "b_prog": "L0_xattn_b_prog", "g1": "L0_xattn_g1",
    "beta1": "L0_xattn_beta1", "g2": "L0_xattn_g2", "beta2": "L0_xattn_beta2",
    "Wq": "L1_xattn_Wq", "bq": "L1_xattn_bq", "Wk": "L1_xattn_Wk", "bk": "L1_xattn_bk", "Wv": "L1_xattn_Wv",
    "bv": "L1_xattn_bv", "Wo": "L1_xattn_Wo", "bo": "L1_xattn_bo", "gamma": "L1_xattn_gamma", "beta": "L1_xattn_beta",
}


def kernel(**inputs):
    import numpy as _np
    import concourse.bacc as _bacc
    from concourse import mybir as _mybir
    from concourse.bass_utils import run_bass_kernel_spmd as _run

    nc = _bacc.Bacc("TRN2", target_bir_lowering=False, num_devices=1)
    arrays, args = {}, {}
    for short, name in _INS.items():
        x = _np.ascontiguousarray(inputs[name])
        if short == "x":
            x = x.reshape(TOKENS, D)
        arrays[f"in_{short}_dram"] = x
        args[short] = nc.dram_tensor(f"in_{short}_dram", x.shape, _mybir.dt.from_np(x.dtype), kind="ExternalInput").ap()
    y = nc.dram_tensor("y_dram", (TOKENS, D), _mybir.dt.float32, kind="ExternalOutput").ap()
    build(nc, args, y)
    got = _run(nc, [arrays], core_ids=[0])
    return got.results[0]["y_dram"].reshape(BATCH, SEQ, D)
```
